# Optimizing a Trainium2 kernel written in Bass

```python
import numpy as np
import jax
import jax.numpy as jnp

def _softmax(x, axis=-1):
    return jax.nn.softmax(x, axis=axis)

def _gelu(x):
    return jax.nn.gelu(x, approximate=True)

def _silu(x):
    return jax.nn.silu(x)

def _sigmoid(x):
    return jax.nn.sigmoid(x)

def _layernorm(x, axis=-1, eps=1e-05):
    m = jnp.mean(x, axis=axis, keepdims=True)
    v = jnp.var(x, axis=axis, keepdims=True)
    return (x - m) / jnp.sqrt(v + eps)

def _scatter_add(tgt, idx, src, axis=0):
    return tgt.at[idx].add(src)

def _segment_sum(src, seg, n):
    return jax.ops.segment_sum(src, seg, n)
kernel_name = 'mk_lm_tower_d1_tok_ids1024_r4_21d450'

def setup_inputs(seed: int=0):
    np.random.seed(seed)
    _w = jnp.asarray

    def _rec_inputs():
        import jax
        import jax.numpy as jnp
        _rk = jax.random.key(seed)
        x = jax.random.randint(jax.random.fold_in(_rk, 1), (32, 256), 0, 2048, jnp.int32)
        return x
    x = _rec_inputs()

    def _L0_tok_setup():
        import jax, jax.numpy as jnp
        import numpy as np
        CODEBOOK_SIZE = 2048
        CODEBOOK_DIM = 256
        HIDDEN_DIM = 1024
        OUT_DIM = 256
        B, M = (32, 144)
        key = jax.random.key(seed)
        k_idx, k_cb, k_w1, k_w2 = jax.random.split(key, 4)
        index = jax.random.randint(k_idx, (B, M), 0, CODEBOOK_SIZE, dtype=jnp.int32)
        codebook = CODEBOOK_DIM ** 0.5 * jax.random.normal(k_cb, (CODEBOOK_SIZE, CODEBOOK_DIM), dtype=jnp.float32)
        s1 = 1.0 / np.sqrt(CODEBOOK_DIM)
        s2 = 1.0 / np.sqrt(HIDDEN_DIM)
        W1 = s1 * jax.random.normal(k_w1, (CODEBOOK_DIM, HIDDEN_DIM), dtype=jnp.float32)
        b1 = jnp.zeros((HIDDEN_DIM,), dtype=jnp.float32)
        W2 = s2 * jax.random.normal(k_w2, (HIDDEN_DIM, OUT_DIM), dtype=jnp.float32)
        b2 = jnp.zeros((OUT_DIM,), dtype=jnp.float32)
        return {'index': index, 'codebook': codebook, 'W1': W1, 'b1': b1, 'W2': W2, 'b2': b2}
    _L0_tok_all = _L0_tok_setup()
    _L0_tok_in = {k: v for k, v in _L0_tok_all.items() if k in ('codebook', 'W1', 'b1', 'W2', 'b2')}
    del _L0_tok_all

    def _L0_attn_setup():
        import jax, jax.numpy as jnp
        import numpy as np
        HID = 256
        NH = 16
        NKV = 4
        HD = 64
        C = 64
        RATIO = 0.125
        KS = 7

        def _block_causal_attention(x, qw, kw, vw, ow, k):
            B, nc, _, D = x.shape
            T = nc * k
            xf = x.reshape(B, T, D)
            q = (xf @ qw.T).reshape(B, T, NH, HD).transpose(0, 2, 1, 3)
            kk = (xf @ kw.T).reshape(B, T, NKV, HD).transpose(0, 2, 1, 3)
            v = (xf @ vw.T).reshape(B, T, NKV, HD).transpose(0, 2, 1, 3)
            rep = NH // NKV
            kk = jnp.repeat(kk, rep, axis=1)
            v = jnp.repeat(v, rep, axis=1)
            chunk_ids = jnp.arange(T) // k
            mask = chunk_ids[:, None] >= chunk_ids[None, :]
            scores = jnp.einsum('bhqd,bhkd->bhqk', q, kk) / np.float32(np.sqrt(HD))
            scores = jnp.where(mask[None, None], scores, jnp.finfo(scores.dtype).min)
            p = jax.nn.softmax(scores, axis=-1)
            o = jnp.einsum('bhqk,bhkd->bhqd', p, v)
            o = o.transpose(0, 2, 1, 3).reshape(B, T, NH * HD)
            return (o @ ow.T).reshape(B, nc, k, D)

        def _causal_conv(x, dw, pw):
            B, nc, L, D = x.shape
            xc = x.reshape(B * nc, L, D).transpose(0, 2, 1)
            xp = jnp.pad(xc, ((0, 0), (0, 0), (KS - 1, 0)))
            y = jax.lax.conv_general_dilated(xp, dw, window_strides=(1,), padding='VALID', dimension_numbers=('NCH', 'OIH', 'NCH'), feature_group_count=D)
            y = jax.nn.gelu(y, approximate=False)
            y = jnp.einsum('ncl,oc->nol', y, pw)
            return y.transpose(0, 2, 1).reshape(B, nc, L, D)

        def _forward(hidden_states, q_w, k_w, v_w, o_w, dw_r, pw_r, dw_i, pw_i, gate_w, alpha_raw):
            B, N, D = hidden_states.shape
            pad_len = -N % C
            x = jnp.pad(hidden_states, ((0, 0), (0, pad_len), (0, 0))) if pad_len else hidden_states
            nc = x.shape[1] // C
            chunks = x.reshape(B, nc, C, D)
            Xh = jnp.fft.rfft(chunks.astype(jnp.float32), axis=2)
            M = Xh.shape[2]
            k = max(1, int(M * RATIO))
            X_low, X_high = (Xh[:, :, :k, :], Xh[:, :, k:, :])
            A_r = _block_causal_attention(X_low.real, q_w, k_w, v_w, o_w, k)
            A_i = _block_causal_attention(X_low.imag, q_w, k_w, v_w, o_w, k)
            A_low = jax.lax.complex(A_r, A_i)
            H_r = _causal_conv(X_high.real, dw_r, pw_r)
            H_i = _causal_conv(X_high.imag, dw_i, pw_i)
            g = jax.nn.sigmoid(chunks.mean(axis=2) @ gate_w.T)[:, :, None, :]
            A_high = jax.lax.complex(H_r * g, H_i * g) + X_high
            alpha = jax.nn.sigmoid(alpha_raw)
            A_low_fused = alpha * A_low + (1.0 - alpha) * X_low
            Y_hat = jnp.concatenate([A_low_fused, A_high], axis=2)
            Y = jnp.fft.irfft(Y_hat, n=C, axis=2)
            return Y.reshape(B, -1, D)[:, :N, :].astype(hidden_states.dtype)
        key = jax.random.key(seed)
        ks = jax.random.split(key, 11)
        B, N = (4, 1024)
        s = 0.02
        return {'hidden_states': jax.random.normal(ks[0], (B, N, HID), jnp.float32), 'q_w': jax.random.normal(ks[1], (NH * HD, HID), jnp.float32) * s, 'k_w': jax.random.normal(ks[2], (NKV * HD, HID), jnp.float32) * s, 'v_w': jax.random.normal(ks[3], (NKV * HD, HID), jnp.float32) * s, 'o_w': jax.random.normal(ks[4], (HID, NH * HD), jnp.float32) * s, 'dw_r': jax.random.normal(ks[5], (HID, 1, KS), jnp.float32) * 0.3, 'pw_r': jax.random.normal(ks[6], (HID, HID), jnp.float32) * s, 'dw_i': jax.random.normal(ks[7], (HID, 1, KS), jnp.float32) * 0.3, 'pw_i': jax.random.normal(ks[8], (HID, HID), jnp.float32) * s, 'gate_w': jax.random.normal(ks[9], (HID, HID), jnp.float32) * s, 'alpha_raw': jnp.zeros((1,), jnp.float32)}
    _L0_attn_all = _L0_attn_setup()
    _L0_attn_in = {k: v for k, v in _L0_attn_all.items() if k in ('q_w', 'k_w', 'v_w', 'o_w', 'dw_r', 'pw_r', 'dw_i', 'pw_i', 'gate_w', 'alpha_raw')}
    del _L0_attn_all

    def _L0_ffn_setup():
        import jax, jax.numpy as jnp
        import numpy as np
        E, K, NG, TG = (64, 8, 8, 4)
        CAP = 256
        SCALE = 2.5

        def _route(x_flat, gate_weight, e_bias):
            T = x_flat.shape[0]
            logits = x_flat.astype(jnp.float32) @ gate_weight.astype(jnp.float32).T
            scores = jax.nn.sigmoid(logits)
            sfc = scores + e_bias[None, :]
            group_scores = jax.lax.top_k(sfc.reshape(T, NG, E // NG), 2)[0].sum(-1)
            _, gidx = jax.lax.top_k(group_scores, TG)
            gmask = jnp.zeros((T, NG), jnp.float32).at[jnp.arange(T)[:, None], gidx].set(1.0)
            smask = jnp.repeat(gmask, E // NG, axis=1)
            tmp = jnp.where(smask > 0, sfc, 0.0)
            _, topk_idx = jax.lax.top_k(tmp, K)
            topk_w = jnp.take_along_axis(scores, topk_idx, axis=1)
            topk_w = topk_w / (topk_w.sum(-1, keepdims=True) + 1e-20)
            return (topk_idx, topk_w * SCALE)

        def _moe_forward(hidden_states, gate_weight, e_bias, w1, w2, w3, shared_gate, shared_up, shared_down):
            B, S, H = hidden_states.shape
            T = B * S
            x = hidden_states.reshape(T, H)
            topk_idx, topk_w = _route(x, gate_weight, e_bias)
            Sk = T * K
            flat_e = topk_idx.reshape(-1)
            order = jnp.argsort(flat_e)
            sorted_e = flat_e[order]
            counts = jax.ops.segment_sum(jnp.ones((Sk,), jnp.int32), flat_e, num_segments=E)
            offsets = jnp.cumsum(counts) - counts
            pos = jnp.arange(Sk) - offsets[sorted_e]
            tok_sorted = x[order // K]
            xe = jnp.zeros((E, CAP, H), x.dtype).at[sorted_e, pos].set(tok_sorted, mode='drop')
            h = jax.nn.silu(jnp.einsum('ech,efh->ecf', xe, w1)) * jnp.einsum('ech,efh->ecf', xe, w3)
            ye = jnp.einsum('ecf,ehf->ech', h, w2)
            pos_c = jnp.minimum(pos, CAP - 1)
            vals = ye[sorted_e, pos_c]
            vals = jnp.where((pos < CAP)[:, None], vals, 0.0)
            flat_w = topk_w.reshape(-1)[order].astype(vals.dtype)
            flat_t = (jnp.arange(Sk) // K)[order]
            out = jax.ops.segment_sum(vals * flat_w[:, None], flat_t, num_segments=T)
            shared = jax.nn.silu(x @ shared_gate.T) * (x @ shared_up.T) @ shared_down.T
            return (out + shared).reshape(B, S, H)
        key = jax.random.key(seed)
        ks = jax.random.split(key, 9)
        B, S, H, F = (1, 512, 256, 128)
        bound = 1.0 / 32.0
        return {'hidden_states': jax.random.normal(ks[0], (B, S, H), jnp.float32), 'gate_weight': jax.random.uniform(ks[1], (E, H), jnp.float32, -bound, bound), 'e_bias': jnp.zeros((E,), jnp.float32), 'w1': jax.random.normal(ks[2], (E, F, H), jnp.float32) * 0.02, 'w2': jax.random.normal(ks[3], (E, H, F), jnp.float32) * 0.02, 'w3': jax.random.normal(ks[4], (E, F, H), jnp.float32) * 0.02, 'shared_gate': jax.random.normal(ks[5], (2 * F, H), jnp.float32) * 0.02, 'shared_up': jax.random.normal(ks[6], (2 * F, H), jnp.float32) * 0.02, 'shared_down': jax.random.normal(ks[7], (H, 2 * F), jnp.float32) * 0.02}
    _L0_ffn_all = _L0_ffn_setup()
    _L0_ffn_in = {k: v for k, v in _L0_ffn_all.items() if k in ('gate_weight', 'e_bias', 'w1', 'w2', 'w3', 'shared_gate', 'shared_up', 'shared_down')}
    del _L0_ffn_all
    return {'x': x, 'L0_tok_codebook': _L0_tok_in['codebook'], 'L0_tok_W1': _L0_tok_in['W1'], 'L0_tok_b1': _L0_tok_in['b1'], 'L0_tok_W2': _L0_tok_in['W2'], 'L0_tok_b2': _L0_tok_in['b2'], 'L0_attn_q_w': _L0_attn_in['q_w'], 'L0_attn_k_w': _L0_attn_in['k_w'], 'L0_attn_v_w': _L0_attn_in['v_w'], 'L0_attn_o_w': _L0_attn_in['o_w'], 'L0_attn_dw_r': _L0_attn_in['dw_r'], 'L0_attn_pw_r': _L0_attn_in['pw_r'], 'L0_attn_dw_i': _L0_attn_in['dw_i'], 'L0_attn_pw_i': _L0_attn_in['pw_i'], 'L0_attn_gate_w': _L0_attn_in['gate_w'], 'L0_attn_alpha_raw': _L0_attn_in['alpha_raw'], 'L0_ffn_gate_weight': _L0_ffn_in['gate_weight'], 'L0_ffn_e_bias': _L0_ffn_in['e_bias'], 'L0_ffn_w1': _L0_ffn_in['w1'], 'L0_ffn_w2': _L0_ffn_in['w2'], 'L0_ffn_w3': _L0_ffn_in['w3'], 'L0_ffn_shared_gate': _L0_ffn_in['shared_gate'], 'L0_ffn_shared_up': _L0_ffn_in['shared_up'], 'L0_ffn_shared_down': _L0_ffn_in['shared_down']}

def reference(x, L0_tok_codebook, L0_tok_W1, L0_tok_b1, L0_tok_W2, L0_tok_b2, L0_attn_q_w, L0_attn_k_w, L0_attn_v_w, L0_attn_o_w, L0_attn_dw_r, L0_attn_pw_r, L0_attn_dw_i, L0_attn_pw_i, L0_attn_gate_w, L0_attn_alpha_raw, L0_ffn_gate_weight, L0_ffn_e_bias, L0_ffn_w1, L0_ffn_w2, L0_ffn_w3, L0_ffn_shared_gate, L0_ffn_shared_up, L0_ffn_shared_down):
    import jax
    import jax.numpy as jnp

    def _L0_tok_ref(index, codebook, W1, b1, W2, b2):
        import jax, jax.numpy as jnp
        import numpy as np
        CODEBOOK_SIZE = 2048
        CODEBOOK_DIM = 256
        HIDDEN_DIM = 1024
        OUT_DIM = 256
        B, M = (32, 144)
        quantized = jnp.take(codebook, index, axis=0)
        h = jax.nn.gelu(jnp.einsum('bmd,dh->bmh', quantized, W1) + b1)
        rec = jnp.einsum('bmh,ho->bmo', h, W2) + b2
        return rec

    def _L0_attn_ref(hidden_states, q_w, k_w, v_w, o_w, dw_r, pw_r, dw_i, pw_i, gate_w, alpha_raw):
        import jax, jax.numpy as jnp
        import numpy as np
        HID = 256
        NH = 16
        NKV = 4
        HD = 64
        C = 64
        RATIO = 0.125
        KS = 7

        def _block_causal_attention(x, qw, kw, vw, ow, k):
            B, nc, _, D = x.shape
            T = nc * k
            xf = x.reshape(B, T, D)
            q = (xf @ qw.T).reshape(B, T, NH, HD).transpose(0, 2, 1, 3)
            kk = (xf @ kw.T).reshape(B, T, NKV, HD).transpose(0, 2, 1, 3)
            v = (xf @ vw.T).reshape(B, T, NKV, HD).transpose(0, 2, 1, 3)
            rep = NH // NKV
            kk = jnp.repeat(kk, rep, axis=1)
            v = jnp.repeat(v, rep, axis=1)
            chunk_ids = jnp.arange(T) // k
            mask = chunk_ids[:, None] >= chunk_ids[None, :]
            scores = jnp.einsum('bhqd,bhkd->bhqk', q, kk) / np.float32(np.sqrt(HD))
            scores = jnp.where(mask[None, None], scores, jnp.finfo(scores.dtype).min)
            p = jax.nn.softmax(scores, axis=-1)
            o = jnp.einsum('bhqk,bhkd->bhqd', p, v)
            o = o.transpose(0, 2, 1, 3).reshape(B, T, NH * HD)
            return (o @ ow.T).reshape(B, nc, k, D)

        def _causal_conv(x, dw, pw):
            B, nc, L, D = x.shape
            xc = x.reshape(B * nc, L, D).transpose(0, 2, 1)
            xp = jnp.pad(xc, ((0, 0), (0, 0), (KS - 1, 0)))
            y = jax.lax.conv_general_dilated(xp, dw, window_strides=(1,), padding='VALID', dimension_numbers=('NCH', 'OIH', 'NCH'), feature_group_count=D)
            y = jax.nn.gelu(y, approximate=False)
            y = jnp.einsum('ncl,oc->nol', y, pw)
            return y.transpose(0, 2, 1).reshape(B, nc, L, D)

        def _forward(hidden_states, q_w, k_w, v_w, o_w, dw_r, pw_r, dw_i, pw_i, gate_w, alpha_raw):
            B, N, D = hidden_states.shape
            pad_len = -N % C
            x = jnp.pad(hidden_states, ((0, 0), (0, pad_len), (0, 0))) if pad_len else hidden_states
            nc = x.shape[1] // C
            chunks = x.reshape(B, nc, C, D)
            Xh = jnp.fft.rfft(chunks.astype(jnp.float32), axis=2)
            M = Xh.shape[2]
            k = max(1, int(M * RATIO))
            X_low, X_high = (Xh[:, :, :k, :], Xh[:, :, k:, :])
            A_r = _block_causal_attention(X_low.real, q_w, k_w, v_w, o_w, k)
            A_i = _block_causal_attention(X_low.imag, q_w, k_w, v_w, o_w, k)
            A_low = jax.lax.complex(A_r, A_i)
            H_r = _causal_conv(X_high.real, dw_r, pw_r)
            H_i = _causal_conv(X_high.imag, dw_i, pw_i)
            g = jax.nn.sigmoid(chunks.mean(axis=2) @ gate_w.T)[:, :, None, :]
            A_high = jax.lax.complex(H_r * g, H_i * g) + X_high
            alpha = jax.nn.sigmoid(alpha_raw)
            A_low_fused = alpha * A_low + (1.0 - alpha) * X_low
            Y_hat = jnp.concatenate([A_low_fused, A_high], axis=2)
            Y = jnp.fft.irfft(Y_hat, n=C, axis=2)
            return Y.reshape(B, -1, D)[:, :N, :].astype(hidden_states.dtype)
        return _forward(hidden_states, q_w, k_w, v_w, o_w, dw_r, pw_r, dw_i, pw_i, gate_w, alpha_raw)

    def _L0_ffn_ref(hidden_states, gate_weight, e_bias, w1, w2, w3, shared_gate, shared_up, shared_down):
        import jax, jax.numpy as jnp
        import numpy as np
        E, K, NG, TG = (64, 8, 8, 4)
        CAP = 256
        SCALE = 2.5

        def _route(x_flat, gate_weight, e_bias):
            T = x_flat.shape[0]
            logits = x_flat.astype(jnp.float32) @ gate_weight.astype(jnp.float32).T
            scores = jax.nn.sigmoid(logits)
            sfc = scores + e_bias[None, :]
            group_scores = jax.lax.top_k(sfc.reshape(T, NG, E // NG), 2)[0].sum(-1)
            _, gidx = jax.lax.top_k(group_scores, TG)
            gmask = jnp.zeros((T, NG), jnp.float32).at[jnp.arange(T)[:, None], gidx].set(1.0)
            smask = jnp.repeat(gmask, E // NG, axis=1)
            tmp = jnp.where(smask > 0, sfc, 0.0)
            _, topk_idx = jax.lax.top_k(tmp, K)
            topk_w = jnp.take_along_axis(scores, topk_idx, axis=1)
            topk_w = topk_w / (topk_w.sum(-1, keepdims=True) + 1e-20)
            return (topk_idx, topk_w * SCALE)

        def _moe_forward(hidden_states, gate_weight, e_bias, w1, w2, w3, shared_gate, shared_up, shared_down):
            B, S, H = hidden_states.shape
            T = B * S
            x = hidden_states.reshape(T, H)
            topk_idx, topk_w = _route(x, gate_weight, e_bias)
            Sk = T * K
            flat_e = topk_idx.reshape(-1)
            order = jnp.argsort(flat_e)
            sorted_e = flat_e[order]
            counts = jax.ops.segment_sum(jnp.ones((Sk,), jnp.int32), flat_e, num_segments=E)
            offsets = jnp.cumsum(counts) - counts
            pos = jnp.arange(Sk) - offsets[sorted_e]
            tok_sorted = x[order // K]
            xe = jnp.zeros((E, CAP, H), x.dtype).at[sorted_e, pos].set(tok_sorted, mode='drop')
            h = jax.nn.silu(jnp.einsum('ech,efh->ecf', xe, w1)) * jnp.einsum('ech,efh->ecf', xe, w3)
            ye = jnp.einsum('ecf,ehf->ech', h, w2)
            pos_c = jnp.minimum(pos, CAP - 1)
            vals = ye[sorted_e, pos_c]
            vals = jnp.where((pos < CAP)[:, None], vals, 0.0)
            flat_w = topk_w.reshape(-1)[order].astype(vals.dtype)
            flat_t = (jnp.arange(Sk) // K)[order]
            out = jax.ops.segment_sum(vals * flat_w[:, None], flat_t, num_segments=T)
            shared = jax.nn.silu(x @ shared_gate.T) * (x @ shared_up.T) @ shared_down.T
            return (out + shared).reshape(B, S, H)
        return _moe_forward(hidden_states, gate_weight, e_bias, w1, w2, w3, shared_gate, shared_up, shared_down)
    h = _L0_tok_ref(x, L0_tok_codebook, L0_tok_W1, L0_tok_b1, L0_tok_W2, L0_tok_b2)
    h = h + _L0_attn_ref(_layernorm(h, axis=-1), L0_attn_q_w, L0_attn_k_w, L0_attn_v_w, L0_attn_o_w, L0_attn_dw_r, L0_attn_pw_r, L0_attn_dw_i, L0_attn_pw_i, L0_attn_gate_w, L0_attn_alpha_raw)
    h = h + _L0_ffn_ref(_layernorm(h, axis=-1), L0_ffn_gate_weight, L0_ffn_e_bias, L0_ffn_w1, L0_ffn_w2, L0_ffn_w3, L0_ffn_shared_gate, L0_ffn_shared_up, L0_ffn_shared_down)
    return h

_drawn_inputs = setup_inputs


def setup_inputs(seed=0):
    import zlib

    import numpy as np

    out = dict(_drawn_inputs(seed))
    spreads = {'L0_tok_b1': (0.0, 0.8), 'L0_tok_b2': (0.0, 0.8), 'L0_ffn_e_bias': (0.0, 0.8)}
    factors = {'L0_attn_q_w': 8.0,
     'L0_attn_k_w': 8.0,
     'L0_attn_v_w': 6.088,
     'L0_attn_o_w': 6.265,
     'L0_attn_dw_r': 8.0,
     'L0_attn_pw_r': 8.0,
     'L0_attn_dw_i': 8.0,
     'L0_attn_pw_i': 8.0,
     'L0_attn_gate_w': 8.0,
     'L0_ffn_gate_weight': 8.0,
     'L0_ffn_w1': 8.0,
     'L0_ffn_w2': 8.0,
     'L0_ffn_w3': 8.0,
     'L0_ffn_shared_gate': 8.0,
     'L0_ffn_shared_up': 8.0,
     'L0_ffn_shared_down': 8.0}
    for name, (base, spread) in spreads.items():
        noise = np.random.default_rng([zlib.crc32(name.encode()), seed]).standard_normal(out[name].shape)
        drawn = base * np.exp(spread * noise) if base else spread * noise
        out[name] = jnp.asarray(drawn.astype(out[name].dtype))
    for name, factor in factors.items():
        out[name] = (out[name] * factor).astype(out[name].dtype)
    return out
```

```python
from contextlib import ExitStack

import numpy as np

import concourse.bass as bass
from concourse import mybir

F32 = mybir.dt.float32
F16 = mybir.dt.float16
I32 = mybir.dt.int32
ALU = mybir.AluOpType
ACT = mybir.ActivationFunctionType
AX = mybir.AxisListType.X

P = 128
B, N, D = 32, 256, 256
T = B * N
TILES = T // P
DH = D // P
CODES, HID = 2048, 1024
HC = HID // P
CHUNK = 64
BINS = CHUNK // 2 + 1
LOW = 4
HIGH = BINS - LOW
TAPS = 7
PAD = TAPS - 1
LOWC = 2 * 2 * LOW
SPEC = LOWC + 2 * 2 * HIGH
NH, NKV, HD = 16, 4, 64
GROUPS = TILES // 8
E, TOPK, NG, TG, FF, CAP = 64, 8, 8, 4, 128, 256
HALVES = CAP // P
XW = D + E
SCALE = 2.5
NEG = -1.0e30
COUNT_MAX = 512.0
TRASH = T
CREDIT = 2


def finished(eng, sem, step):
    eng.wait_ge(sem, step + (1 + CREDIT))


def pool_finished(pool, k, sem, step):
    finished(pool, sem, step)
    pool.sem_inc(k.pool_waited, 1)


class Kept:
    pass


class Chain:

    def __init__(self, eng, sem):
        self.eng, self.sem, self.n = eng, sem, 0

    def mark(self, ins):
        ins.then_inc(self.sem, 1)
        self.n += 1
        return self.n

    def reach(self, n):
        self.eng.wait_ge(self.sem, n)

    def link(self, ins):
        self.reach(self.mark(ins))

    def restart(self):
        self.reach(self.n)
        self.eng.sem_clear(self.sem)
        self.n = 0


def shape_constants():
    t = np.arange(CHUNK)[:, None]
    k = np.arange(BINS)[None, :]
    ang = 2 * np.pi * ((t * k) % CHUNK) / CHUNK
    re, im = np.cos(ang), -np.sin(ang)
    im[:, 0] = 0
    im[:, BINS - 1] = 0
    dft = np.zeros((P, SPEC))
    for c in range(2):
        rows = slice(c * CHUNK, (c + 1) * CHUNK)
        for r, m in enumerate((re, im)):
            dft[rows, (c * 2 + r) * LOW:(c * 2 + r + 1) * LOW] = m[:, :LOW]
            at = LOWC + (r * 2 + c) * HIGH
            dft[rows, at:at + HIGH] = m[:, LOW:]
    weight = np.full(BINS, 2.0 / CHUNK)
    weight[0] = weight[-1] = 1.0 / CHUNK
    inv = [(re * weight).T, (im * weight).T]
    low = np.zeros((P, P))
    blk = re[:, :LOW] @ inv[0][:LOW] + im[:, :LOW] @ inv[1][:LOW]
    for c in range(2):
        low[c * CHUNK:(c + 1) * CHUNK, c * CHUNK:(c + 1) * CHUNK] = blk
    rows = 4 * HIGH
    idft_high = np.zeros((rows, 2, 2, P))
    for r in range(2):
        for tile in range(2):
            for c in range(2):
                at = (tile * 2 + c) * HIGH
                idft_high[at:at + HIGH, r, tile, c * CHUNK:(c + 1) * CHUNK] = 0.5 * inv[r][LOW:]
    idft_low = np.zeros((P, 8, P))
    for tile in range(8):
        for c in range(2):
            for r in range(2):
                at = tile * LOWC + (c * 2 + r) * LOW
                idft_low[at:at + LOW, tile, c * CHUNK:(c + 1) * CHUNK] = inv[r][:LOW]
    row = np.arange(P)
    batch, chunk, ri = row // (2 * LOWC), row // (2 * LOW) % 4, row // LOW % 2
    ok = (batch[:, None] == batch) & (ri[:, None] == ri) & (chunk[:, None] >= chunk)
    mask = np.where(ok, 0.0, NEG)
    eye = np.eye(P)
    tri = np.triu(np.ones((P, P)))
    before = (np.arange(NG)[None, :] < np.arange(NG)[:, None]).astype(float)
    tie = np.broadcast_to(np.stack([before, 1 - before]).reshape(1, 2 * NG * NG), (P, 2 * NG * NG))
    slot = np.broadcast_to(np.arange(CAP), (P, CAP))
    cols = np.zeros((P, 8))
    cols[:, 0], cols[:, 1] = row, row + P
    cols[:, 2], cols[:, 3] = TRASH - P + row, TRASH + row
    cols[:, 4] = -0.5
    cols[:, 5] = row % TILES != 0
    f32 = np.concatenate([dft, low, idft_low.reshape(P, -1), mask, eye, tie, cols], 1).astype(np.float32)
    f16 = np.concatenate([slot, eye, (row % TILES)[:, None], np.zeros((P, 1)), tri, np.ones((P, P))], 1).astype(np.float16)
    return f32, idft_high.reshape(rows, -1).astype(np.float32), f16


def build(nc, d, out, sizes):
    ctx = ExitStack()
    with ctx:
        def sb(name, shape, dt=F32):
            return ctx.enter_context(nc.sbuf_tensor(name, shape, dt))

        def sem(name):
            return ctx.enter_context(nc.semaphore(name))

        k = Kept()
        k.dve_chain, k.act_chain, k.pool_chain = sem("dve_chain"), sem("act_chain"), sem("pool_chain")
        k.table = nc.dram_tensor("code_table", [CODES, 2 * D], F32)
        k.token_rows = nc.dram_tensor("token_rows", [T, XW], F32)
        k.z = sb("z", [P, TILES * D])
        k.const = sb("const", [P, sizes["c_f32"]])
        k.idft_high = sb("idft_high", [4 * HIGH, 2, 2, P])
        k.c16 = sb("c16", [P, sizes["c_f16"]], F16)
        at = [0]

        def part(n):
            at[0] += n
            return k.const[:, at[0] - n:at[0]]

        k.dft = part(SPEC)
        k.low_proj = part(P)
        k.idft_low = part(8 * P).rearrange("p (v t) -> p v t", v=8)
        k.mask = part(P)
        k.ident = part(P)
        k.tie = part(2 * NG * NG).rearrange("p (a g h) -> p a g h", a=2, g=NG)
        k.cols = part(8)
        k.slot_row, k.ident16, k.tile_col = k.c16[:, 0:CAP], k.c16[:, CAP:CAP + P], k.c16[:, CAP + P:CAP + P + 1]
        k.tri, k.ones = (k.c16[:, CAP + P + 2 + i * P:CAP + P + 2 + (i + 1) * P] for i in range(2))
        k.idx = sb("idx", [P, TILES], I32)
        k.keep_proj = sb("keep_proj", [P, P])
        k.alpha_raw = sb("alpha_raw", [P, 1])
        k.alpha = sb("alpha", [P, 2])
        k.low_T = sb("low_T", [P, DH, TILES * LOWC])
        k.att = sb("att", [P, GROUPS * D])
        k.counts = sb("counts", [P, 1 + E * TILES], F16)
        k.gather_idx = sb("gather_idx", [P, E, HALVES], I32)
        k.scatter_idx = sb("scatter_idx", [P, E, HALVES], I32)
        k.zeros = sb("zeros", [P, HALVES * D])[:, :]
        k.trash_zeroed, k.trash_stored, k.pool_waited = sem("trash_zeroed"), sem("trash_stored"), sem("pool_waited")
        stage_a(nc, d, k)
        stage_b(nc, d, k)
        stage_c(nc, d, k)
        stage_d(nc, d, k, out)
        stage_e(nc, d, k)
        stage_f(nc, d, k, out)


class Stage:

    def __init__(self, nc, tag):
        self.nc, self.tag, self.ctx = nc, tag, ExitStack()

    def __enter__(self):
        return self

    def __exit__(self, *a):
        return self.ctx.__exit__(*a)

    def sb(self, name, shape, dt=F32):
        return self.ctx.enter_context(self.nc.sbuf_tensor(f"{self.tag}_{name}", shape, dt))

    def bank(self, name, dt=F32):
        return self.ctx.enter_context(self.nc.psum_tensor(f"{self.tag}_ps_{name}", [P, 512], dt))

    def banks(self, name, n):
        return self.ctx.enter_context(self.nc.psum_tensor(f"{self.tag}_ps_{name}", [P, n, 512], F32))

    def sems(self, names):
        return [self.ctx.enter_context(self.nc.semaphore(f"{self.tag}_{n}")) for n in names.split()]

    def block(self):
        return self.ctx.enter_context(self.nc.Block())


def stage_a(nc, d, k):
    with Stage(nc, "a") as st:
        w_loaded, c_loaded = st.sems("w_loaded c_loaded")
        codes_loaded = st.sems("codes0 codes1 codes2 codes3")
        row_stored = st.sems("row_stored0 row_stored1")
        stages = st.sems("up_done gelu_done down_done row_read var_ready rstd_ready row_ready")
        up_done, gelu_done, down_done, row_read, var_ready, rstd_ready, row_ready = stages
        up = [st.bank(f"up{i}") for i in range(2)]
        down = [st.bank(f"down{i}") for i in range(2)]
        used = [0]

        def zpart(n):
            used[0] += n
            return k.z[:, used[0] - n:used[0]]

        codes_T = zpart(DH * CODES).rearrange("p (c n) -> p c n", c=DH)
        w1 = zpart(DH * HID).rearrange("p (c n) -> p c n", c=DH)
        w2 = zpart(HC * D).rearrange("p (c n) -> p c n", c=HC)
        hid = zpart(HC * 512).rearrange("p (c n) -> p c n", c=HC)
        b1, b2 = zpart(HC), zpart(D)
        rows = [zpart(2 * D) for _ in range(2)]
        stats = zpart(6)
        mv, veps, rstd = ([zpart(n) for _ in range(2)] for n in (2, 1, 1))
        block = st.block()

        @block.sync
        def _(sp):
            for s in stages:
                sp.sem_inc(s, CREDIT)
            sp.dma_start(w1, d["tok_W1"].rearrange("(c p) n -> p c n", p=P)).then_inc(w_loaded, 16)
            sp.dma_start(b1, d["tok_b1"]).then_inc(w_loaded, 16)
            codes = d["codes_T"].rearrange("(c p) n -> p c n", p=P)
            for g in range(4):
                sp.dma_start(codes_T[:, :, g * 512:(g + 1) * 512], codes[:, :, g * 512:(g + 1) * 512]
                             ).then_inc(codes_loaded[g], 16)
            sp.dma_start(w2, d["tok_W2"].rearrange("(c p) n -> p c n", p=P)).then_inc(w_loaded, 16)
            sp.dma_start(b2, d["tok_b2"].partition_broadcast(P)).then_inc(w_loaded, 16)
            sp.dma_start(k.const[:, :], d["c_f32"]).then_inc(c_loaded, 16)
            sp.dma_start(k.idft_high[:, :, :, :], d["c_high"].rearrange("p (a b c) -> p a b c", a=2, b=2)
                         ).then_inc(c_loaded, 16)
            sp.dma_start(k.c16[:, :], d["c_f16"]).then_inc(c_loaded, 16)
            sp.dma_start(k.idx[:, :], d["x"]).then_inc(c_loaded, 16)
            sp.dma_start(k.alpha_raw[:, :], d["alpha_raw"].partition_broadcast(P)).then_inc(c_loaded, 16)
            with sp.Fori(0, 4) as g:
                for r in range(4):
                    finished(sp, row_ready, g * 4 + r)
                    sp.dma_start(k.table[bass.ds(g * 512 + r * P, P), :], rows[r % 2]).then_inc(row_stored[r % 2], 16)
            for s in row_stored:
                sp.wait_ge(s, 16 * (CODES // P // 2))

        @block.tensor
        def _(pe):
            pe.wait_ge(w_loaded, 16 * 4)
            for g in range(4):
                pe.wait_ge(codes_loaded[g], 16)
            with pe.Fori(0, 4) as g:
                for h in range(HC):
                    finished(pe, gelu_done, g * HC + (h - 2))
                    for c in range(DH):
                        mm = nc.tensor.matmul(up[h % 2][:, :], w1[:, c, h * P:(h + 1) * P],
                                              codes_T[:, c, bass.ds(g * 512, 512)], start=c == 0, stop=c == DH - 1)
                    mm.then_inc(up_done, 1)
                for r in range(4):
                    if r == 0:
                        finished(pe, gelu_done, g * HC + (HC - 1))
                    finished(pe, row_read, g * 4 + (r - 2))
                    for h in range(HC):
                        mm = nc.tensor.matmul(down[r % 2][:, 0:D], hid[:, h, r * P:(r + 1) * P], w2[:, h, :],
                                              start=h == 0, stop=h == HC - 1)
                    mm.then_inc(down_done, 1)

        @block.scalar
        def _(act):
            act.wait_ge(w_loaded, 16 * 4)
            with act.Fori(0, 4) as g:
                for h in range(HC):
                    finished(act, up_done, g * HC + h)
                    if h == 0:
                        finished(act, down_done, g * 4 - 1)
                    nc.scalar.activation(hid[:, h, :], up[h % 2][:, :], ACT.Gelu_apprx_tanh,
                                         bias=b1[:, h:h + 1]).then_inc(gelu_done, 1)
            ch = Chain(act, k.act_chain)
            act.wait_ge(c_loaded, 16 * 5)
            ch.link(nc.scalar.activation(k.alpha[:, 0:1], k.alpha_raw[:, :], ACT.Sigmoid))
            ch.link(nc.scalar.activation(k.alpha[:, 1:2], k.alpha[:, 0:1], ACT.Copy, scale=-1.0))
            ch.link(nc.scalar.activation(k.keep_proj[:, :], k.low_proj, ACT.Copy, scale=k.alpha[:, 1:2]))
            ch.restart()

        @block.gpsimd
        def _(pool):
            pool.wait_ge(c_loaded, 16 * 5)
            with pool.Fori(0, 8) as i:
                for par in range(2):
                    pool_finished(pool, k, var_ready, 2 * i + par)
                    nc.gpsimd.tensor_tensor(rstd[par], veps[par], k.cols[:, 4:5], ALU.pow).then_inc(rstd_ready, 1)

        @block.vector
        def _(dve):
            ch = Chain(dve, k.dve_chain)
            dve.wait_ge(w_loaded, 16 * 4)
            with dve.Fori(0, 4) as g:
                for r in range(4):
                    m, row = g * 4 + r, rows[r % 2]
                    finished(dve, down_done, m)
                    dve.wait_ge(row_stored[r % 2], g * 32 + 16 * (r // 2))
                    nc.vector.tensor_tensor(row[:, D:2 * D], down[r % 2][:, 0:D], b2, ALU.add).then_inc(row_read, 1)
                    finished(dve, row_read, m)
                    ch.link(nc.vector.bn_stats(stats, row[:, D:2 * D]))
                    ch.link(nc.vector.bn_aggr(mv[r % 2], stats))
                    nc.vector.tensor_scalar(veps[r % 2], mv[r % 2][:, 1:2], 1e-5, None, ALU.add).then_inc(var_ready, 1)
                    finished(dve, rstd_ready, m)
                    nc.vector.tensor_scalar(row[:, 0:D], row[:, D:2 * D], mv[r % 2][:, 0:1], rstd[r % 2],
                                            ALU.subtract, ALU.mult).then_inc(row_ready, 1)
                ch.restart()


def stage_b(nc, d, k):
    with Stage(nc, "b") as st:
        w_loaded, taps_zeroed, keep_added = st.sems("w_loaded pads_zeroed keep_added")
        rows_gathered = st.sems("rows_gathered0 rows_gathered1 rows_gathered2 rows_gathered3")
        idx_ready = st.sems("idx_ready")[0]
        stages = st.sems("dft_done mean_spread gate_mm mixed residual_mm low_copied first_tap gate_ready gelu_done mixed_copied "
                         "conv_done summed z_done")
        (dft_done, mean_spread, gate_mm, mixed, residual_mm, low_copied, first_tap, gate_ready, gelu_done, mixed_copied,
         conv_done, summed, z_done) = stages
        pw = st.sb("pw", [P, 2, DH, D])
        gate_w = st.sb("gate_w", [P, DH, D])
        dw = st.sb("dw", [P, 2, DH, TAPS])
        rows = [st.sb(f"rows{i}", [P, 2, 2 * D]) for i in range(4)]
        tile_idx = [st.sb(f"tile_idx{i}", [P, 2], I32) for i in range(4)]
        low = [st.sb(f"low{i}", [P, 2, DH, LOWC]) for i in range(2)]
        spread = [st.sb(f"spread{i}", [P, 2 * DH * 2, CHUNK]) for i in range(2)]
        high = [st.sb(f"high{i}", [P, DH, 2, 4, PAD + HIGH]) for i in range(2)]
        conv = [st.sb(f"conv{i}", [P, 2, DH, 4, HIGH]) for i in range(2)]
        act_in = [st.sb(f"gelu{i}", [P, 2, DH, 4 * HIGH]) for i in range(2)]
        mix = [st.sb(f"mix{i}", [4 * HIGH, 2, D]) for i in range(2)]
        gate = [st.sb(f"gate{i}", [P, 2 * D]) for i in range(2)]
        total = [st.sb(f"total{i}", [P, 2 * D]) for i in range(2)]
        spec_ps = st.banks("spec", 2)
        gate_ps, mix_ps, back_ps, keep_ps = (st.bank(n) for n in ("gate", "mix", "back", "keep"))
        block = st.block()
        STEPS = B

        def at(i, c):
            return 4 * i + c, c % 4, i + c // 4

        @block.sync
        def _(sp):
            for s in stages:
                sp.sem_inc(s, CREDIT)
            sp.dma_start(pw[:, :, :, :], d["pw_T"].rearrange("r (c p) n -> p r c n", p=P)).then_inc(w_loaded, 16)
            sp.dma_start(gate_w[:, :, :], d["gate_wT"].rearrange("(c p) n -> p c n", p=P)).then_inc(w_loaded, 16)
            sp.dma_start(dw[:, :, :, :], d["dw"].rearrange("p (r c t) -> p r c t", r=2, c=DH)).then_inc(w_loaded, 16)

        @block.gpsimd
        def _(pool):
            def z_add(step):
                s, slot, _ = step
                pool_finished(pool, k, summed, s)
                nc.gpsimd.tensor_tensor(k.z[:, bass.ds(s * 2 * D, 2 * D)].rearrange("p (t n) -> p t n", t=2),
                                        total[slot % 2][:, :].rearrange("p (t n) -> p t n", t=2),
                                        rows[slot][:, :, D:2 * D], ALU.add).then_inc(z_done, 1)

            def gather(step):
                s, slot, _ = step
                nc.gpsimd.tensor_copy(tile_idx[slot][:, :], k.idx[:, bass.ds(s * 2, 2)]).then_inc(idx_ready, 1)
                pool.wait_ge(idx_ready, s + 1)
                pool.sem_inc(k.pool_waited, 1)
                for t in range(2):
                    nc.gpsimd.indirect_dma_start(rows[slot][:, t, :], None, k.table[:, :],
                                                 bass.IndirectOffsetOnAxis(ap=tile_idx[slot][:, t:t + 1], axis=0),
                                                 bounds_check=CODES - 1).then_inc(rows_gathered[slot], 16)

            def spread_mean(step):
                s, slot, _ = step
                pool_finished(pool, k, low_copied, s)
                pool_finished(pool, k, gate_mm, s - 2)
                bins = low[slot % 2][:, :, :, :].rearrange("p t c n -> p (t c n)")[:, 0:2 * DH * LOWC:2 * LOW]
                nc.gpsimd.tensor_copy(spread[slot % 2][:, :, :], bins.unsqueeze(2).to_broadcast([P, 2 * DH * 2, CHUNK])
                                      ).then_inc(mean_spread, 1)

            for c in range(4):
                gather(at(0, c))
            spread_mean(at(0, 0))
            with pool.Fori(0, STEPS // 4 - 1) as i:
                for c in range(4):
                    spread_mean(at(i, c + 1))
                    z_add(at(i, c))
                    pool_finished(pool, k, z_done, 4 * i + c)
                    gather(at(i, c + 4))
            for c in range(STEPS - 4, STEPS):
                if c < STEPS - 1:
                    spread_mean(at(0, c + 1))
                z_add(at(0, c))

        @block.tensor
        def _(pe):
            def spectrum(step):
                s, slot, used = step
                par = slot % 2
                pe.wait_ge(rows_gathered[slot], used * 32 + 32)
                finished(pe, low_copied, s - 1)
                finished(pe, first_tap, s - 1)
                for c in range(DH):
                    for t in range(2):
                        x = rows[slot][:, t, c * P:(c + 1) * P]
                        nc.tensor.matmul(spec_ps[:, c, t * LOWC:(t + 1) * LOWC], x, k.dft[:, 0:LOWC], start=True, stop=True)
                        to = spec_ps[:, c, 2 * LOWC:2 * SPEC].rearrange("p (r t n) -> p r t n", r=2, t=2)[:, :, t, :]
                        mm = nc.tensor.matmul(to, x, k.dft[:, LOWC:SPEC].rearrange("p (r n) -> p r n", r=2),
                                              start=True, stop=True)
                mm.then_inc(dft_done, 1)
                finished(pe, mean_spread, s)
                finished(pe, gate_ready, s - 1)
                for t in range(2):
                    for c in range(DH):
                        q = (t * DH + c) * 2
                        mean = spread[par][:, q:q + 2, :].rearrange("p a n -> p (a n)")
                        mm = nc.tensor.matmul(gate_ps[:, t * D:(t + 1) * D], mean, gate_w[:, c, :],
                                              start=c == 0, stop=c == DH - 1)
                mm.then_inc(gate_mm, 1)

            def mixing(step):
                s, slot, _ = step
                par = slot % 2
                finished(pe, gelu_done, s)
                finished(pe, mixed_copied, s - 1)
                for r in range(2):
                    for c in range(DH):
                        mm = nc.tensor.matmul(mix_ps[0:4 * HIGH, r * D:(r + 1) * D], act_in[par][:, r, c, :], pw[:, r, c, :],
                                              start=c == 0, stop=c == DH - 1)
                mm.then_inc(mixed, 1)
                finished(pe, summed, s - 1)
                for t in range(2):
                    nc.tensor.matmul(keep_ps[:, t * D:(t + 1) * D], k.keep_proj[:, :], rows[slot][:, t, 0:D],
                                     start=True, stop=True)
                finished(pe, mixed_copied, s)
                for t in range(2):
                    for r in range(2):
                        mm = nc.tensor.matmul(back_ps[:, t * D:(t + 1) * D], k.idft_high[:, r, t, :], mix[par][:, r, :],
                                              start=r == 0, stop=r == 1)
                mm.then_inc(residual_mm, 1)

            pe.wait_ge(w_loaded, 16 * 3)
            pe.wait_ge(keep_added, 1)
            def body(i, c):
                if c < STEPS - 1:
                    spectrum(at(i, c + 1))
                mixing(at(i, c))

            spectrum(at(0, 0))
            body(0, 0)
            with pe.Fori(0, STEPS // 4 - 1) as i:
                for c in range(1, 5):
                    body(i, c)
            for c in range(STEPS - 3, STEPS):
                body(0, c)

        @block.scalar
        def _(act):
            ch = Chain(act, k.act_chain)

            def unpack(step):
                s, slot, _ = step
                par = slot % 2
                finished(act, dft_done, s)
                finished(act, mean_spread, s - 2)
                nc.scalar.activation(low[par][:, :, :, :].rearrange("p t c n -> p c t n"),
                                     spec_ps[:, :, 0:2 * LOWC].rearrange("p c (t n) -> p c t n", t=2), ACT.Copy
                                     ).then_inc(low_copied, 1)
                finished(act, conv_done, s - 2)
                ch.link(nc.scalar.activation(high[par][:, :, :, :, PAD:].rearrange("p c r q l -> p c (r q) l"),
                                             spec_ps[:, :, 2 * LOWC:2 * SPEC].rearrange("p c (q l) -> p c q l", l=HIGH),
                                             ACT.Copy))
                finished(act, gelu_done, s - 2)
                for r in range(2):
                    for c in range(DH):
                        last = nc.scalar.activation(conv[par][:, r, c, :, :], high[par][:, c, r, :, 0:HIGH],
                                                    ACT.Copy, scale=dw[:, r, c, 0:1])
                last.then_inc(first_tap, 1)
                finished(act, low_copied, s)
                for t in range(2):
                    ch.mark(nc.scalar.activation(k.low_T[:, :, bass.ds(s * 2 * LOWC + t * LOWC, LOWC)],
                                                 low[par][:, t, :, :], ACT.Copy))
                finished(act, gate_mm, s)
                finished(act, summed, s - 2)
                nc.scalar.activation(gate[par][:, :], gate_ps[:, :], ACT.Tanh, scale=0.5 / CHUNK).then_inc(gate_ready, 1)

            def rest(step):
                s, slot, _ = step
                par = slot % 2
                finished(act, conv_done, s)
                finished(act, mixed, s - 2)
                nc.scalar.activation(act_in[par][:, :, :, :].rearrange("p r c l -> p (r c l)"), conv[par][:, :, :, :, :].rearrange("p r c q l -> p (r c q l)"),
                                     ACT.Gelu).then_inc(gelu_done, 1)
                finished(act, mixed, s)
                finished(act, residual_mm, s - 2)
                nc.scalar.activation(mix[par][:, :, :].rearrange("p r n -> p (r n)"), mix_ps[0:4 * HIGH, :],
                                     ACT.Copy).then_inc(mixed_copied, 1)

            act.wait_ge(w_loaded, 16 * 3)
            act.wait_ge(taps_zeroed, 2)
            def body(i, c):
                if c < STEPS - 1:
                    unpack(at(i, c + 1))
                rest(at(i, c))

            unpack(at(0, 0))
            body(0, 0)
            ch.restart()
            with act.Fori(0, STEPS // 4 - 1) as i:
                for c in range(1, 5):
                    body(i, c)
                ch.restart()
            for c in range(STEPS - 3, STEPS):
                body(0, c)
            ch.restart()

        @block.vector
        def _(dve):
            ch = Chain(dve, k.dve_chain)

            def convolve(step):
                s, slot, _ = step
                par = slot % 2
                finished(dve, first_tap, s)
                done = [ch.n] * 4
                for tap in range(1, TAPS):
                    for g in range(4):
                        r, c = divmod(g, 2)
                        if tap > 1:
                            ch.reach(done[g])
                        acc = conv[par][:, r, c, :, :]
                        ins = nc.vector.scalar_tensor_tensor(out=acc, in0=high[par][:, c, r, :, tap:tap + HIGH],
                                                             scalar=dw[:, r, c, tap:tap + 1], in1=acc,
                                                             op0=ALU.mult, op1=ALU.add)
                        if tap == TAPS - 1 and g == 3:
                            ins.then_inc(conv_done, 1)
                        else:
                            done[g] = ch.mark(ins)

            def sum_up(step):
                s, slot, _ = step
                par = slot % 2
                finished(dve, residual_mm, s)
                finished(dve, gate_ready, s)
                finished(dve, z_done, s - 2)
                ch.link(nc.vector.scalar_tensor_tensor(out=total[par][:, :], in0=gate[par][:, :], scalar=1.0,
                                                       in1=back_ps[:, :], op0=ALU.add, op1=ALU.mult))
                nc.vector.tensor_tensor(total[par][:, :], keep_ps[:, :], total[par][:, :], ALU.add).then_inc(summed, 1)

            for t in range(2):
                nc.vector.memset(high[t][:, :, :, :, 0:PAD].rearrange("p c r q l -> p (c r q) l"), 0.0
                                 ).then_inc(taps_zeroed, 1)
            nc.vector.tensor_tensor(k.keep_proj[:, :], k.keep_proj[:, :], k.ident, ALU.add).then_inc(keep_added, 1)
            dve.wait_ge(w_loaded, 16 * 3)
            def body(i, c):
                if c > 0:
                    sum_up(at(i, c - 1))
                if c < STEPS - 1:
                    convolve(at(i, c + 1))

            convolve(at(0, 0))
            body(0, 0)
            ch.restart()
            with dve.Fori(0, STEPS // 4 - 1) as i:
                for c in range(1, 5):
                    body(i, c)
                ch.restart()
            for c in range(STEPS - 3, STEPS):
                body(0, c)
            sum_up(at(0, STEPS - 1))
            ch.restart()


def stage_c(nc, d, k):
    with Stage(nc, "c") as st:
        w_loaded = st.sems("w_loaded")[0]
        stages = st.sems("rows_ready q_mm kv_mm q_copied kv_copied scores_mm biased max_ready exp_done normed turned "
                         "turned_act turned_dve values_mm values_act values_dve out_mm out_copied")
        (rows_ready, q_mm, kv_mm, q_copied, kv_copied, scores_mm, biased, max_ready, exp_done, normed, turned,
         turned_act, turned_dve, values_mm, values_act, values_dve, out_mm, out_copied) = stages
        q_w = st.sb("q_w", [P, DH, NH * HD])
        k_w = st.sb("k_w", [P, DH, NKV * 2 * HD])
        v_w = st.sb("v_w", [P, DH, NKV * HD])
        o_w = st.sb("o_w", [P, NH // 2, D])
        rows = st.sb("rows", [P, DH, P])
        qT = st.sb("qT", [P, NH // 2, P])
        kT = st.sb("kT", [P, NKV, P])
        v = st.sb("v", [P, NKV * HD])
        prob = st.sb("prob", [P, 4, 4, P])
        probT = st.sb("probT", [P, 4, 4, P])
        top = st.sb("top", [P, 4, 4])
        shift = st.sb("shift", [P, 4, 4])
        rsum = st.sb("rsum", [P, 4, 4])
        rinv = st.sb("rinv", [P, 4, 4])
        vals = st.sb("vals", [P, NH // 2, P])
        psA, psB = st.banks("A", 4), st.banks("B", 4)
        block = st.block()
        INV = 1.0 / float(np.sqrt(HD))

        @block.sync
        def _(sp):
            for s in stages:
                sp.sem_inc(s, CREDIT)
            for w, name in ((q_w, "q_T"), (k_w, "k_T"), (v_w, "v_T"), (o_w, "o_T")):
                sp.dma_start(w[:, :, :], d[name].rearrange("(c p) n -> p c n", p=P)).then_inc(w_loaded, 16)

        @block.gpsimd
        def _(pool):
            with pool.Fori(0, GROUPS) as g:
                pool_finished(pool, k, kv_mm, g - 1)
                nc.gpsimd.tensor_copy(rows[:, :, :], k.low_T[:, :, bass.ds(g * P, P)]).then_inc(rows_ready, 1)

        @block.tensor
        def _(pe):
            pe.wait_ge(w_loaded, 16 * 4)
            with pe.Fori(0, GROUPS) as g:
                finished(pe, rows_ready, g)
                finished(pe, turned_act, g - 1)
                finished(pe, turned_dve, g - 1)
                for hp in range(NH // 2):
                    for c in range(DH):
                        mm = nc.tensor.matmul(psA[:, hp // 4, hp % 4 * P:(hp % 4 + 1) * P], q_w[:, c, hp * P:(hp + 1) * P],
                                              rows[:, c, :], start=c == 0, stop=c == DH - 1)
                mm.then_inc(q_mm, 1)
                for j in range(NKV):
                    for c in range(DH):
                        nc.tensor.matmul(psA[:, 2, j * P:(j + 1) * P], k_w[:, c, j * P:(j + 1) * P], rows[:, c, :],
                                         start=c == 0, stop=c == DH - 1)
                for c in range(DH):
                    mm = nc.tensor.matmul(psA[:, 3, 0:NKV * HD], rows[:, c, :], v_w[:, c, :], start=c == 0, stop=c == DH - 1)
                mm.then_inc(kv_mm, 1)
                finished(pe, q_copied, g)
                finished(pe, kv_copied, g)
                finished(pe, values_act, g - 1)
                finished(pe, values_dve, g - 1)
                finished(pe, out_copied, g - 1)
                for n in range(4):
                    jj, parity = divmod(n, 2)
                    for i in range(4):
                        h = 8 * jj + parity + 2 * i
                        half = slice(parity * HD, (parity + 1) * HD)
                        mm = nc.tensor.matmul(psB[:, n, i * P:(i + 1) * P], qT[half, h // 2, :], kT[half, h // 4, :],
                                              start=True, stop=True)
                    mm.then_inc(scores_mm, 1)
                for n in range(4):
                    finished(pe, normed, g * 4 + n)
                    if n == 0:
                        finished(pe, q_copied, g)
                    for i in range(4):
                        mm = nc.tensor.transpose(psA[:, n, i * P:(i + 1) * P], prob[:, n, i, :], k.ident)
                    mm.then_inc(turned, 1)
                finished(pe, turned_act, g)
                finished(pe, turned_dve, g)
                for jj in range(2):
                    for parity in range(2):
                        for half in range(2):
                            j = 2 * jj + half
                            mm = nc.tensor.matmul(psB[parity * HD:(parity + 1) * HD, jj, half * 2 * P:(half + 1) * 2 * P],
                                                  v[:, j * HD:(j + 1) * HD],
                                                  probT[:, 2 * jj + parity, 2 * half:2 * half + 2, :].rearrange("p i n -> p (i n)"),
                                                  start=True, stop=True)
                mm.then_inc(values_mm, 1)
                finished(pe, values_act, g)
                finished(pe, values_dve, g)
                for hp in range(NH // 2):
                    mm = nc.tensor.matmul(psB[:, 2, 0:D], vals[:, hp, :], o_w[:, hp, :], start=hp == 0, stop=hp == NH // 2 - 1)
                mm.then_inc(out_mm, 1)

        @block.scalar
        def _(act):
            with act.Fori(0, GROUPS) as g:
                finished(act, q_mm, g)
                nc.scalar.activation(qT[:, :, :].rearrange("p h n -> p (h n)"),
                                     psA[:, 0:2, :].rearrange("p a n -> p (a n)"), ACT.Copy).then_inc(q_copied, 1)
                for n in range(4):
                    finished(act, max_ready, g * 4 + n)
                    for i in range(4):
                        ins = nc.scalar.activation(prob[:, n, i, :], prob[:, n, i, :], ACT.Exp, scale=INV,
                                                   bias=shift[:, n, i:i + 1], accum_out=rsum[:, n, i:i + 1])
                    ins.then_inc(exp_done, 1)
                for n in range(2):
                    finished(act, turned, g * 4 + n)
                finished(act, values_mm, g - 1)
                nc.scalar.activation(probT[:, 0:2, :, :].rearrange("p a i n -> p (a i n)"),
                                     psA[:, 0:2, :].rearrange("p a n -> p (a n)"), ACT.Copy).then_inc(turned_act, 1)
                finished(act, values_mm, g)
                finished(act, out_mm, g - 1)
                nc.scalar.activation(vals[:, 0:4, :].rearrange("p h n -> p (h n)"), psB[:, 0, :], ACT.Copy
                                     ).then_inc(values_act, 1)
                finished(act, out_mm, g)
                nc.scalar.activation(k.att[:, bass.ds(g * D, D)], psB[:, 2, 0:D], ACT.Copy, scale=k.alpha[:, 0:1]
                                     ).then_inc(out_copied, 1)

        @block.vector
        def _(dve):
            ch = Chain(dve, k.dve_chain)
            with dve.Fori(0, GROUPS) as g:
                finished(dve, kv_mm, g)
                nc.vector.tensor_copy(kT[:, :, :].rearrange("p j n -> p (j n)"), psA[:, 2, :])
                nc.vector.tensor_copy(v[:, :], psA[:, 3, 0:NKV * HD]).then_inc(kv_copied, 1)
                for n in range(4):
                    finished(dve, scores_mm, g * 4 + n)
                    finished(dve, turned, g * 4 + (n - 4) if n == 3 else g * 4 - 1)
                    ch.link(nc.vector.tensor_tensor(prob[:, n, :, :], psB[:, n, :].rearrange("p (i n) -> p i n", i=4),
                                                    k.mask.unsqueeze(1).to_broadcast([P, 4, P]), ALU.add))
                    ch.link(nc.vector.tensor_reduce(top[:, n, :], prob[:, n, :, :], AX, ALU.max))
                    nc.vector.tensor_scalar(shift[:, n, :], top[:, n, :], -INV, None, ALU.mult).then_inc(max_ready, 1)
                for n in range(4):
                    finished(dve, exp_done, g * 4 + n)
                    ch.link(nc.vector.reciprocal(rinv[:, n, :], rsum[:, n, :]))
                    nc.vector.tensor_tensor(prob[:, n, :, :], prob[:, n, :, :],
                                            rinv[:, n, :].unsqueeze(2).to_broadcast([P, 4, P]), ALU.mult
                                            ).then_inc(normed, 1)
                for n in range(2, 4):
                    finished(dve, turned, g * 4 + n)
                finished(dve, values_mm, g - 1)
                nc.vector.tensor_copy(probT[:, 2:4, :, :].rearrange("p a i n -> p (a i n)"),
                                      psA[:, 2:4, :].rearrange("p a n -> p (a n)")).then_inc(turned_dve, 1)
                finished(dve, values_mm, g)
                finished(dve, out_mm, g - 1)
                nc.vector.tensor_copy(vals[:, 4:8, :].rearrange("p h n -> p (h n)"), psB[:, 1, :]).then_inc(values_dve, 1)
                ch.restart()


def stage_d(nc, d, k, out):
    QT = 4
    STEPS = TILES // QT
    QE = QT * E
    with Stage(nc, "d") as st:
        w_loaded, counts_zeroed = st.sems("w_loaded counts_zeroed")
        rows_stored = st.sems("rows_stored0 rows_stored1")
        out_stored = st.sems("out_stored0 out_stored1")
        stages = st.sems("low_mm h_ready var_ready rstd_ready x_ready turned xT_ready route_mm scores_ready chosen counts_mm "
                         "counted total_ready up_mm silu_done hidden_ready down_mm out_ready rows_ready")
        (low_mm, h_ready, var_ready, rstd_ready, x_ready, turned, xT_ready, route_mm, scores_ready, chosen, counts_mm,
         counted, total_ready, up_mm, silu_done, hidden_ready, down_mm, out_ready, rows_ready) = stages
        route = st.sb("route", [P, DH, E])
        shared = st.sb("shared", [P, DH, 2 * D])
        down = st.sb("down", [P, DH, D])
        bias = st.sb("bias", [P, E])
        h = [st.sb(f"h{i}", [P, QT, D]) for i in range(2)]
        x = [st.sb(f"x{i}", [P, QT, XW]) for i in range(2)]
        xT = [st.sb(f"xT{i}", [P, DH, QT * P]) for i in range(2)]
        stats = st.sb("stats", [P, QT, 6])
        mv = st.sb("mv", [P, QT, 2])
        veps = st.sb("veps", [P, QT])
        rstd = st.sb("rstd", [P, QT])
        scores = st.sb("scores", [P, QE])
        biased = st.sb("biased", [P, QE])
        m1, n1 = st.sb("m1", [P, QT * NG * 4]), st.sb("n1", [P, QT * NG * 4])
        m2, n2, l2 = (st.sb(n, [P, QT * NG * 2]) for n in ("m2", "n2", "l2"))
        m3, n3, l3 = (st.sb(n, [P, QT * NG]) for n in ("m3", "n3", "l3"))
        ge, gt = st.sb("ge", [P, QT, NG * NG]), st.sb("gt", [P, QT, NG * NG])
        best = st.sb("best", [P, QT, 8])
        taken = st.sb("taken", [P, QE])
        sel = st.sb("sel", [P, QE], F16)
        sel_sum = st.sb("sel_sum", [P, E])
        before = st.sb("before", [P, E], F16)
        wsum, winv = st.sb("wsum", [P, QT]), st.sb("winv", [P, QT])
        silu = [st.sb(f"silu{i}", [P, QT * P]) for i in range(2)]
        hidden = [st.sb(f"hidden{i}", [P, QT * P]) for i in range(2)]
        res = [st.sb(f"res{i}", [P, QT, D]) for i in range(2)]
        low_ps, x_ps = st.banks("low", 2), st.banks("x", 2)
        route_ps, count_ps = st.bank("route"), st.bank("count")
        gate_ps, up_ps = st.bank("gate"), st.bank("up")
        block = st.block()

        @block.sync
        def _(sp):
            for s in stages:
                sp.sem_inc(s, CREDIT)
            sp.dma_start(route[:, :, :], d["route_T"].rearrange("(c p) n -> p c n", p=P)).then_inc(w_loaded, 16)
            sp.dma_start(shared[:, :, :], d["shared_T"].rearrange("(c p) n -> p c n", p=P)).then_inc(w_loaded, 16)
            sp.dma_start(down[:, :, :], d["down_T"].rearrange("(c p) n -> p c n", p=P)).then_inc(w_loaded, 16)
            sp.dma_start(bias[:, :], d["e_bias"].partition_broadcast(P)).then_inc(w_loaded, 16)
            with sp.Fori(0, STEPS // 2) as i:
                for par in range(2):
                    s = 2 * i + par
                    finished(sp, rows_ready, s)
                    finished(sp, x_ready, s)
                    sp.dma_start(k.token_rows[bass.ds(s * QT * P, QT * P), :].rearrange("(t p) n -> p t n", p=P),
                                 x[par][:, :, :]).then_inc(rows_stored[par], 16)
                    finished(sp, out_ready, s)
                    sp.dma_start(out[bass.ds(s * QT * P, QT * P), :].rearrange("(t p) n -> p t n", p=P),
                                 res[par][:, :, :]).then_inc(out_stored[par], 16)
            for s in rows_stored + out_stored:
                sp.wait_ge(s, 16 * (STEPS // 2))

        @block.gpsimd
        def _(pool):
            pool.wait_ge(k.trash_zeroed, 1)
            pool.dma_start(out[T:T + CAP, :].rearrange("(t p) n -> p t n", p=P),
                           k.zeros.rearrange("p (t n) -> p t n", t=HALVES)).then_inc(k.trash_stored, 16)
            with pool.Fori(0, STEPS) as s:
                pool_finished(pool, k, var_ready, s)
                nc.gpsimd.tensor_tensor(rstd[:, :], veps[:, :], k.cols[:, 4:5].to_broadcast([P, QT]), ALU.pow
                                        ).then_inc(rstd_ready, 1)
            pool.wait_ge(k.trash_stored, 16)

        @block.tensor
        def _(pe):
            def step(i, par):
                s = 2 * i + par
                finished(pe, h_ready, s - 1)
                for t in range(QT):
                    mm = nc.tensor.matmul(low_ps[:, t // 2, t % 2 * D:(t % 2 + 1) * D], k.idft_low[:, QT * par + t, :],
                                          k.att[:, bass.ds(i * D, D)], start=True, stop=True)
                mm.then_inc(low_mm, 1)
                finished(pe, x_ready, s)
                finished(pe, out_ready, s - 1)
                for t in range(QT):
                    for c in range(DH):
                        mm = nc.tensor.transpose(x_ps[:, c, t * P:(t + 1) * P], x[par][:, t, c * P:(c + 1) * P], k.ident)
                mm.then_inc(turned, 1)
                finished(pe, xT_ready, s)
                finished(pe, scores_ready, s - 1)
                for t in range(QT):
                    for c in range(DH):
                        mm = nc.tensor.matmul(route_ps[:, t * E:(t + 1) * E], xT[par][:, c, t * P:(t + 1) * P], route[:, c, :],
                                              start=c == 0, stop=c == DH - 1)
                mm.then_inc(route_mm, 1)
                for f in range(2):
                    finished(pe, hidden_ready, s * 2 + (f - 1))
                    for ps, o in ((gate_ps, 0), (up_ps, D)):
                        for c in range(DH):
                            mm = nc.tensor.matmul(ps[:, :], shared[:, c, o + f * P:o + (f + 1) * P], xT[par][:, c, :],
                                                  start=c == 0, stop=c == DH - 1)
                    mm.then_inc(up_mm, 1)
                finished(pe, hidden_ready, s * 2 + 1)
                for t in range(QT):
                    for f in range(2):
                        mm = nc.tensor.matmul(x_ps[:, t // 2, t % 2 * D:(t % 2 + 1) * D], hidden[f][:, t * P:(t + 1) * P],
                                              down[:, f, :], start=f == 0, stop=f == 1)
                mm.then_inc(down_mm, 1)
                finished(pe, chosen, s)
                finished(pe, total_ready, s - 1)
                finished(pe, counted, s - 1)
                for t in range(QT):
                    to = count_ps[:, t * E:(t + 1) * E]
                    nc.tensor.matmul(to, k.ones, before[:, :], start=True, stop=False)
                    for u in range(t):
                        nc.tensor.matmul(to, k.ones, sel[:, u * E:(u + 1) * E], start=False, stop=False)
                    mm = nc.tensor.matmul(to, k.tri, sel[:, t * E:(t + 1) * E], start=False, stop=True)
                mm.then_inc(counts_mm, 1)

            pe.wait_ge(w_loaded, 16 * 4)
            pe.wait_ge(counts_zeroed, 2)
            with pe.Fori(0, STEPS // 2) as i:
                for par in range(2):
                    step(i, par)

        @block.scalar
        def _(act):
            with act.Fori(0, STEPS // 2) as i:
                for par in range(2):
                    s = 2 * i + par
                    finished(act, turned, s)
                    finished(act, down_mm, s - 2)
                    nc.scalar.activation(xT[par][:, :, :].rearrange("p c n -> p (c n)"),
                                         x_ps[:, :, :].rearrange("p c n -> p (c n)"), ACT.Copy).then_inc(xT_ready, 1)
                    finished(act, route_mm, s)
                    finished(act, chosen, s - 1)
                    finished(act, rows_ready, s - 1)
                    nc.scalar.activation(scores[:, :], route_ps[:, 0:QE], ACT.Sigmoid).then_inc(scores_ready, 1)
                    for f in range(2):
                        finished(act, up_mm, s * 2 + f)
                        finished(act, hidden_ready, s * 2 + (f - 2))
                        nc.scalar.activation(silu[f][:, :], gate_ps[:, :], ACT.Sigmoid).then_inc(silu_done, 1)

        @block.vector
        def _(dve):
            ch = Chain(dve, k.dve_chain)

            def tt(o, a, b, op):
                return nc.vector.tensor_tensor(o, a, b, op)

            def token_norm(s, par):
                finished(dve, low_mm, s)
                finished(dve, out_ready, s - 2)
                for b in range(2):
                    ch.mark(tt(h[par][:, 2 * b:2 * b + 2, :].rearrange("p t n -> p (t n)"), low_ps[:, b, :],
                               k.z[:, bass.ds(s * QT * D + b * 2 * D, 2 * D)], ALU.add))
                nc.vector.tensor_copy(veps[:, :], k.cols[:, 4:5].to_broadcast([P, QT])).then_inc(h_ready, 1)
                ch.reach(ch.n)
                for t in range(QT):
                    ch.mark(nc.vector.bn_stats(stats[:, t, :], h[par][:, t, :]))
                ch.reach(ch.n)
                for t in range(QT):
                    ch.mark(nc.vector.bn_aggr(mv[:, t, :], stats[:, t, :]))
                ch.reach(ch.n)
                finished(dve, h_ready, s)
                nc.vector.tensor_scalar(veps[:, :], mv[:, :, 1], 1e-5, None, ALU.add).then_inc(var_ready, 1)
                finished(dve, rstd_ready, s)
                dve.wait_ge(rows_stored[par], (s - par) * 8)
                for t in range(QT):
                    ins = nc.vector.tensor_scalar(x[par][:, t, 0:D], h[par][:, t, :], mv[:, t, 0:1], rstd[:, t:t + 1],
                                                  ALU.subtract, ALU.mult)
                ins.then_inc(x_ready, 1)

            def choose(s, par):
                finished(dve, scores_ready, s)
                ch.link(tt(biased[:, :].rearrange("p (t e) -> p t e", t=QT), scores[:, :].rearrange("p (t e) -> p t e", t=QT),
                           bias[:, :].unsqueeze(1).to_broadcast([P, QT, E]), ALU.add))
                v = biased[:, :].rearrange("p (g a) -> p g a", a=2)
                ch.mark(tt(m1[:, :], v[:, :, 0], v[:, :, 1], ALU.max))
                ch.link(tt(n1[:, :], v[:, :, 0], v[:, :, 1], ALU.min))
                for (m, n), (mo, no, lo) in (((m1, n1), (m2, n2, l2)), ((m2, n2), (m3, n3, l3))):
                    mm, nn = (q[:, :].rearrange("p (g a) -> p g a", a=2) for q in (m, n))
                    ch.mark(tt(mo[:, :], mm[:, :, 0], mm[:, :, 1], ALU.max))
                    ch.mark(tt(lo[:, :], mm[:, :, 0], mm[:, :, 1], ALU.min))
                    ch.link(tt(no[:, :], nn[:, :, 0], nn[:, :, 1], ALU.max))
                    ch.link(tt(no[:, :], no[:, :], lo[:, :], ALU.max))
                ch.link(tt(m3[:, :], m3[:, :], n3[:, :], ALU.add))
                gs = m3[:, :].rearrange("p (t g) -> p t g", t=QT)
                for t in range(QT):
                    other = gs[:, t, :].unsqueeze(1).to_broadcast([P, NG, NG])
                    own = gs[:, t, :].unsqueeze(2).to_broadcast([P, NG, NG])
                    ch.mark(tt(ge[:, t, :].rearrange("p (g o) -> p g o", g=NG), other, own, ALU.is_ge))
                    ch.mark(tt(gt[:, t, :].rearrange("p (g o) -> p g o", g=NG), other, own, ALU.is_gt))
                ch.reach(ch.n)
                for q, a in ((ge, 0), (gt, 1)):
                    ch.mark(tt(q[:, :, :], q[:, :, :], k.tie[:, a, :, :].rearrange("p g o -> p (g o)").unsqueeze(1)
                               .to_broadcast([P, QT, NG * NG]), ALU.mult))
                ch.reach(ch.n)
                ch.link(tt(ge[:, :, :], ge[:, :, :], gt[:, :, :], ALU.add))
                ch.link(nc.vector.tensor_reduce(l3[:, :], ge[:, :, :].rearrange("p t (g o) -> p (t g) o", g=NG), AX, ALU.add))
                ch.link(nc.vector.tensor_scalar(l3[:, :], l3[:, :], float(TG), None, ALU.is_lt))
                ch.link(tt(biased[:, :].rearrange("p (g e) -> p g e", e=E // NG),
                           biased[:, :].rearrange("p (g e) -> p g e", e=E // NG),
                           l3[:, :].unsqueeze(2).to_broadcast([P, QT * NG, E // NG]), ALU.mult))
                for t in range(QT):
                    ch.mark(nc.vector.max(best[:, t, :], biased[:, t * E:(t + 1) * E]))
                ch.reach(ch.n)
                for t in range(QT):
                    ch.mark(nc.vector.match_replace(taken[:, t * E:(t + 1) * E], best[:, t, :],
                                                    biased[:, t * E:(t + 1) * E], NEG))
                ch.reach(ch.n)
                finished(dve, counts_mm, s - 1)
                tt(sel[:, :], taken[:, :], biased[:, :], ALU.not_equal).then_inc(chosen, 1)
                finished(dve, chosen, s)

            def weights(s, par):
                w = x[par][:, :, D:XW]
                ch.link(tt(w, scores[:, :].rearrange("p (t e) -> p t e", t=QT), sel[:, :].rearrange("p (t e) -> p t e", t=QT),
                           ALU.mult))
                ch.link(nc.vector.tensor_reduce(wsum[:, :], w, AX, ALU.add))
                ch.link(nc.vector.tensor_scalar(wsum[:, :], wsum[:, :], 1e-20, None, ALU.add))
                ch.link(nc.vector.reciprocal(winv[:, :], wsum[:, :]))
                nc.vector.scalar_tensor_tensor(out=w, in0=w, scalar=SCALE, in1=winv[:, :].unsqueeze(2).to_broadcast([P, QT, E]),
                                               op0=ALU.mult, op1=ALU.mult).then_inc(rows_ready, 1)

            def shared_expert(s, par):
                for f in range(2):
                    finished(dve, silu_done, s * 2 + f)
                    finished(dve, down_mm, s - 1)
                    ch.link(tt(silu[f][:, :], gate_ps[:, :], silu[f][:, :], ALU.mult))
                    tt(hidden[f][:, :], up_ps[:, :], silu[f][:, :], ALU.mult).then_inc(hidden_ready, 1)

            def count(s):
                finished(dve, counts_mm, s)
                to = k.counts[:, 1:].rearrange("p (e t) -> p t e", e=E)[:, bass.ds(s * QT, QT), :]
                nc.vector.tensor_scalar(to, count_ps[:, 0:QE].rearrange("p (t e) -> p t e", t=QT), COUNT_MAX, None, ALU.min
                                        ).then_inc(counted, 1)
                ch.link(nc.vector.tensor_reduce(sel_sum[:, :], sel[:, :].rearrange("p (t e) -> p e t", t=QT), AX, ALU.add))
                tt(before[:, :], before[:, :], sel_sum[:, :], ALU.add).then_inc(total_ready, 1)

            ch.link(nc.vector.memset(k.zeros, 0.0))
            nc.vector.memset(before[:, :], 0.0).then_inc(counts_zeroed, 1)
            nc.vector.memset(k.counts[:, 0:1], 0.0).then_inc(counts_zeroed, 1)
            nc.vector.memset(l3[:, :], 0.0).then_inc(k.trash_zeroed, 1)
            ch.restart()
            dve.wait_ge(w_loaded, 16 * 4)
            with dve.Fori(0, STEPS // 2) as i:
                for par in range(2):
                    s = 2 * i + par
                    token_norm(s, par)
                    shared_expert(s, par)
                    choose(s, par)
                    weights(s, par)
                    finished(dve, down_mm, s)
                    dve.wait_ge(out_stored[par], i * 16)
                    for b in range(2):
                        ins = tt(res[par][:, 2 * b:2 * b + 2, :].rearrange("p t n -> p (t n)"), x_ps[:, b, :],
                                 h[par][:, 2 * b:2 * b + 2, :].rearrange("p t n -> p (t n)"), ALU.add)
                    ins.then_inc(out_ready, 1)
                    count(s)
                ch.restart()


def stage_e(nc, d, k):
    STEPS = E // 2
    with Stage(nc, "e") as st:
        stages = st.sems("counts_mm copied bounds_ready tile_found picked compared indices_ready col_ready")
        counts_mm, copied, bounds_ready, tile_found, picked, compared, indices_ready, col_ready = stages
        cts = [st.sb(f"cts{i}", [P, P], F16) for i in range(2)]
        bounds = [st.sb(f"bounds{i}", [P, 2]) for i in range(2)]
        hot = [st.sb(f"hot{i}", [P, CAP], F16) for i in range(2)]
        below = st.sb("below", [P, 2, HALVES, P])
        fine = st.sb("fine", [P, 2 * HALVES])
        token = st.sb("token", [P, 2 * HALVES])
        empty = st.sb("empty", [P, 2 * HALVES])
        col_ps = [st.bank(f"col{i}") for i in range(2)]
        pick_ps = [st.banks(f"pick{i}", 2) for i in range(2)]
        block = st.block()

        @block.sync
        def _(sp):
            for s in stages:
                sp.sem_inc(s, CREDIT)

        @block.tensor
        def _(pe):
            def columns(s, par):
                finished(pe, copied, s - 2)
                finished(pe, bounds_ready, s - 2)
                now = k.counts[:, bass.ds(s * P + 1, P)]
                last = k.counts[:, bass.ds(s * P, P)]
                nc.tensor.matmul(col_ps[par][:, 0:P], now, k.ident16, start=True, stop=True)
                nc.tensor.matmul(col_ps[par][:, P:P + 1], last, k.ident16[:, P - 1:P], start=True, stop=True
                                 ).then_inc(counts_mm, 1)

            def pick(s, par):
                finished(pe, tile_found, s)
                finished(pe, copied, s)
                finished(pe, compared, s - 2)
                for e in range(2):
                    rows = slice(e * TILES, (e + 1) * TILES)
                    for hf in range(HALVES):
                        w = hot[par][rows, hf * P:(hf + 1) * P]
                        nc.tensor.matmul(pick_ps[par][:, e, hf * P:(hf + 1) * P], w, cts[par][rows, :], start=True, stop=True)
                        mm = nc.tensor.matmul(pick_ps[par][:, e, CAP + hf:CAP + hf + 1], w, k.tile_col[rows, :],
                                              start=True, stop=True)
                mm.then_inc(picked, 1)

            columns(0, 0)
            with pe.Fori(0, STEPS // 2 - 1) as i:
                for par in range(2):
                    s = 2 * i + par
                    columns(s + 1, 1 - par)
                    pick(s, par)
            columns(STEPS - 1, 1)
            pick(STEPS - 2, 0)
            pick(STEPS - 1, 1)

        @block.scalar
        def _(act):
            with act.Fori(0, STEPS // 2) as i:
                for par in range(2):
                    s = 2 * i + par
                    finished(act, counts_mm, s)
                    finished(act, tile_found, s - 2)
                    nc.scalar.activation(bounds[par][:, 0:1], col_ps[par][:, P - 1:P], ACT.Copy)
                    nc.scalar.activation(bounds[par][:, 1:2], col_ps[par][:, P:P + 1], ACT.Copy, scale=k.cols[:, 5:6]
                                         ).then_inc(bounds_ready, 1)
                    finished(act, picked, s - 2)
                    nc.scalar.activation(cts[par][:, :], col_ps[par][:, 0:P], ACT.Copy).then_inc(copied, 1)

        @block.vector
        def _(dve):
            ch = Chain(dve, k.dve_chain)

            def find_tile(s, par):
                finished(dve, bounds_ready, s)
                finished(dve, picked, s - 2)
                ch.link(nc.vector.tensor_scalar(hot[par][:, :], k.slot_row, bounds[par][:, 1:2], None, ALU.is_ge))
                nc.vector.scalar_tensor_tensor(out=hot[par][:, :], in0=k.slot_row, scalar=bounds[par][:, 0:1],
                                               in1=hot[par][:, :], op0=ALU.is_lt, op1=ALU.mult).then_inc(tile_found, 1)

            def find_token(s, par):
                finished(dve, picked, s)
                for hf in range(HALVES):
                    ch.mark(nc.vector.tensor_scalar(below[:, :, hf, :], pick_ps[par][:, :, hf * P:(hf + 1) * P],
                                                    k.cols[:, hf:hf + 1], None, ALU.is_le))
                ch.reach(ch.n)
                ch.link(nc.vector.tensor_reduce(fine[:, :], below[:, :, :, :].rearrange("p e h n -> p (e h) n"), AX, ALU.add))
                ch.mark(nc.vector.tensor_scalar(empty[:, :], fine[:, :], P - 0.5, None, ALU.is_ge))
                nc.vector.scalar_tensor_tensor(out=token[:, :].rearrange("p (e h) -> p e h", e=2),
                                               in0=pick_ps[par][:, :, CAP:CAP + HALVES], scalar=float(P),
                                               in1=fine[:, :].rearrange("p (e h) -> p e h", e=2),
                                               op0=ALU.mult, op1=ALU.add).then_inc(compared, 1)
                finished(dve, compared, s)
                ch.reach(ch.n)
                pair = token[:, :].rearrange("p (e h) -> p e h", e=2)
                ch.mark(nc.vector.tensor_copy(k.gather_idx[:, bass.ds(2 * s, 2), :], pair))
                ch.link(nc.vector.tensor_tensor(empty[:, :].rearrange("p (e h) -> p e h", e=2),
                                                empty[:, :].rearrange("p (e h) -> p e h", e=2),
                                                k.cols[:, 2:4].unsqueeze(1).to_broadcast([P, 2, HALVES]), ALU.mult))
                nc.vector.tensor_tensor(k.scatter_idx[:, bass.ds(2 * s, 2), :], pair,
                                        empty[:, :].rearrange("p (e h) -> p e h", e=2), ALU.add).then_inc(indices_ready, 1)

            find_tile(0, 0)
            ch.restart()
            with dve.Fori(0, STEPS // 2 - 1) as i:
                for par in range(2):
                    s = 2 * i + par
                    find_tile(s + 1, 1 - par)
                    find_token(s, par)
                ch.restart()
            find_tile(STEPS - 1, 1)
            find_token(STEPS - 2, 0)
            find_token(STEPS - 1, 1)
            ch.restart()


def stage_f(nc, d, k, out):
    with Stage(nc, "f") as st:
        w_loaded = st.sems("w_loaded0 w_loaded1")
        gathered = st.sems("gathered0 gathered1")
        added = st.sems("added0 added1")
        gi_ready, si_ready = st.sems("gi_ready si_ready")
        stages = st.sems("turned xT_ready up_mm gate_ready hidden_ready down_mm weights_ready scaled")
        turned, xT_ready, up_mm, gate_ready, hidden_ready, down_mm, weights_ready, scaled = stages
        w = [st.sb(f"w{i}", [P, 3 * D]) for i in range(2)]
        x = [st.sb(f"x{i}", [P, HALVES, XW]) for i in range(2)]
        gi = [st.sb(f"gi{i}", [P, HALVES], I32) for i in range(2)]
        si = [st.sb(f"si{i}", [P, HALVES], I32) for i in range(2)]
        xT = [st.sb(f"xT{i}", [P, DH, CAP]) for i in range(2)]
        gate = [st.sb(f"gate{i}", [P, CAP]) for i in range(2)]
        hidden = [st.sb(f"hidden{i}", [P, CAP]) for i in range(2)]
        wcol = [st.sb(f"wcol{i}", [P, HALVES]) for i in range(2)]
        y = [st.sb(f"y{i}", [P, HALVES, D]) for i in range(2)]
        x_ps, up_ps, down_ps = ([st.bank(f"{n}{i}") for i in range(2)] for n in ("x", "up", "down"))
        block = st.block()

        @block.sync
        def _(sp):
            for s in stages:
                sp.sem_inc(s, CREDIT)
            with sp.Fori(0, E // 2) as i:
                for par in range(2):
                    finished(sp, down_mm, 2 * i + (par - 2))
                    sp.dma_start(w[par][:, :], d["experts"][bass.ds(2 * i + par, 1), :, :].rearrange("a p n -> p (a n)")
                                 ).then_inc(w_loaded[par], 16)

        @block.gpsimd
        def _(pool):
            def gather(s, par):
                pool_finished(pool, k, weights_ready, s - 2)
                pool_finished(pool, k, turned, s - 2)
                nc.gpsimd.tensor_copy(gi[par][:, :], k.gather_idx[:, bass.ds(s, 1), :].rearrange("p a h -> p (a h)")
                                      ).then_inc(gi_ready, 1)
                pool.wait_ge(gi_ready, s + 1)
                pool.sem_inc(k.pool_waited, 1)
                for hf in range(HALVES):
                    nc.gpsimd.indirect_dma_start(x[par][:, hf, :], None, k.token_rows[:, :],
                                                 bass.IndirectOffsetOnAxis(ap=gi[par][:, hf:hf + 1], axis=0),
                                                 bounds_check=T - 1).then_inc(gathered[par], 16)

            def add(s, par, before, own):
                nc.gpsimd.tensor_copy(si[par][:, :], k.scatter_idx[:, bass.ds(s, 1), :].rearrange("p a h -> p (a h)")
                                      ).then_inc(si_ready, 1)
                pool.wait_ge(si_ready, s + 1)
                pool.sem_inc(k.pool_waited, 1)
                pool_finished(pool, k, scaled, s)
                pool.wait_ge(added[1 - par], before)
                pool.sem_inc(k.pool_waited, 1)
                for hf in range(HALVES):
                    nc.gpsimd.indirect_dma_start(out[:, :], bass.IndirectOffsetOnAxis(ap=si[par][:, hf:hf + 1], axis=0),
                                                 y[par][:, hf, :], None, bounds_check=T + CAP - 1, compute_op=ALU.add
                                                 ).then_inc(added[par], 16)

            gather(0, 0)
            gather(1, 1)
            with pool.Fori(0, E // 2 - 1) as i:
                add(2 * i, 0, 32 * i, 32 * i)
                gather(2 * i + 2, 0)
                add(2 * i + 1, 1, 32 * i + 32, 32 * i)
                gather(2 * i + 3, 1)
            n = E // 2 - 1
            add(E - 2, 0, 32 * n, 32 * n)
            add(E - 1, 1, 32 * n + 32, 32 * n)
            pool.wait_ge(added[0], 32 * (n + 1))
            pool.wait_ge(added[1], 32 * (n + 1))

        @block.tensor
        def _(pe):
            def turn(s, par, i):
                pe.wait_ge(gathered[par], i * 32 + 32)
                finished(pe, xT_ready, s - 2)
                for hf in range(HALVES):
                    for c in range(DH):
                        mm = nc.tensor.transpose(x_ps[par][:, c * CAP + hf * P:c * CAP + (hf + 1) * P],
                                                 x[par][:, hf, c * P:(c + 1) * P], k.ident)
                mm.then_inc(turned, 1)

            def expand(s, par, i):
                finished(pe, xT_ready, s)
                finished(pe, hidden_ready, s - 2)
                pe.wait_ge(w_loaded[par], i * 16 + 16)
                for m in range(2):
                    for c in range(DH):
                        mm = nc.tensor.matmul(up_ps[par][:, m * CAP:(m + 1) * CAP],
                                              w[par][:, m * D + c * FF:m * D + (c + 1) * FF], xT[par][:, c, :],
                                              start=c == 0, stop=c == DH - 1)
                mm.then_inc(up_mm, 1)

            def contract(s, par):
                finished(pe, hidden_ready, s)
                finished(pe, scaled, s - 2)
                for hf in range(HALVES):
                    mm = nc.tensor.matmul(down_ps[par][:, hf * D:(hf + 1) * D], hidden[par][:, hf * P:(hf + 1) * P],
                                          w[par][:, 2 * D:3 * D], start=True, stop=True)
                mm.then_inc(down_mm, 1)

            turn(0, 0, 0)
            expand(0, 0, 0)
            with pe.Fori(0, E // 2 - 1) as i:
                turn(2 * i + 1, 1, i)
                contract(2 * i, 0)
                expand(2 * i + 1, 1, i)
                turn(2 * i + 2, 0, i + 1)
                contract(2 * i + 1, 1)
                expand(2 * i + 2, 0, i + 1)
            turn(E - 1, 1, E // 2 - 1)
            contract(E - 2, 0)
            expand(E - 1, 1, E // 2 - 1)
            contract(E - 1, 1)

        @block.scalar
        def _(act):
            def scale(s, par, i):
                finished(act, down_mm, s)
                finished(act, weights_ready, s)
                act.wait_ge(added[par], i * 32)
                for hf in range(HALVES):
                    ins = nc.scalar.activation(y[par][:, hf, :], down_ps[par][:, hf * D:(hf + 1) * D], ACT.Copy,
                                               scale=wcol[par][:, hf:hf + 1])
                ins.then_inc(scaled, 1)

            with act.Fori(0, E // 2) as i:
                for par in range(2):
                    s = 2 * i + par
                    finished(act, turned, s)
                    finished(act, up_mm, s - 2)
                    nc.scalar.activation(xT[par][:, :, :].rearrange("p c n -> p (c n)"), x_ps[par][:, :], ACT.Copy
                                         ).then_inc(xT_ready, 1)
                    finished(act, up_mm, s)
                    finished(act, hidden_ready, s - 2)
                    nc.scalar.activation(gate[par][:, :], up_ps[par][:, 0:CAP], ACT.Sigmoid).then_inc(gate_ready, 1)
                    scale(s, par, i)

        @block.vector
        def _(dve):
            ch = Chain(dve, k.dve_chain)
            with dve.Fori(0, E // 2) as i:
                for par in range(2):
                    s = 2 * i + par
                    dve.wait_ge(gathered[par], i * 32 + 32)
                    finished(dve, scaled, s - 2)
                    nc.vector.tensor_copy(wcol[par][:, :], x[par][:, :, bass.ds(2 * i + (D + par), 1)]
                                          .rearrange("p h a -> p (h a)")).then_inc(weights_ready, 1)
                    finished(dve, gate_ready, s)
                    finished(dve, down_mm, s - 2)
                    ch.link(nc.vector.tensor_tensor(gate[par][:, :], up_ps[par][:, 0:CAP], gate[par][:, :], ALU.mult))
                    nc.vector.tensor_tensor(hidden[par][:, :], up_ps[par][:, CAP:2 * CAP], gate[par][:, :], ALU.mult
                                            ).then_inc(hidden_ready, 1)
                ch.restart()


_IN = [("x", [P, TILES], I32), ("codes_T", [D, CODES], F32), ("tok_W1", [D, HID], F32), ("tok_b1", [P, HC], F32),
       ("tok_W2", [HID, D], F32), ("tok_b2", [1, D], F32), ("alpha_raw", [1, 1], F32),
       ("pw_T", [2, D, D], F32), ("gate_wT", [D, D], F32), ("dw", [P, 2 * DH * TAPS], F32),
       ("q_T", [D, NH * HD], F32), ("k_T", [D, NKV * 2 * HD], F32), ("v_T", [D, NKV * HD], F32), ("o_T", [NH * HD, D], F32),
       ("route_T", [D, E], F32), ("e_bias", [1, E], F32), ("shared_T", [D, 2 * D], F32), ("down_T", [D, D], F32),
       ("experts", [E, P, 3 * D], F32)]


def kernel(x, L0_tok_codebook, L0_tok_W1, L0_tok_b1, L0_tok_W2, L0_tok_b2, L0_attn_q_w, L0_attn_k_w, L0_attn_v_w,
           L0_attn_o_w, L0_attn_dw_r, L0_attn_pw_r, L0_attn_dw_i, L0_attn_pw_i, L0_attn_gate_w, L0_attn_alpha_raw,
           L0_ffn_gate_weight, L0_ffn_e_bias, L0_ffn_w1, L0_ffn_w2, L0_ffn_w3, L0_ffn_shared_gate, L0_ffn_shared_up,
           L0_ffn_shared_down):
    import numpy as _np
    import concourse.bacc as _bacc
    from concourse.bass_utils import run_bass_kernel_spmd as _run

    def c(a):
        return _np.ascontiguousarray(a)

    def a_(a):
        return _np.asarray(a)

    f32, high, f16 = shape_constants()
    dw = _np.stack([a_(L0_attn_dw_r)[:, 0], a_(L0_attn_dw_i)[:, 0]]).reshape(2, DH, P, TAPS).transpose(2, 0, 1, 3)
    k_T = a_(L0_attn_k_w).reshape(NKV, 1, HD, D).repeat(2, 1).reshape(NKV * 2 * HD, D).T
    w1, w3 = (a_(w).transpose(0, 2, 1).reshape(E, DH, P, FF).transpose(0, 2, 1, 3).reshape(E, P, DH * FF)
              for w in (L0_ffn_w1, L0_ffn_w3))
    w2 = a_(L0_ffn_w2).transpose(0, 2, 1)
    arrays = {
        "x": c(a_(x).reshape(TILES, P).T), "codes_T": c(a_(L0_tok_codebook).T), "tok_W1": c(L0_tok_W1),
        "tok_b1": c(a_(L0_tok_b1).reshape(HC, P).T), "tok_W2": c(L0_tok_W2), "tok_b2": c(a_(L0_tok_b2).reshape(1, D)),
        "alpha_raw": c(a_(L0_attn_alpha_raw).reshape(1, 1)),
        "pw_T": c(_np.stack([a_(L0_attn_pw_r).T, a_(L0_attn_pw_i).T])), "gate_wT": c(a_(L0_attn_gate_w).T),
        "dw": c(dw.reshape(P, -1)), "q_T": c(a_(L0_attn_q_w).T), "k_T": c(k_T), "v_T": c(a_(L0_attn_v_w).T),
        "o_T": c(a_(L0_attn_o_w).T), "route_T": c(a_(L0_ffn_gate_weight).T), "e_bias": c(a_(L0_ffn_e_bias).reshape(1, E)),
        "shared_T": c(_np.concatenate([a_(L0_ffn_shared_gate), a_(L0_ffn_shared_up)]).T),
        "down_T": c(a_(L0_ffn_shared_down).T), "experts": c(_np.concatenate([w1, w3, w2], 2)),
        "c_f32": f32, "c_high": high, "c_f16": f16,
    }
    nc = _bacc.Bacc("TRN2", target_bir_lowering=False, num_devices=1)
    d = {}
    for name, shape, dt in _IN:
        assert list(arrays[name].shape) == shape, (name, arrays[name].shape)
        d[name] = nc.dram_tensor(f"in_{name}", shape, dt, kind="ExternalInput").ap()
    for name in ("c_f32", "c_high", "c_f16"):
        a = arrays[name]
        d[name] = nc.dram_tensor(f"in_{name}", a.shape, mybir.dt.from_np(a.dtype), kind="ExternalInput").ap()
    out = nc.dram_tensor("out_rows", [T + CAP, D], F32, kind="ExternalOutput")
    build(nc, d, out, {n: arrays[n].shape[1] for n in ("c_f32", "c_f16")})
    r = _run(nc, [{f"in_{n}": a for n, a in arrays.items()}], core_ids=[0])
    return r.results[0]["out_rows"][:T].reshape(B, N, D)
```

```python
from contextlib import ExitStack

import numpy as np

import concourse.bass as bass
from concourse import mybir

F32 = mybir.dt.float32
F16 = mybir.dt.float16
I32 = mybir.dt.int32
ALU = mybir.AluOpType
ACT = mybir.ActivationFunctionType
AX = mybir.AxisListType.X

P = 128
B, N, D = 32, 256, 256
T = B * N
TILES = T // P
DH = D // P
CODES, HID = 2048, 1024
HC = HID // P
CHUNK = 64
BINS = CHUNK // 2 + 1
LOW = 4
HIGH = BINS - LOW
TAPS = 7
PAD = TAPS - 1
LOWC = 2 * 2 * LOW
SPEC = LOWC + 2 * 2 * HIGH
NH, NKV, HD = 16, 4, 64
GROUPS = TILES // 8
E, TOPK, NG, TG, FF, CAP = 64, 8, 8, 4, 128, 256
HALVES = CAP // P
XW = D + E
SCALE = 2.5
NEG = -1.0e30
COUNT_MAX = 512.0
TRASH = T
CREDIT = 2


def finished(eng, sem, step):
    eng.wait_ge(sem, step + (1 + CREDIT))


def pool_finished(pool, k, sem, step):
    finished(pool, sem, step)
    pool.sem_inc(k.pool_waited, 1)


class Kept:
    pass


class Chain:

    def __init__(self, eng, sem):
        self.eng, self.sem, self.n = eng, sem, 0

    def mark(self, ins):
        ins.then_inc(self.sem, 1)
        self.n += 1
        return self.n

    def reach(self, n):
        self.eng.wait_ge(self.sem, n)

    def link(self, ins):
        self.reach(self.mark(ins))

    def restart(self):
        self.reach(self.n)
        self.eng.sem_clear(self.sem)
        self.n = 0


def shape_constants():
    t = np.arange(CHUNK)[:, None]
    k = np.arange(BINS)[None, :]
    ang = 2 * np.pi * ((t * k) % CHUNK) / CHUNK
    re, im = np.cos(ang), -np.sin(ang)
    im[:, 0] = 0
    im[:, BINS - 1] = 0
    dft = np.zeros((P, SPEC))
    for c in range(2):
        rows = slice(c * CHUNK, (c + 1) * CHUNK)
        for r, m in enumerate((re, im)):
            dft[rows, (c * 2 + r) * LOW:(c * 2 + r + 1) * LOW] = m[:, :LOW]
            at = LOWC + (r * 2 + c) * HIGH
            dft[rows, at:at + HIGH] = m[:, LOW:]
    weight = np.full(BINS, 2.0 / CHUNK)
    weight[0] = weight[-1] = 1.0 / CHUNK
    inv = [(re * weight).T, (im * weight).T]
    rows = 4 * HIGH
    idft_high = np.zeros((rows, 2, 2, P))
    for r in range(2):
        for tile in range(2):
            for c in range(2):
                at = (tile * 2 + c) * HIGH
                idft_high[at:at + HIGH, r, tile, c * CHUNK:(c + 1) * CHUNK] = 0.5 * inv[r][LOW:]
    idft_low = np.zeros((P, 8, P))
    for tile in range(8):
        for c in range(2):
            for r in range(2):
                at = tile * LOWC + (c * 2 + r) * LOW
                idft_low[at:at + LOW, tile, c * CHUNK:(c + 1) * CHUNK] = inv[r][:LOW]
    row = np.arange(P)
    batch, chunk, ri = row // (2 * LOWC), row // (2 * LOW) % 4, row // LOW % 2
    ok = (batch[:, None] == batch) & (ri[:, None] == ri) & (chunk[:, None] >= chunk)
    mask = np.where(ok, 0.0, NEG)
    eye = np.eye(P)
    tri = np.triu(np.ones((P, P)))
    before = (np.arange(NG)[None, :] < np.arange(NG)[:, None]).astype(float)
    tie = np.broadcast_to(np.stack([before, 1 - before]).reshape(1, 2 * NG * NG), (P, 2 * NG * NG))
    slot = np.broadcast_to(np.arange(CAP), (P, CAP))
    cols = np.zeros((P, 8))
    cols[:, 0], cols[:, 1] = row, row + P
    cols[:, 2], cols[:, 3] = TRASH - P + row, TRASH + row
    cols[:, 4] = -0.5
    cols[:, 5] = row % TILES != 0
    f32 = np.concatenate([dft, idft_low.reshape(P, -1), mask, eye, tie, cols], 1).astype(np.float32)
    f16 = np.concatenate([slot, eye, (row % TILES)[:, None], np.zeros((P, 1)), tri, np.ones((P, P))], 1).astype(np.float16)
    return f32, idft_high.reshape(rows, -1).astype(np.float32), f16


def build(nc, d, out, sizes):
    ctx = ExitStack()
    with ctx:
        def sb(name, shape, dt=F32):
            return ctx.enter_context(nc.sbuf_tensor(name, shape, dt))

        def sem(name):
            return ctx.enter_context(nc.semaphore(name))

        k = Kept()
        k.dve_chain, k.act_chain, k.pool_chain = sem("dve_chain"), sem("act_chain"), sem("pool_chain")
        k.table = nc.dram_tensor("code_table", [CODES, 2 * D], F32)
        k.token_rows = nc.dram_tensor("token_rows", [T, XW], F32)
        k.z = sb("z", [P, TILES * D])
        k.const = sb("const", [P, sizes["c_f32"]])
        k.idft_high = sb("idft_high", [4 * HIGH, 2, 2, P])
        k.c16 = sb("c16", [P, sizes["c_f16"]], F16)
        at = [0]

        def part(n):
            at[0] += n
            return k.const[:, at[0] - n:at[0]]

        k.dft = part(SPEC)
        k.idft_low = part(8 * P).rearrange("p (v t) -> p v t", v=8)
        k.mask = part(P)
        k.ident = part(P)
        k.tie = part(2 * NG * NG).rearrange("p (a g h) -> p a g h", a=2, g=NG)
        k.cols = part(8)
        k.slot_row, k.ident16, k.tile_col = k.c16[:, 0:CAP], k.c16[:, CAP:CAP + P], k.c16[:, CAP + P:CAP + P + 1]
        k.tri, k.ones = (k.c16[:, CAP + P + 2 + i * P:CAP + P + 2 + (i + 1) * P] for i in range(2))
        k.idx = sb("idx", [P, TILES], I32)
        k.alpha_raw = sb("alpha_raw", [P, 1])
        k.alpha = sb("alpha", [P, 1])
        k.low_T = sb("low_T", [P, DH, TILES * LOWC])
        k.att = sb("att", [P, GROUPS * D])
        k.counts = sb("counts", [P, 1 + E * TILES], F16)
        k.gather_idx = sb("gather_idx", [P, E, HALVES], I32)
        k.scatter_idx = sb("scatter_idx", [P, E, HALVES], I32)
        k.zeros = sb("zeros", [P, HALVES * D])[:, :]
        k.trash_zeroed, k.trash_stored, k.pool_waited = sem("trash_zeroed"), sem("trash_stored"), sem("pool_waited")
        stage_a(nc, d, k)
        stage_b(nc, d, k)
        stage_c(nc, d, k)
        stage_d(nc, d, k, out)
        stage_e(nc, d, k, out)


class Stage:

    def __init__(self, nc, tag):
        self.nc, self.tag, self.ctx = nc, tag, ExitStack()

    def __enter__(self):
        return self

    def __exit__(self, *a):
        return self.ctx.__exit__(*a)

    def sb(self, name, shape, dt=F32):
        return self.ctx.enter_context(self.nc.sbuf_tensor(f"{self.tag}_{name}", shape, dt))

    def bank(self, name, dt=F32):
        return self.ctx.enter_context(self.nc.psum_tensor(f"{self.tag}_ps_{name}", [P, 512], dt))

    def banks(self, name, n):
        return self.ctx.enter_context(self.nc.psum_tensor(f"{self.tag}_ps_{name}", [P, n, 512], F32))

    def sems(self, names):
        return [self.ctx.enter_context(self.nc.semaphore(f"{self.tag}_{n}")) for n in names.split()]

    def block(self):
        return self.ctx.enter_context(self.nc.Block())


def stage_a(nc, d, k):
    with Stage(nc, "a") as st:
        w_loaded, c_loaded = st.sems("w_loaded c_loaded")
        codes_loaded = st.sems("codes0 codes1 codes2 codes3")
        row_stored = st.sems("row_stored0 row_stored1")
        stages = st.sems("up_done gelu_done down_done row_read var_ready rstd_ready row_ready")
        up_done, gelu_done, down_done, row_read, var_ready, rstd_ready, row_ready = stages
        up = [st.bank(f"up{i}") for i in range(2)]
        down = [st.bank(f"down{i}") for i in range(2)]
        used = [0]

        def zpart(n):
            used[0] += n
            return k.z[:, used[0] - n:used[0]]

        codes_T = zpart(DH * CODES).rearrange("p (c n) -> p c n", c=DH)
        w1 = zpart(DH * HID).rearrange("p (c n) -> p c n", c=DH)
        w2 = zpart(HC * D).rearrange("p (c n) -> p c n", c=HC)
        hid = zpart(HC * 512).rearrange("p (c n) -> p c n", c=HC)
        b1, b2 = zpart(HC), zpart(D)
        rows = [zpart(2 * D) for _ in range(2)]
        stats = zpart(6)
        mv, veps, rstd = ([zpart(n) for _ in range(2)] for n in (2, 1, 1))
        block = st.block()

        @block.sync
        def _(sp):
            for s in stages:
                sp.sem_inc(s, CREDIT)
            sp.dma_start(w1, d["tok_W1"].rearrange("(c p) n -> p c n", p=P)).then_inc(w_loaded, 16)
            sp.dma_start(b1, d["tok_b1"]).then_inc(w_loaded, 16)
            codes = d["codes_T"].rearrange("(c p) n -> p c n", p=P)
            for g in range(4):
                sp.dma_start(codes_T[:, :, g * 512:(g + 1) * 512], codes[:, :, g * 512:(g + 1) * 512]
                             ).then_inc(codes_loaded[g], 16)
            sp.dma_start(w2, d["tok_W2"].rearrange("(c p) n -> p c n", p=P)).then_inc(w_loaded, 16)
            sp.dma_start(b2, d["tok_b2"].partition_broadcast(P)).then_inc(w_loaded, 16)
            sp.dma_start(k.const[:, :], d["c_f32"]).then_inc(c_loaded, 16)
            sp.dma_start(k.idft_high[:, :, :, :], d["c_high"].rearrange("p (a b c) -> p a b c", a=2, b=2)
                         ).then_inc(c_loaded, 16)
            sp.dma_start(k.c16[:, :], d["c_f16"]).then_inc(c_loaded, 16)
            sp.dma_start(k.idx[:, :], d["x"]).then_inc(c_loaded, 16)
            sp.dma_start(k.alpha_raw[:, :], d["alpha_raw"].partition_broadcast(P)).then_inc(c_loaded, 16)
            for s in row_stored:
                sp.sem_inc(s, 16)
            with sp.Fori(0, 4) as g:
                for r in range(4):
                    finished(sp, row_ready, g * 4 + r)
                    sp.dma_start(k.table[bass.ds(g * 512 + r * P, P), :], rows[r % 2]).then_inc(row_stored[r % 2], 16)
            for s in row_stored:
                sp.wait_ge(s, 16 * (CODES // P // 2 + 1))

        @block.tensor
        def _(pe):
            pe.wait_ge(w_loaded, 16 * 4)
            for g in range(4):
                pe.wait_ge(codes_loaded[g], 16)
            with pe.Fori(0, 4) as g:
                for h in range(HC):
                    finished(pe, gelu_done, g * HC + (h - 2))
                    for c in range(DH):
                        mm = nc.tensor.matmul(up[h % 2][:, :], w1[:, c, h * P:(h + 1) * P],
                                              codes_T[:, c, bass.ds(g * 512, 512)], start=c == 0, stop=c == DH - 1)
                    mm.then_inc(up_done, 1)
                for r in range(4):
                    if r == 0:
                        finished(pe, gelu_done, g * HC + (HC - 1))
                    finished(pe, row_read, g * 4 + (r - 2))
                    for h in range(HC):
                        mm = nc.tensor.matmul(down[r % 2][:, 0:D], hid[:, h, r * P:(r + 1) * P], w2[:, h, :],
                                              start=h == 0, stop=h == HC - 1)
                    mm.then_inc(down_done, 1)

        @block.scalar
        def _(act):
            act.wait_ge(w_loaded, 16 * 4)
            with act.Fori(0, 4) as g:
                for h in range(HC):
                    finished(act, up_done, g * HC + h)
                    if h == 0:
                        finished(act, down_done, g * 4 - 1)
                    nc.scalar.activation(hid[:, h, :], up[h % 2][:, :], ACT.Gelu_apprx_tanh,
                                         bias=b1[:, h:h + 1]).then_inc(gelu_done, 1)
            act.wait_ge(c_loaded, 16 * 5)
            nc.scalar.activation(k.alpha[:, 0:1], k.alpha_raw[:, :], ACT.Sigmoid)

        @block.gpsimd
        def _(pool):
            pool.wait_ge(c_loaded, 16 * 5)
            with pool.Fori(0, 8) as i:
                for par in range(2):
                    pool_finished(pool, k, var_ready, 2 * i + par)
                    nc.gpsimd.tensor_tensor(rstd[par], veps[par], k.cols[:, 4:5], ALU.pow).then_inc(rstd_ready, 1)

        @block.vector
        def _(dve):
            ch = Chain(dve, k.dve_chain)
            dve.wait_ge(w_loaded, 16 * 4)
            with dve.Fori(0, 4) as g:
                for r in range(4):
                    m, row = g * 4 + r, rows[r % 2]
                    finished(dve, down_done, m)
                    dve.wait_ge(row_stored[r % 2], g * 32 + 16 * (r // 2 + 1))
                    nc.vector.tensor_tensor(row[:, D:2 * D], down[r % 2][:, 0:D], b2, ALU.add).then_inc(row_read, 1)
                    finished(dve, row_read, m)
                    ch.link(nc.vector.bn_stats(stats, row[:, D:2 * D]))
                    ch.link(nc.vector.bn_aggr(mv[r % 2], stats))
                    nc.vector.tensor_scalar(veps[r % 2], mv[r % 2][:, 1:2], 1e-5, None, ALU.add).then_inc(var_ready, 1)
                    finished(dve, rstd_ready, m)
                    ch.link(nc.vector.tensor_scalar(row[:, 0:D], row[:, D:2 * D], mv[r % 2][:, 0:1], rstd[r % 2],
                                                    ALU.subtract, ALU.mult))
                    nc.vector.tensor_tensor(row[:, D:2 * D], row[:, 0:D], row[:, D:2 * D], ALU.add).then_inc(row_ready, 1)
                ch.restart()


def stage_b(nc, d, k):
    with Stage(nc, "b") as st:
        w_loaded, pads_zeroed = st.sems("w_loaded pads_zeroed")
        rows_gathered = st.sems("rows_gathered0 rows_gathered1 rows_gathered2 rows_gathered3")
        idx_ready = st.sems("idx_ready")[0]
        stages = st.sems("dft_done gate_mm gate_turned mixed back_mm low_copied high_copied first_tap gate_ready gate_copied "
                         "gelu_done mixed_copied conv_done summed z_done kept")
        (dft_done, gate_mm, gate_turned, mixed, back_mm, low_copied, high_copied, first_tap, gate_ready, gate_copied,
         gelu_done, mixed_copied, conv_done, summed, z_done, kept) = stages
        pw = st.sb("pw", [P, 2, DH, D])
        gate_w = st.sb("gate_w", [P, DH, D])
        dw = st.sb("dw", [P, 2, DH, TAPS])
        rows = [st.sb(f"rows{i}", [P, 2, 2 * D]) for i in range(4)]
        tile_idx = [st.sb(f"tile_idx{i}", [P, 2], I32) for i in range(4)]
        high = [st.sb(f"high{i}", [P, DH, 2, 2, 4, PAD + HIGH]) for i in range(2)]
        conv = [st.sb(f"conv{i}", [P, DH, 2, 8, HIGH]) for i in range(2)]
        act_in = [st.sb(f"gelu{i}", [P, DH, 2, 2, 4 * HIGH]) for i in range(2)]
        mix = [st.sb(f"mix{i}", [4 * HIGH, 2, D]) for i in range(2)]
        spread = [st.sb(f"spread{i}", [P, DH * 4, CHUNK]) for i in range(2)]
        gate = [st.sb(f"gate{i}", [P, 2 * D]) for i in range(4)]
        total = [st.sb(f"total{i}", [P, 2 * D]) for i in range(2)]
        spec_ps = st.banks("spec", 2)
        gate_ps, turn_ps = st.bank("gate"), st.bank("turn")
        mix_ps, back_ps = st.banks("mix", 2), st.banks("back", 2)
        block = st.block()
        BATCHES, PAIRS = B, B // 2

        @block.sync
        def _(sp):
            for s in stages:
                sp.sem_inc(s, CREDIT)
            sp.dma_start(pw[:, :, :, :], d["pw_T"].rearrange("r (c p) n -> p r c n", p=P)).then_inc(w_loaded, 16)
            sp.dma_start(gate_w[:, :, :], d["gate_wT"].rearrange("(c p) n -> p c n", p=P)).then_inc(w_loaded, 16)
            sp.dma_start(dw[:, :, :, :], d["dw"].rearrange("p (r c t) -> p r c t", r=2, c=DH)).then_inc(w_loaded, 16)

        @block.gpsimd
        def _(pool):
            def gather(s, slot):
                nc.gpsimd.tensor_copy(tile_idx[slot][:, :], k.idx[:, bass.ds(s * 2, 2)]).then_inc(idx_ready, 1)
                pool.wait_ge(idx_ready, s + 1)
                pool.sem_inc(k.pool_waited, 1)
                for t in range(2):
                    nc.gpsimd.indirect_dma_start(rows[slot][:, t, :], None, k.table[:, :],
                                                 bass.IndirectOffsetOnAxis(ap=tile_idx[slot][:, t:t + 1], axis=0),
                                                 bounds_check=CODES - 1).then_inc(rows_gathered[slot], 16)

            def keep(s, slot, rounds):
                pool.wait_ge(rows_gathered[slot], rounds)
                pool.sem_inc(k.pool_waited, 1)
                nc.gpsimd.tensor_copy(k.z[:, bass.ds(s * 2 * D, 2 * D)].rearrange("p (t n) -> p t n", t=2),
                                      rows[slot][:, :, D:2 * D]).then_inc(kept, 1)
                pool_finished(pool, k, kept, s)
                pool_finished(pool, k, dft_done, s)

            def z_add(s, slot):
                pool_finished(pool, k, summed, s)
                nc.gpsimd.tensor_tensor(k.z[:, bass.ds(s * 2 * D, 2 * D)], k.z[:, bass.ds(s * 2 * D, 2 * D)],
                                        total[slot % 2][:, :], ALU.add).then_inc(z_done, 1)

            def step(i, c, more=True):
                s = 4 * i + c
                slot = (c + 2) % 4
                if more or c + 2 < 8:
                    keep(s + 2, slot, i * 32 + 32 * ((c + 2) // 4 + 1))
                if more or c + 6 < 8:
                    gather(s + 6, slot)
                z_add(s, c % 4)

            for c in range(4):
                gather(c, c)
            for c in range(2):
                keep(c, c, 32)
                gather(c + 4, c)
            rounds = BATCHES // 4 - 2
            with pool.Fori(0, rounds) as i:
                for c in range(4):
                    step(i, c)
            for c in range(8):
                step(rounds, c, more=False)

        @block.tensor
        def _(pe):
            def spectrum(i, c):
                s, slot = 4 * i + c, c % 4
                pe.wait_ge(rows_gathered[slot], i * 32 + 32 * (c // 4 + 1))
                finished(pe, high_copied, s - 1)
                for c in range(DH):
                    for t in range(2):
                        x = rows[slot][:, t, c * P:(c + 1) * P]
                        nc.tensor.matmul(spec_ps[:, c, t * LOWC:(t + 1) * LOWC], x, k.dft[:, 0:LOWC], start=True, stop=True)
                        to = spec_ps[:, c, 2 * LOWC:2 * SPEC].rearrange("p (r t n) -> p r t n", r=2, t=2)[:, :, t, :]
                        mm = nc.tensor.matmul(to, x, k.dft[:, LOWC:SPEC].rearrange("p (r n) -> p r n", r=2),
                                              start=True, stop=True)
                mm.then_inc(dft_done, 1)

            def gate_up(s):
                finished(pe, low_copied, s)
                finished(pe, gate_ready, s - 1)
                for o in range(DH):
                    for c in range(DH):
                        mean = k.low_T[:, c, bass.ds(s * 2 * LOWC, 2 * LOWC)].rearrange("p (q n) -> p q n", n=2 * LOW)[:, :, 0]
                        mm = nc.tensor.matmul(gate_ps[:, o * 4:(o + 1) * 4], gate_w[:, c, o * P:(o + 1) * P], mean,
                                              start=c == 0, stop=c == DH - 1)
                mm.then_inc(gate_mm, 1)

            def gate_turn(s, par):
                finished(pe, gate_ready, s)
                finished(pe, gate_copied, s - 1)
                for t in range(2):
                    for o in range(DH):
                        q = (o * 2 + t) * 2
                        mm = nc.tensor.transpose(turn_ps[:, t * D + o * P:t * D + (o + 1) * P],
                                                 spread[par][:, q:q + 2, :].rearrange("p a n -> p (a n)"), k.ident)
                mm.then_inc(gate_turned, 1)

            def mixing(s, u, pair, pair_par):
                if u == 0:
                    finished(pe, gelu_done, pair)
                finished(pe, mixed_copied, s - 2)
                for r in range(2):
                    for c in range(DH):
                        mm = nc.tensor.matmul(mix_ps[0:4 * HIGH, u, r * D:(r + 1) * D], act_in[pair_par][:, c, r, u, :],
                                              pw[:, r, c, :], start=c == 0, stop=c == DH - 1)
                mm.then_inc(mixed, 1)

            def inverse(s, u):
                finished(pe, mixed_copied, s)
                finished(pe, summed, s - 2)
                for t in range(2):
                    for r in range(2):
                        mm = nc.tensor.matmul(back_ps[:, u, t * D:(t + 1) * D], k.idft_high[:, r, t, :], mix[u][:, r, :],
                                              start=r == 0, stop=r == 1)
                mm.then_inc(back_mm, 1)

            def body(i, j, last=PAIRS):
                pair, s = 2 * i + j, 4 * i + 2 * j
                if last > 2:
                    spectrum(i, 2 * j + 4)
                mixing(s, 0, pair, j % 2)
                if last > 1:
                    gate_up(s + 2)
                if last > 2:
                    spectrum(i, 2 * j + 5)
                mixing(s + 1, 1, pair, j % 2)
                if last > 1:
                    gate_turn(s + 2, 0)
                inverse(s, 0)
                if last > 1:
                    gate_up(s + 3)
                inverse(s + 1, 1)
                if last > 1:
                    gate_turn(s + 3, 1)

            pe.wait_ge(w_loaded, 16 * 3)
            for c in range(4):
                spectrum(0, c)
            for c in range(2):
                gate_up(c)
                gate_turn(c, c)
            rounds = PAIRS // 2 - 1
            with pe.Fori(0, rounds) as i:
                for j in range(2):
                    body(i, j)
            for j in range(2):
                body(rounds, j, last=2 - j)

        @block.scalar
        def _(act):
            def unpack(s, u, pair, pair_par):
                finished(act, dft_done, s)
                nc.scalar.activation(k.low_T[:, :, bass.ds(s * 2 * LOWC, 2 * LOWC)], spec_ps[:, :, 0:2 * LOWC],
                                     ACT.Copy).then_inc(low_copied, 1)
                finished(act, conv_done, pair - 2)
                for c in range(DH):
                    ins = nc.scalar.activation(high[pair_par][:, c, :, u, :, PAD:],
                                               spec_ps[:, c, 2 * LOWC:2 * SPEC].rearrange("p (r q l) -> p r q l", r=2, l=HIGH),
                                               ACT.Copy)
                ins.then_inc(high_copied, 1)

            def tap0(s, pair, pair_par):
                finished(act, high_copied, s)
                finished(act, gelu_done, pair - 2)
                for c in range(DH):
                    for r in range(2):
                        last = nc.scalar.activation(conv[pair_par][:, c, r, :, :],
                                                    high[pair_par][:, c, r, :, :, 0:HIGH].rearrange("p u q l -> p (u q) l"),
                                                    ACT.Copy, scale=dw[:, r, c, 0:1])
                last.then_inc(first_tap, 1)

            def gate_fn(s, u):
                finished(act, gate_mm, s)
                finished(act, gate_turned, s - 2)
                nc.scalar.activation(spread[u][:, :, :], gate_ps[:, 0:DH * 4].unsqueeze(2).to_broadcast([P, DH * 4, CHUNK]),
                                     ACT.Tanh, scale=0.5 / CHUNK).then_inc(gate_ready, 1)

            def gate_copy(s, slot, first=False):
                finished(act, gate_turned, s)
                if not first:
                    finished(act, summed, s - 4)
                nc.scalar.activation(gate[slot][:, :], turn_ps[:, :], ACT.Copy).then_inc(gate_copied, 1)

            def gelu(pair, pair_par, first=False):
                finished(act, conv_done, pair)
                if not first:
                    finished(act, mixed, pair * 2 - 3)
                nc.scalar.activation(act_in[pair_par][:, :, :, :, :].rearrange("p c r u n -> p (c r u n)"),
                                     conv[pair_par][:, :, :, :, :].rearrange("p c r q l -> p (c r q l)"), ACT.Gelu
                                     ).then_inc(gelu_done, 1)

            def mix_copy(s, u):
                finished(act, mixed, s)
                finished(act, back_mm, s - 2)
                nc.scalar.activation(mix[u][:, :, :].rearrange("p r n -> p (r n)"), mix_ps[0:4 * HIGH, u, :],
                                     ACT.Copy).then_inc(mixed_copied, 1)

            def body(i, j, last=PAIRS):
                pair, s, nxt = 2 * i + j, 4 * i + 2 * j, (2 * j + 2) % 4
                if last > 2:
                    unpack(s + 4, 0, pair + 2, j % 2)
                mix_copy(s, 0)
                if last > 2:
                    unpack(s + 5, 1, pair + 2, j % 2)
                if last > 1:
                    gate_fn(s + 2, 0)
                mix_copy(s + 1, 1)
                if last > 2:
                    tap0(s + 5, pair + 2, j % 2)
                if last > 1:
                    gate_copy(s + 2, nxt)
                    gate_fn(s + 3, 1)
                    gate_copy(s + 3, nxt + 1)
                    gelu(pair + 1, (j + 1) % 2)

            act.wait_ge(w_loaded, 16 * 3)
            act.wait_ge(pads_zeroed, 2)
            for pair in range(2):
                for u in range(2):
                    unpack(2 * pair + u, u, pair, pair)
                tap0(2 * pair + 1, pair, pair)
            for c in range(2):
                gate_fn(c, c)
                gate_copy(c, c, first=True)
            gelu(0, 0, first=True)
            rounds = PAIRS // 2 - 1
            with act.Fori(0, rounds) as i:
                for j in range(2):
                    body(i, j)
            for j in range(2):
                body(rounds, j, last=2 - j)

        @block.vector
        def _(dve):
            ch = Chain(dve, k.dve_chain)

            def convolve(pair, par):
                finished(dve, first_tap, pair)
                done = [0] * 4
                for tap in range(1, TAPS):
                    for g in range(4):
                        c, r = divmod(g, 2)
                        if tap > 1:
                            ch.reach(done[g])
                        acc = conv[par][:, c, r, :, :]
                        ins = nc.vector.scalar_tensor_tensor(
                            out=acc, in0=high[par][:, c, r, :, :, tap:tap + HIGH].rearrange("p u q l -> p (u q) l"),
                            scalar=dw[:, r, c, tap:tap + 1], in1=acc, op0=ALU.mult, op1=ALU.add)
                        if tap == TAPS - 1 and g == 3:
                            ins.then_inc(conv_done, 1)
                        else:
                            done[g] = ch.mark(ins)

            def sum_up(s, slot):
                finished(dve, back_mm, s)
                finished(dve, gate_copied, s)
                finished(dve, z_done, s - 2)
                nc.vector.scalar_tensor_tensor(out=total[slot % 2][:, :], in0=gate[slot][:, :], scalar=1.0,
                                               in1=back_ps[:, slot % 2, :], op0=ALU.add, op1=ALU.mult).then_inc(summed, 1)

            def body(i, j, last=PAIRS):
                pair, s = 2 * i + j, 4 * i + 2 * j
                if last > 1:
                    convolve(pair + 1, (j + 1) % 2)
                for u in range(2):
                    sum_up(s + u, (2 * j + u) % 4)

            for t in range(2):
                nc.vector.memset(high[t][:, :, :, :, :, 0:PAD].rearrange("p c r u q l -> p (c r u q) l"), 0.0
                                 ).then_inc(pads_zeroed, 1)
            dve.wait_ge(w_loaded, 16 * 3)
            convolve(0, 0)
            ch.restart()
            rounds = PAIRS // 2 - 1
            with dve.Fori(0, rounds) as i:
                for j in range(2):
                    body(i, j)
                ch.restart()
            for j in range(2):
                body(rounds, j, last=2 - j)
            ch.restart()


def stage_c(nc, d, k):
    with Stage(nc, "c") as st:
        w_loaded = st.sems("w_loaded")[0]
        stages = st.sems("rows_ready q_mm kv_mm q_copied kv_copied scores_mm biased max_ready exp_done normed turned "
                         "turned_act turned_dve values_mm values_act values_dve out_mm out_copied low_scaled")
        (rows_ready, q_mm, kv_mm, q_copied, kv_copied, scores_mm, biased, max_ready, exp_done, normed, turned,
         turned_act, turned_dve, values_mm, values_act, values_dve, out_mm, out_copied, low_scaled) = stages
        q_w = st.sb("q_w", [P, DH, NH * HD])
        k_w = st.sb("k_w", [P, DH, NKV * 2 * HD])
        v_w = st.sb("v_w", [P, DH, NKV * HD])
        o_w = st.sb("o_w", [P, NH // 2, D])
        rows = st.sb("rows", [P, DH, P])
        qT = st.sb("qT", [P, NH // 2, P])
        kT = st.sb("kT", [P, NKV, P])
        v = st.sb("v", [P, NKV * HD])
        prob = st.sb("prob", [P, 4, 4, P])
        probT = st.sb("probT", [P, 4, 4, P])
        top = st.sb("top", [P, 4, 4])
        shift = st.sb("shift", [P, 4, 4])
        rsum = st.sb("rsum", [P, 4, 4])
        rinv = st.sb("rinv", [P, 4, 4])
        vals = st.sb("vals", [P, NH // 2, P])
        low_rows = st.sb("low_rows", [P, D])
        psA, psB = st.banks("A", 4), st.banks("B", 4)
        block = st.block()
        INV = 1.0 / float(np.sqrt(HD))

        @block.sync
        def _(sp):
            for s in stages:
                sp.sem_inc(s, CREDIT)
            for w, name in ((q_w, "q_T"), (k_w, "k_T"), (v_w, "v_T"), (o_w, "o_T")):
                sp.dma_start(w[:, :, :], d[name].rearrange("(c p) n -> p c n", p=P)).then_inc(w_loaded, 16)

        @block.gpsimd
        def _(pool):
            with pool.Fori(0, GROUPS) as g:
                pool_finished(pool, k, kv_mm, g - 1)
                nc.gpsimd.tensor_copy(rows[:, :, :], k.low_T[:, :, bass.ds(g * P, P)]).then_inc(rows_ready, 1)

        @block.tensor
        def _(pe):
            pe.wait_ge(w_loaded, 16 * 4)
            with pe.Fori(0, GROUPS) as g:
                finished(pe, rows_ready, g)
                finished(pe, turned_act, g - 1)
                finished(pe, turned_dve, g - 1)
                for hp in range(NH // 2):
                    for c in range(DH):
                        mm = nc.tensor.matmul(psA[:, hp // 4, hp % 4 * P:(hp % 4 + 1) * P], q_w[:, c, hp * P:(hp + 1) * P],
                                              rows[:, c, :], start=c == 0, stop=c == DH - 1)
                mm.then_inc(q_mm, 1)
                for j in range(NKV):
                    for c in range(DH):
                        nc.tensor.matmul(psA[:, 2, j * P:(j + 1) * P], k_w[:, c, j * P:(j + 1) * P], rows[:, c, :],
                                         start=c == 0, stop=c == DH - 1)
                for c in range(DH):
                    nc.tensor.matmul(psA[:, 3, 0:NKV * HD], rows[:, c, :], v_w[:, c, :], start=c == 0, stop=c == DH - 1)
                for c in range(DH):
                    mm = nc.tensor.transpose(psA[:, 3, NKV * HD + c * P:NKV * HD + (c + 1) * P], rows[:, c, :], k.ident)
                mm.then_inc(kv_mm, 1)
                finished(pe, q_copied, g)
                finished(pe, kv_copied, g)
                finished(pe, values_act, g - 1)
                finished(pe, values_dve, g - 1)
                finished(pe, out_copied, g - 1)
                for n in range(4):
                    jj, parity = divmod(n, 2)
                    for i in range(4):
                        h = 8 * jj + parity + 2 * i
                        half = slice(parity * HD, (parity + 1) * HD)
                        mm = nc.tensor.matmul(psB[:, n, i * P:(i + 1) * P], qT[half, h // 2, :], kT[half, h // 4, :],
                                              start=True, stop=True)
                    mm.then_inc(scores_mm, 1)
                for n in range(4):
                    finished(pe, normed, g * 4 + n)
                    if n == 3:
                        finished(pe, low_scaled, g)
                    for i in range(4):
                        mm = nc.tensor.transpose(psA[:, n, i * P:(i + 1) * P], prob[:, n, i, :], k.ident)
                    mm.then_inc(turned, 1)
                finished(pe, turned_act, g)
                finished(pe, turned_dve, g)
                for jj in range(2):
                    for parity in range(2):
                        for half in range(2):
                            j = 2 * jj + half
                            mm = nc.tensor.matmul(psB[parity * HD:(parity + 1) * HD, jj, half * 2 * P:(half + 1) * 2 * P],
                                                  v[:, j * HD:(j + 1) * HD],
                                                  probT[:, 2 * jj + parity, 2 * half:2 * half + 2, :].rearrange("p i n -> p (i n)"),
                                                  start=True, stop=True)
                mm.then_inc(values_mm, 1)
                finished(pe, values_act, g)
                finished(pe, values_dve, g)
                for hp in range(NH // 2):
                    mm = nc.tensor.matmul(psB[:, 2, 0:D], vals[:, hp, :], o_w[:, hp, :], start=hp == 0, stop=hp == NH // 2 - 1)
                mm.then_inc(out_mm, 1)

        @block.scalar
        def _(act):
            with act.Fori(0, GROUPS) as g:
                finished(act, q_mm, g)
                nc.scalar.activation(qT[:, :, :].rearrange("p h n -> p (h n)"),
                                     psA[:, 0:2, :].rearrange("p a n -> p (a n)"), ACT.Copy).then_inc(q_copied, 1)
                finished(act, kv_copied, g)
                finished(act, out_copied, g - 1)
                nc.scalar.activation(low_rows[:, :], psA[:, 3, NKV * HD:], ACT.Copy, scale=k.alpha[:, 0:1]
                                     ).then_inc(low_scaled, 1)
                for n in range(4):
                    finished(act, max_ready, g * 4 + n)
                    for i in range(4):
                        ins = nc.scalar.activation(prob[:, n, i, :], prob[:, n, i, :], ACT.Exp, scale=INV,
                                                   bias=shift[:, n, i:i + 1], accum_out=rsum[:, n, i:i + 1])
                    ins.then_inc(exp_done, 1)
                for n in range(2):
                    finished(act, turned, g * 4 + n)
                finished(act, values_mm, g - 1)
                nc.scalar.activation(probT[:, 0:2, :, :].rearrange("p a i n -> p (a i n)"),
                                     psA[:, 0:2, :].rearrange("p a n -> p (a n)"), ACT.Copy).then_inc(turned_act, 1)
                finished(act, values_mm, g)
                finished(act, out_mm, g - 1)
                nc.scalar.activation(vals[:, 0:4, :].rearrange("p h n -> p (h n)"), psB[:, 0, :], ACT.Copy
                                     ).then_inc(values_act, 1)

        @block.vector
        def _(dve):
            ch = Chain(dve, k.dve_chain)
            with dve.Fori(0, GROUPS) as g:
                finished(dve, kv_mm, g)
                nc.vector.tensor_copy(kT[:, :, :].rearrange("p j n -> p (j n)"), psA[:, 2, :])
                nc.vector.tensor_copy(v[:, :], psA[:, 3, 0:NKV * HD]).then_inc(kv_copied, 1)
                for n in range(4):
                    finished(dve, scores_mm, g * 4 + n)
                    finished(dve, turned, g * 4 + (n - 4) if n == 3 else g * 4 - 1)
                    ch.link(nc.vector.tensor_tensor(prob[:, n, :, :], psB[:, n, :].rearrange("p (i n) -> p i n", i=4),
                                                    k.mask.unsqueeze(1).to_broadcast([P, 4, P]), ALU.add))
                    ch.link(nc.vector.tensor_reduce(top[:, n, :], prob[:, n, :, :], AX, ALU.max))
                    nc.vector.tensor_scalar(shift[:, n, :], top[:, n, :], -INV, None, ALU.mult).then_inc(max_ready, 1)
                for n in range(4):
                    finished(dve, exp_done, g * 4 + n)
                    ch.link(nc.vector.reciprocal(rinv[:, n, :], rsum[:, n, :]))
                    nc.vector.tensor_tensor(prob[:, n, :, :], prob[:, n, :, :],
                                            rinv[:, n, :].unsqueeze(2).to_broadcast([P, 4, P]), ALU.mult
                                            ).then_inc(normed, 1)
                for n in range(2, 4):
                    finished(dve, turned, g * 4 + n)
                finished(dve, values_mm, g - 1)
                nc.vector.tensor_copy(probT[:, 2:4, :, :].rearrange("p a i n -> p (a i n)"),
                                      psA[:, 2:4, :].rearrange("p a n -> p (a n)")).then_inc(turned_dve, 1)
                finished(dve, values_mm, g)
                finished(dve, out_mm, g - 1)
                nc.vector.tensor_copy(vals[:, 4:8, :].rearrange("p h n -> p (h n)"), psB[:, 1, :]).then_inc(values_dve, 1)
                finished(dve, out_mm, g)
                finished(dve, low_scaled, g)
                nc.vector.scalar_tensor_tensor(out=k.att[:, bass.ds(g * D, D)], in0=psB[:, 2, 0:D], scalar=k.alpha[:, 0:1],
                                               in1=low_rows[:, :], op0=ALU.mult, op1=ALU.subtract).then_inc(out_copied, 1)
                ch.restart()


def stage_d(nc, d, k, out):
    QT = 4
    STEPS = TILES // QT
    QE = QT * E
    with Stage(nc, "d") as st:
        w_loaded, counts_zeroed = st.sems("w_loaded counts_zeroed")
        rows_stored = st.sems("rows_stored0 rows_stored1")
        out_stored = st.sems("out_stored0 out_stored1")
        stages = st.sems("low_mm h_ready var_ready rstd_ready x_ready turned xT_ready route_mm scores_ready chosen counts_mm "
                         "counted total_ready up_mm silu_done hidden_ready down_mm out_ready rows_ready pow_done")
        (low_mm, h_ready, var_ready, rstd_ready, x_ready, turned, xT_ready, route_mm, scores_ready, chosen, counts_mm,
         counted, total_ready, up_mm, silu_done, hidden_ready, down_mm, out_ready, rows_ready, pow_done) = stages
        route = st.sb("route", [P, DH, E])
        shared = st.sb("shared", [P, DH, 2 * D])
        down = st.sb("down", [P, DH, D])
        bias = st.sb("bias", [P, E])
        h = [st.sb(f"h{i}", [P, QT, D]) for i in range(2)]
        x = [st.sb(f"x{i}", [P, QT, XW]) for i in range(2)]
        xT = [st.sb(f"xT{i}", [P, DH, QT * P]) for i in range(2)]
        stats = st.sb("stats", [P, QT, 6])
        mv = st.sb("mv", [P, QT, 2])
        veps = st.sb("veps", [P, QT])
        rstd = st.sb("rstd", [P, QT])
        shift = st.sb("shift", [P, QT])
        neg_mean = st.sb("neg_mean", [P, QT])
        scores = [st.sb(f"scores{i}", [P, QE]) for i in range(2)]
        biased = st.sb("biased", [P, QE])
        m1, n1 = st.sb("m1", [P, QT * NG * 4]), st.sb("n1", [P, QT * NG * 4])
        m2, n2, l2 = (st.sb(n, [P, QT * NG * 2]) for n in ("m2", "n2", "l2"))
        m3, n3, l3 = (st.sb(n, [P, QT * NG]) for n in ("m3", "n3", "l3"))
        ge, gt = st.sb("ge", [P, QT, NG * NG]), st.sb("gt", [P, QT, NG * NG])
        best = st.sb("best", [P, QT, 8])
        taken = st.sb("taken", [P, QE])
        sel = st.sb("sel", [P, QE], F16)
        sel_sum = st.sb("sel_sum", [P, E])
        before = st.sb("before", [P, E], F16)
        wsum, winv = st.sb("wsum", [P, QT]), st.sb("winv", [P, QT])
        silu = [st.sb(f"silu{i}", [P, QT * P]) for i in range(2)]
        hidden = [st.sb(f"hidden{i}", [P, QT * P]) for i in range(2)]
        res = [st.sb(f"res{i}", [P, QT, D]) for i in range(2)]
        low_ps, x_ps = st.banks("low", 2), st.banks("x", 2)
        route_ps, count_ps = st.bank("route"), st.bank("count")
        gate_ps, up_ps = st.bank("gate"), st.bank("up")
        block = st.block()

        @block.sync
        def _(sp):
            for s in stages:
                sp.sem_inc(s, CREDIT)
            for s in rows_stored + out_stored:
                sp.sem_inc(s, 16)
            sp.dma_start(route[:, :, :], d["route_T"].rearrange("(c p) n -> p c n", p=P)).then_inc(w_loaded, 16)
            sp.dma_start(shared[:, :, :], d["shared_T"].rearrange("(c p) n -> p c n", p=P)).then_inc(w_loaded, 16)
            sp.dma_start(down[:, :, :], d["down_T"].rearrange("(c p) n -> p c n", p=P)).then_inc(w_loaded, 16)
            sp.dma_start(bias[:, :], d["e_bias"].partition_broadcast(P)).then_inc(w_loaded, 16)
            with sp.Fori(0, STEPS // 2) as i:
                for par in range(2):
                    s = 2 * i + par
                    finished(sp, rows_ready, s)
                    finished(sp, x_ready, s)
                    sp.dma_start(k.token_rows[bass.ds(s * QT * P, QT * P), :].rearrange("(t p) n -> p t n", p=P),
                                 x[par][:, :, :]).then_inc(rows_stored[par], 16)
                    finished(sp, out_ready, s)
                    sp.dma_start(out[bass.ds(s * QT * P, QT * P), :].rearrange("(t p) n -> p t n", p=P),
                                 res[par][:, :, :]).then_inc(out_stored[par], 16)
            for s in rows_stored + out_stored:
                sp.wait_ge(s, 16 * (STEPS // 2 + 1))

        @block.gpsimd
        def _(pool):
            pool.wait_ge(k.trash_zeroed, 1)
            pool.dma_start(out[T:T + CAP, :].rearrange("(t p) n -> p t n", p=P),
                           k.zeros.rearrange("p (t n) -> p t n", t=HALVES)).then_inc(k.trash_stored, 16)
            with pool.Fori(0, STEPS) as s:
                pool_finished(pool, k, var_ready, s)
                pool_finished(pool, k, x_ready, s - 1)
                nc.gpsimd.tensor_tensor(rstd[:, :], veps[:, :], k.cols[:, 4:5].to_broadcast([P, QT]), ALU.pow
                                        ).then_inc(pow_done, 1)
                pool_finished(pool, k, pow_done, s)
                nc.gpsimd.tensor_tensor(shift[:, :], neg_mean[:, :], rstd[:, :], ALU.mult).then_inc(rstd_ready, 1)
            pool.wait_ge(k.trash_stored, 16)

        @block.tensor
        def _(pe):
            def low_bins(i, c):
                s = 2 * i + c
                finished(pe, h_ready, s - 1)
                for t in range(QT):
                    mm = nc.tensor.matmul(low_ps[:, t // 2, t % 2 * D:(t % 2 + 1) * D], k.idft_low[:, QT * (c % 2) + t, :],
                                          k.att[:, bass.ds((i + c // 2) * D, D)], start=True, stop=True)
                mm.then_inc(low_mm, 1)

            def turn(s, par):
                finished(pe, x_ready, s)
                finished(pe, out_ready, s - 2)
                for t in range(QT):
                    for c in range(DH):
                        mm = nc.tensor.transpose(x_ps[:, c, t * P:(t + 1) * P], x[par][:, t, c * P:(c + 1) * P], k.ident)
                mm.then_inc(turned, 1)

            def routing(s, par):
                finished(pe, xT_ready, s)
                finished(pe, scores_ready, s - 1)
                for t in range(QT):
                    for c in range(DH):
                        mm = nc.tensor.matmul(route_ps[:, t * E:(t + 1) * E], xT[par][:, c, t * P:(t + 1) * P], route[:, c, :],
                                              start=c == 0, stop=c == DH - 1)
                mm.then_inc(route_mm, 1)

            def up(s, par, f):
                finished(pe, hidden_ready, s * 2 + (f - 1))
                for ps, o in ((gate_ps, 0), (up_ps, D)):
                    for c in range(DH):
                        mm = nc.tensor.matmul(ps[:, :], shared[:, c, o + f * P:o + (f + 1) * P], xT[par][:, c, :],
                                              start=c == 0, stop=c == DH - 1)
                mm.then_inc(up_mm, 1)

            def down_product(s):
                finished(pe, hidden_ready, s * 2 + 1)
                for t in range(QT):
                    for f in range(2):
                        mm = nc.tensor.matmul(x_ps[:, t // 2, t % 2 * D:(t % 2 + 1) * D], hidden[f][:, t * P:(t + 1) * P],
                                              down[:, f, :], start=f == 0, stop=f == 1)
                mm.then_inc(down_mm, 1)

            def count(s):
                finished(pe, chosen, s)
                finished(pe, total_ready, s - 1)
                finished(pe, counted, s - 1)
                for t in range(QT):
                    to = count_ps[:, t * E:(t + 1) * E]
                    nc.tensor.matmul(to, k.ones, before[:, :], start=True, stop=False)
                    for u in range(t):
                        nc.tensor.matmul(to, k.ones, sel[:, u * E:(u + 1) * E], start=False, stop=False)
                    mm = nc.tensor.matmul(to, k.tri, sel[:, t * E:(t + 1) * E], start=False, stop=True)
                mm.then_inc(counts_mm, 1)

            def body(i, par, last=STEPS):
                s, nxt = 2 * i + par, 1 - par
                up(s, par, 1)
                if last > 1:
                    turn(s + 1, nxt)
                    routing(s + 1, nxt)
                count(s)
                down_product(s)
                if last > 1:
                    up(s + 1, nxt, 0)
                if last > 2:
                    low_bins(i, par + 2)

            pe.wait_ge(w_loaded, 16 * 4)
            pe.wait_ge(counts_zeroed, 2)
            low_bins(0, 0)
            turn(0, 0)
            low_bins(0, 1)
            routing(0, 0)
            up(0, 0, 0)
            rounds = STEPS // 2 - 1
            with pe.Fori(0, rounds) as i:
                for par in range(2):
                    body(i, par)
            for par in range(2):
                body(rounds, par, last=2 - par)

        @block.scalar
        def _(act):
            def normalise(i, c):
                s, par = 2 * i + c, c % 2
                finished(act, rstd_ready, s)
                act.wait_ge(rows_stored[par], 16 * i + 16 * (c // 2 + 1))
                for t in range(QT):
                    ins = nc.scalar.activation(x[par][:, t, 0:D], h[par][:, t, :], ACT.Identity, scale=rstd[:, t:t + 1],
                                               bias=shift[:, t:t + 1])
                ins.then_inc(x_ready, 1)

            def turn_copy(s, par):
                finished(act, turned, s)
                finished(act, up_mm, 2 * s - 3)
                nc.scalar.activation(xT[par][:, :, :].rearrange("p c n -> p (c n)"),
                                     x_ps[:, :, :].rearrange("p c n -> p (c n)"), ACT.Copy).then_inc(xT_ready, 1)

            def score(s, par, first=False):
                finished(act, route_mm, s)
                finished(act, rows_ready, s - 2)
                nc.scalar.activation(scores[par][:, :], route_ps[:, 0:QE], ACT.Sigmoid).then_inc(scores_ready, 1)

            def silu_fn(s, f):
                finished(act, up_mm, s * 2 + f)
                finished(act, hidden_ready, s * 2 + (f - 2))
                nc.scalar.activation(silu[f][:, :], gate_ps[:, :], ACT.Silu).then_inc(silu_done, 1)

            def body(i, par, more=True):
                s, nxt = 2 * i + par, 1 - par
                silu_fn(s, 1)
                if more:
                    normalise(i, par + 1)
                    turn_copy(s + 1, nxt)
                    score(s + 1, nxt)
                    silu_fn(s + 1, 0)

            normalise(0, 0)
            finished(act, turned, 0)
            nc.scalar.activation(xT[0][:, :, :].rearrange("p c n -> p (c n)"),
                                 x_ps[:, :, :].rearrange("p c n -> p (c n)"), ACT.Copy).then_inc(xT_ready, 1)
            score(0, 0)
            silu_fn(0, 0)
            rounds = STEPS // 2 - 1
            with act.Fori(0, rounds) as i:
                for par in range(2):
                    body(i, par)
            for par in range(2):
                body(rounds, par, more=par == 0)

        @block.vector
        def _(dve):
            ch = Chain(dve, k.dve_chain)

            def tt(o, a, b, op):
                return nc.vector.tensor_tensor(o, a, b, op)

            def token_norm(s, par):
                finished(dve, low_mm, s)
                finished(dve, rstd_ready, s - 1)
                finished(dve, out_ready, s - 2)
                for b in range(2):
                    ch.mark(tt(h[par][:, 2 * b:2 * b + 2, :].rearrange("p t n -> p (t n)"), low_ps[:, b, :],
                               k.z[:, bass.ds(s * QT * D + b * 2 * D, 2 * D)], ALU.add))
                ch.reach(ch.n)
                for t in range(QT):
                    ch.mark(nc.vector.bn_stats(stats[:, t, :], h[par][:, t, :]))
                ch.reach(ch.n)
                for t in range(QT):
                    ch.mark(nc.vector.bn_aggr(mv[:, t, :], stats[:, t, :]))
                ch.reach(ch.n)
                nc.vector.tensor_scalar(neg_mean[:, :], mv[:, :, 0], -1.0, None, ALU.mult).then_inc(h_ready, 1)
                nc.vector.tensor_scalar(veps[:, :], mv[:, :, 1], 1e-5, None, ALU.add).then_inc(var_ready, 1)

            def choose(s, par):
                finished(dve, scores_ready, s)
                ch.link(tt(biased[:, :].rearrange("p (t e) -> p t e", t=QT), scores[par][:, :].rearrange("p (t e) -> p t e", t=QT),
                           bias[:, :].unsqueeze(1).to_broadcast([P, QT, E]), ALU.add))
                v = biased[:, :].rearrange("p (g a) -> p g a", a=2)
                ch.mark(tt(m1[:, :], v[:, :, 0], v[:, :, 1], ALU.max))
                ch.link(tt(n1[:, :], v[:, :, 0], v[:, :, 1], ALU.min))
                for (m, n), (mo, no, lo) in (((m1, n1), (m2, n2, l2)), ((m2, n2), (m3, n3, l3))):
                    mm, nn = (q[:, :].rearrange("p (g a) -> p g a", a=2) for q in (m, n))
                    ch.mark(tt(mo[:, :], mm[:, :, 0], mm[:, :, 1], ALU.max))
                    ch.mark(tt(lo[:, :], mm[:, :, 0], mm[:, :, 1], ALU.min))
                    ch.link(tt(no[:, :], nn[:, :, 0], nn[:, :, 1], ALU.max))
                    ch.link(tt(no[:, :], no[:, :], lo[:, :], ALU.max))
                ch.link(tt(m3[:, :], m3[:, :], n3[:, :], ALU.add))
                gs = m3[:, :].rearrange("p (t g) -> p t g", t=QT)
                for t in range(QT):
                    other = gs[:, t, :].unsqueeze(1).to_broadcast([P, NG, NG])
                    own = gs[:, t, :].unsqueeze(2).to_broadcast([P, NG, NG])
                    ch.mark(tt(ge[:, t, :].rearrange("p (g o) -> p g o", g=NG), other, own, ALU.is_ge))
                    ch.mark(tt(gt[:, t, :].rearrange("p (g o) -> p g o", g=NG), other, own, ALU.is_gt))
                ch.reach(ch.n)
                for q, a in ((ge, 0), (gt, 1)):
                    ch.mark(tt(q[:, :, :], q[:, :, :], k.tie[:, a, :, :].rearrange("p g o -> p (g o)").unsqueeze(1)
                               .to_broadcast([P, QT, NG * NG]), ALU.mult))
                ch.reach(ch.n)
                ch.link(tt(ge[:, :, :], ge[:, :, :], gt[:, :, :], ALU.add))
                ch.link(nc.vector.tensor_reduce(l3[:, :], ge[:, :, :].rearrange("p t (g o) -> p (t g) o", g=NG), AX, ALU.add))
                ch.link(nc.vector.tensor_scalar(l3[:, :], l3[:, :], float(TG), None, ALU.is_lt))
                ch.link(tt(biased[:, :].rearrange("p (g e) -> p g e", e=E // NG),
                           biased[:, :].rearrange("p (g e) -> p g e", e=E // NG),
                           l3[:, :].unsqueeze(2).to_broadcast([P, QT * NG, E // NG]), ALU.mult))
                for t in range(QT):
                    ch.mark(nc.vector.max(best[:, t, :], biased[:, t * E:(t + 1) * E]))
                ch.reach(ch.n)
                for t in range(QT):
                    ch.mark(nc.vector.match_replace(taken[:, t * E:(t + 1) * E], best[:, t, :],
                                                    biased[:, t * E:(t + 1) * E], NEG))
                ch.reach(ch.n)
                finished(dve, counts_mm, s - 1)
                tt(sel[:, :], taken[:, :], biased[:, :], ALU.not_equal).then_inc(chosen, 1)
                finished(dve, chosen, s)

            def weights(s, par):
                w = x[par][:, :, D:XW]
                ch.link(tt(w, scores[par][:, :].rearrange("p (t e) -> p t e", t=QT), sel[:, :].rearrange("p (t e) -> p t e", t=QT),
                           ALU.mult))
                ch.link(nc.vector.tensor_reduce(wsum[:, :], w, AX, ALU.add))
                ch.link(nc.vector.tensor_scalar(wsum[:, :], wsum[:, :], 1e-20, None, ALU.add))
                ch.link(nc.vector.reciprocal(winv[:, :], wsum[:, :]))
                nc.vector.scalar_tensor_tensor(out=w, in0=w, scalar=SCALE, in1=winv[:, :].unsqueeze(2).to_broadcast([P, QT, E]),
                                               op0=ALU.mult, op1=ALU.mult).then_inc(rows_ready, 1)

            def act_mul(s, f):
                finished(dve, silu_done, s * 2 + f)
                finished(dve, down_mm, s - 1)
                tt(hidden[f][:, :], up_ps[:, :], silu[f][:, :], ALU.mult).then_inc(hidden_ready, 1)

            def result(i, par):
                s = 2 * i + par
                finished(dve, down_mm, s)
                dve.wait_ge(out_stored[par], 16 * i + 16)
                for b in range(2):
                    ins = tt(res[par][:, 2 * b:2 * b + 2, :].rearrange("p t n -> p (t n)"), x_ps[:, b, :],
                             h[par][:, 2 * b:2 * b + 2, :].rearrange("p t n -> p (t n)"), ALU.add)
                ins.then_inc(out_ready, 1)

            def count(s):
                finished(dve, counts_mm, s)
                to = k.counts[:, 1:].rearrange("p (e t) -> p t e", e=E)[:, bass.ds(s * QT, QT), :]
                nc.vector.tensor_scalar(to, count_ps[:, 0:QE].rearrange("p (t e) -> p t e", t=QT), COUNT_MAX, None, ALU.min
                                        ).then_inc(counted, 1)
                ch.link(nc.vector.tensor_reduce(sel_sum[:, :], sel[:, :].rearrange("p (t e) -> p e t", t=QT), AX, ALU.add))
                tt(before[:, :], before[:, :], sel_sum[:, :], ALU.add).then_inc(total_ready, 1)

            ch.link(nc.vector.memset(k.zeros, 0.0))
            nc.vector.memset(before[:, :], 0.0).then_inc(counts_zeroed, 1)
            nc.vector.memset(k.counts[:, 0:1], 0.0).then_inc(counts_zeroed, 1)
            nc.vector.memset(l3[:, :], 0.0).then_inc(k.trash_zeroed, 1)
            ch.restart()
            dve.wait_ge(w_loaded, 16 * 4)
            def body(i, par, more=True):
                s = 2 * i + par
                if more:
                    token_norm(s + 1, 1 - par)
                act_mul(s, 0)
                choose(s, par)
                act_mul(s, 1)
                weights(s, par)
                result(i, par)
                count(s)

            token_norm(0, 0)
            ch.restart()
            rounds = STEPS // 2 - 1
            with dve.Fori(0, rounds) as i:
                for par in range(2):
                    body(i, par)
                ch.restart()
            for par in range(2):
                body(rounds, par, more=par == 0)
            ch.restart()


def stage_e(nc, d, k, out):
    PAIRS, LEAD, AHEAD, ROUND = E // 2, 4, 3, 4
    LOOPS = (PAIRS - LEAD) // 2
    with Stage(nc, "e") as st:
        w_loaded = st.sems("w_loaded0 w_loaded1 w_loaded2 w_loaded3")
        gathered = st.sems("gathered0 gathered1 gathered2 gathered3")
        added = st.sems("added0 added1")
        gi_ready, si_ready = st.sems("gi_ready si_ready")
        stages = st.sems("indices_ready counts_mm counts_copied bounds_ready tile_found picked compared turned xT_ready "
                         "gate_mm up_mm gate_ready hidden_ready down_mm weights_ready scaled")
        (indices_ready, counts_mm, counts_copied, bounds_ready, tile_found, picked, compared, turned, xT_ready,
         gate_mm, up_mm, gate_ready, hidden_ready, down_mm, weights_ready, scaled) = stages
        cts = st.sb("cts", [P, P], F16)
        bounds = st.sb("bounds", [P, 2])
        hot = st.sb("hot", [P, CAP], F16)
        below = st.sb("below", [P, 2, HALVES, P])
        fine = st.sb("fine", [P, 2 * HALVES])
        token = st.sb("token", [P, 2 * HALVES])
        empty = st.sb("empty", [P, 2 * HALVES])
        w = [st.sb(f"w{i}", [P, 3 * D]) for i in range(ROUND)]
        x = [st.sb(f"x{i}", [P, HALVES, XW]) for i in range(ROUND)]
        gi = [st.sb(f"gi{i}", [P, HALVES], I32) for i in range(ROUND)]
        si = [st.sb(f"si{i}", [P, HALVES], I32) for i in range(2)]
        xT = [st.sb(f"xT{i}", [P, DH, CAP]) for i in range(2)]
        gate = [st.sb(f"gate{i}", [P, CAP]) for i in range(2)]
        hidden = [st.sb(f"hidden{i}", [P, CAP]) for i in range(2)]
        wcol = [st.sb(f"wcol{i}", [P, HALVES]) for i in range(2)]
        y = [st.sb(f"y{i}", [P, HALVES, D]) for i in range(2)]
        x_ps = [st.bank(f"x{i}") for i in range(2)]
        gate_ps, up_ps, down_ps, col_ps = (st.bank(n) for n in ("gate", "up", "down", "col"))
        pick_ps = st.banks("pick", 2)
        block = st.block()

        def seen(s_sems, i, c):
            return s_sems[c % ROUND], 32 * i + 32 * (c // ROUND + 1)

        @block.sync
        def _(sp):
            for s in stages:
                sp.sem_inc(s, CREDIT)

            def load(i, c):
                sp.dma_start(w[c][:, :], d["experts"][bass.ds(ROUND * i + c, 1), :, :].rearrange("a p n -> p (a n)")
                             ).then_inc(w_loaded[c], 16)

            for c in range(ROUND):
                load(0, c)
            with sp.Fori(1, E // ROUND) as i:
                for c in range(ROUND):
                    finished(sp, down_mm, ROUND * i + (c - ROUND))
                    load(i, c)

        @block.gpsimd
        def _(pool):
            def gather(i, c):
                s, slot = ROUND * i + c, c % ROUND
                pool_finished(pool, k, indices_ready, (ROUND // 2) * i + c // 2)
                if not (isinstance(s, int) and s < ROUND):
                    pool_finished(pool, k, weights_ready, s - ROUND)
                    pool_finished(pool, k, turned, s - ROUND)
                nc.gpsimd.tensor_copy(gi[slot][:, :], k.gather_idx[:, bass.ds(s, 1), :].rearrange("p a h -> p (a h)")
                                      ).then_inc(gi_ready, 1)
                pool.wait_ge(gi_ready, s + 1)
                pool.sem_inc(k.pool_waited, 1)
                for hf in range(HALVES):
                    nc.gpsimd.indirect_dma_start(x[slot][:, hf, :], None, k.token_rows[:, :],
                                                 bass.IndirectOffsetOnAxis(ap=gi[slot][:, hf:hf + 1], axis=0),
                                                 bounds_check=T - 1).then_inc(gathered[slot], 16)

            def add(i, c):
                s, par = ROUND * i + c, c % 2
                nc.gpsimd.tensor_copy(si[par][:, :], k.scatter_idx[:, bass.ds(s, 1), :].rearrange("p a h -> p (a h)")
                                      ).then_inc(si_ready, 1)
                pool.wait_ge(si_ready, s + 1)
                pool.sem_inc(k.pool_waited, 1)
                pool_finished(pool, k, scaled, s)
                if not (isinstance(s, int) and s == 0):
                    pool.wait_ge(added[1 - par], 64 * i + 32 * ((c + 1) // 2))
                    pool.sem_inc(k.pool_waited, 1)
                for hf in range(HALVES):
                    nc.gpsimd.indirect_dma_start(out[:, :], bass.IndirectOffsetOnAxis(ap=si[par][:, hf:hf + 1], axis=0),
                                                 y[par][:, hf, :], None, bounds_check=T + CAP - 1, compute_op=ALU.add
                                                 ).then_inc(added[par], 16)

            for c in range(AHEAD):
                gather(0, c)
            for c in range(ROUND):
                gather(0, c + AHEAD)
                add(0, c)
            with pool.Fori(1, LOOPS) as i:
                for c in range(ROUND):
                    gather(i, c + AHEAD)
                    add(i, c)
            for c in range(2 * ROUND):
                if c + AHEAD < 2 * ROUND:
                    gather(LOOPS, c + AHEAD)
                add(LOOPS, c)
            for s in added:
                pool.wait_ge(s, 32 * (E // 2))

        @block.tensor
        def _(pe):
            def columns(q):
                finished(pe, counts_copied, q - 1)
                now = k.counts[:, bass.ds(q * P + 1, P)]
                last = k.counts[:, bass.ds(q * P, P)]
                nc.tensor.matmul(col_ps[:, 0:P], now, k.ident16, start=True, stop=True)
                nc.tensor.matmul(col_ps[:, P:P + 1], last, k.ident16[:, P - 1:P], start=True, stop=True
                                 ).then_inc(counts_mm, 1)

            def pick(q):
                finished(pe, tile_found, q)
                finished(pe, counts_copied, q)
                finished(pe, compared, q - 1)
                for e in range(2):
                    rows = slice(e * TILES, (e + 1) * TILES)
                    for hf in range(HALVES):
                        one = hot[rows, hf * P:(hf + 1) * P]
                        nc.tensor.matmul(pick_ps[:, e, hf * P:(hf + 1) * P], one, cts[rows, :], start=True, stop=True)
                        mm = nc.tensor.matmul(pick_ps[:, e, CAP + hf:CAP + hf + 1], one, k.tile_col[rows, :],
                                              start=True, stop=True)
                mm.then_inc(picked, 1)

            def turn(i, c):
                s, slot, par = ROUND * i + c, c % ROUND, c % 2
                pe.wait_ge(*seen(gathered, i, c))
                finished(pe, xT_ready, s - 2)
                for hf in range(HALVES):
                    for h in range(DH):
                        mm = nc.tensor.transpose(x_ps[par][:, h * CAP + hf * P:h * CAP + (hf + 1) * P],
                                                 x[slot][:, hf, h * P:(h + 1) * P], k.ident)
                mm.then_inc(turned, 1)

            def expand(i, c):
                s, slot, par = ROUND * i + c, c % ROUND, c % 2
                finished(pe, xT_ready, s)
                finished(pe, hidden_ready, s - 1)
                pe.wait_ge(w_loaded[slot], 16 * i + 16 * (c // ROUND + 1))
                for m, (ps, done) in enumerate(((gate_ps, gate_mm), (up_ps, up_mm))):
                    for h in range(DH):
                        mm = nc.tensor.matmul(ps[:, 0:CAP], w[slot][:, m * D + h * FF:m * D + (h + 1) * FF], xT[par][:, h, :],
                                              start=h == 0, stop=h == DH - 1)
                    mm.then_inc(done, 1)

            def contract(i, c):
                s, slot, par = ROUND * i + c, c % ROUND, c % 2
                finished(pe, hidden_ready, s)
                finished(pe, scaled, s - 1)
                for hf in range(HALVES):
                    mm = nc.tensor.matmul(down_ps[:, hf * D:(hf + 1) * D], hidden[par][:, hf * P:(hf + 1) * P],
                                          w[slot][:, 2 * D:3 * D], start=True, stop=True)
                mm.then_inc(down_mm, 1)

            def body(i, c, slots=True, more=True):
                if more:
                    turn(i, c + 1)
                if slots:
                    (columns if c % 2 == 0 else pick)(2 * i + (c // 2 + LEAD))
                contract(i, c)
                if more:
                    expand(i, c + 1)

            for q in range(LEAD):
                columns(q)
                pick(q)
            turn(0, 0)
            expand(0, 0)
            with pe.Fori(0, LOOPS) as i:
                for c in range(ROUND):
                    body(i, c)
            for c in range(2 * ROUND):
                body(LOOPS, c, slots=False, more=c < 2 * ROUND - 1)

        @block.scalar
        def _(act):
            def column_copies(q):
                finished(act, counts_mm, q)
                finished(act, tile_found, q - 1)
                nc.scalar.activation(bounds[:, 0:1], col_ps[:, P - 1:P], ACT.Copy)
                nc.scalar.activation(bounds[:, 1:2], col_ps[:, P:P + 1], ACT.Copy, scale=k.cols[:, 5:6]
                                     ).then_inc(bounds_ready, 1)
                finished(act, picked, q - 1)
                nc.scalar.activation(cts[:, :], col_ps[:, 0:P], ACT.Copy).then_inc(counts_copied, 1)

            def turn_copy(s, par):
                finished(act, turned, s)
                finished(act, up_mm, s - 2)
                nc.scalar.activation(xT[par][:, :, :].rearrange("p c n -> p (c n)"), x_ps[par][:, :], ACT.Copy
                                     ).then_inc(xT_ready, 1)

            def gate_fn(s, par):
                finished(act, gate_mm, s)
                finished(act, hidden_ready, s - 2)
                nc.scalar.activation(gate[par][:, :], gate_ps[:, 0:CAP], ACT.Silu).then_inc(gate_ready, 1)

            def scale(i, c):
                s, par = ROUND * i + c, c % 2
                finished(act, down_mm, s)
                finished(act, weights_ready, s)
                if not (isinstance(s, int) and s < 2):
                    act.wait_ge(added[par], 64 * i + 32 * (c // 2))
                for hf in range(HALVES):
                    ins = nc.scalar.activation(y[par][:, hf, :], down_ps[:, hf * D:(hf + 1) * D], ACT.Copy,
                                               scale=wcol[par][:, hf:hf + 1])
                ins.then_inc(scaled, 1)

            def body(i, c, slots=True, more=True):
                s = ROUND * i + c
                if more:
                    turn_copy(s + 1, (c + 1) % 2)
                if slots and c % 2 == 0:
                    column_copies(2 * i + (c // 2 + LEAD))
                scale(i, c)
                if more:
                    gate_fn(s + 1, (c + 1) % 2)

            for q in range(LEAD):
                column_copies(q)
            turn_copy(0, 0)
            gate_fn(0, 0)
            for c in range(ROUND):
                body(0, c)
            with act.Fori(1, LOOPS) as i:
                for c in range(ROUND):
                    body(i, c)
            for c in range(2 * ROUND):
                body(LOOPS, c, slots=False, more=c < 2 * ROUND - 1)

        @block.vector
        def _(dve):
            ch = Chain(dve, k.dve_chain)

            def find_tile(q):
                finished(dve, bounds_ready, q)
                finished(dve, picked, q - 1)
                ch.link(nc.vector.tensor_scalar(hot[:, :], k.slot_row, bounds[:, 1:2], None, ALU.is_ge))
                nc.vector.scalar_tensor_tensor(out=hot[:, :], in0=k.slot_row, scalar=bounds[:, 0:1],
                                               in1=hot[:, :], op0=ALU.is_lt, op1=ALU.mult).then_inc(tile_found, 1)

            def find_token(q):
                finished(dve, picked, q)
                for hf in range(HALVES):
                    ch.mark(nc.vector.tensor_scalar(below[:, :, hf, :], pick_ps[:, :, hf * P:(hf + 1) * P],
                                                    k.cols[:, hf:hf + 1], None, ALU.is_le))
                ch.reach(ch.n)
                ch.link(nc.vector.tensor_reduce(fine[:, :], below[:, :, :, :].rearrange("p e h n -> p (e h) n"), AX, ALU.add))
                ch.mark(nc.vector.tensor_scalar(empty[:, :], fine[:, :], P - 0.5, None, ALU.is_ge))
                nc.vector.scalar_tensor_tensor(out=token[:, :].rearrange("p (e h) -> p e h", e=2),
                                               in0=pick_ps[:, :, CAP:CAP + HALVES], scalar=float(P),
                                               in1=fine[:, :].rearrange("p (e h) -> p e h", e=2),
                                               op0=ALU.mult, op1=ALU.add).then_inc(compared, 1)
                finished(dve, compared, q)
                ch.reach(ch.n)
                pair = token[:, :].rearrange("p (e h) -> p e h", e=2)
                ch.mark(nc.vector.tensor_copy(k.gather_idx[:, bass.ds(2 * q, 2), :], pair))
                ch.link(nc.vector.tensor_tensor(empty[:, :].rearrange("p (e h) -> p e h", e=2),
                                                empty[:, :].rearrange("p (e h) -> p e h", e=2),
                                                k.cols[:, 2:4].unsqueeze(1).to_broadcast([P, 2, HALVES]), ALU.mult))
                nc.vector.tensor_tensor(k.scatter_idx[:, bass.ds(2 * q, 2), :], pair,
                                        empty[:, :].rearrange("p (e h) -> p e h", e=2), ALU.add).then_inc(indices_ready, 1)

            def weight_columns(i, c):
                s, slot, par = ROUND * i + c, c % ROUND, c % 2
                dve.wait_ge(*seen(gathered, i, c))
                finished(dve, scaled, s - 2)
                nc.vector.tensor_copy(wcol[par][:, :], x[slot][:, :, bass.ds(s + D, 1)].rearrange("p h a -> p (h a)")
                                      ).then_inc(weights_ready, 1)

            def act_mul(i, c):
                s, par = ROUND * i + c, c % 2
                finished(dve, gate_ready, s)
                finished(dve, down_mm, s - 2)
                finished(dve, up_mm, s)
                nc.vector.tensor_tensor(hidden[par][:, :], up_ps[:, 0:CAP], gate[par][:, :], ALU.mult
                                        ).then_inc(hidden_ready, 1)

            def body(i, c, slots=True, more=True):
                if more:
                    weight_columns(i, c + 1)
                if slots:
                    (find_tile if c % 2 == 0 else find_token)(2 * i + (c // 2 + LEAD))
                if more:
                    act_mul(i, c + 1)

            for q in range(LEAD):
                find_tile(q)
                find_token(q)
            weight_columns(0, 0)
            act_mul(0, 0)
            ch.restart()
            with dve.Fori(0, LOOPS) as i:
                for c in range(ROUND):
                    body(i, c)
                ch.restart()
            for c in range(2 * ROUND):
                body(LOOPS, c, slots=False, more=c < 2 * ROUND - 1)
            ch.restart()


_IN = [("x", [P, TILES], I32), ("codes_T", [D, CODES], F32), ("tok_W1", [D, HID], F32), ("tok_b1", [P, HC], F32),
       ("tok_W2", [HID, D], F32), ("tok_b2", [1, D], F32), ("alpha_raw", [1, 1], F32),
       ("pw_T", [2, D, D], F32), ("gate_wT", [D, D], F32), ("dw", [P, 2 * DH * TAPS], F32),
       ("q_T", [D, NH * HD], F32), ("k_T", [D, NKV * 2 * HD], F32), ("v_T", [D, NKV * HD], F32), ("o_T", [NH * HD, D], F32),
       ("route_T", [D, E], F32), ("e_bias", [1, E], F32), ("shared_T", [D, 2 * D], F32), ("down_T", [D, D], F32),
       ("experts", [E, P, 3 * D], F32)]


def kernel(x, L0_tok_codebook, L0_tok_W1, L0_tok_b1, L0_tok_W2, L0_tok_b2, L0_attn_q_w, L0_attn_k_w, L0_attn_v_w,
           L0_attn_o_w, L0_attn_dw_r, L0_attn_pw_r, L0_attn_dw_i, L0_attn_pw_i, L0_attn_gate_w, L0_attn_alpha_raw,
           L0_ffn_gate_weight, L0_ffn_e_bias, L0_ffn_w1, L0_ffn_w2, L0_ffn_w3, L0_ffn_shared_gate, L0_ffn_shared_up,
           L0_ffn_shared_down):
    import numpy as _np
    import concourse.bacc as _bacc
    from concourse.bass_utils import run_bass_kernel_spmd as _run

    def c(a):
        return _np.ascontiguousarray(a)

    def a_(a):
        return _np.asarray(a)

    f32, high, f16 = shape_constants()
    dw = _np.stack([a_(L0_attn_dw_r)[:, 0], a_(L0_attn_dw_i)[:, 0]]).reshape(2, DH, P, TAPS).transpose(2, 0, 1, 3)
    k_T = a_(L0_attn_k_w).reshape(NKV, 1, HD, D).repeat(2, 1).reshape(NKV * 2 * HD, D).T
    w1, w3 = (a_(w).transpose(0, 2, 1).reshape(E, DH, P, FF).transpose(0, 2, 1, 3).reshape(E, P, DH * FF)
              for w in (L0_ffn_w1, L0_ffn_w3))
    w2 = a_(L0_ffn_w2).transpose(0, 2, 1)
    arrays = {
        "x": c(a_(x).reshape(TILES, P).T), "codes_T": c(a_(L0_tok_codebook).T), "tok_W1": c(L0_tok_W1),
        "tok_b1": c(a_(L0_tok_b1).reshape(HC, P).T), "tok_W2": c(L0_tok_W2), "tok_b2": c(a_(L0_tok_b2).reshape(1, D)),
        "alpha_raw": c(a_(L0_attn_alpha_raw).reshape(1, 1)),
        "pw_T": c(_np.stack([a_(L0_attn_pw_r).T, a_(L0_attn_pw_i).T])), "gate_wT": c(a_(L0_attn_gate_w).T),
        "dw": c(dw.reshape(P, -1)), "q_T": c(a_(L0_attn_q_w).T), "k_T": c(k_T), "v_T": c(a_(L0_attn_v_w).T),
        "o_T": c(a_(L0_attn_o_w).T), "route_T": c(a_(L0_ffn_gate_weight).T), "e_bias": c(a_(L0_ffn_e_bias).reshape(1, E)),
        "shared_T": c(_np.concatenate([a_(L0_ffn_shared_gate), a_(L0_ffn_shared_up)]).T),
        "down_T": c(a_(L0_ffn_shared_down).T), "experts": c(_np.concatenate([w1, w3, w2], 2)),
        "c_f32": f32, "c_high": high, "c_f16": f16,
    }
    nc = _bacc.Bacc("TRN2", target_bir_lowering=False, num_devices=1)
    d = {}
    for name, shape, dt in _IN:
        assert list(arrays[name].shape) == shape, (name, arrays[name].shape)
        d[name] = nc.dram_tensor(f"in_{name}", shape, dt, kind="ExternalInput").ap()
    for name in ("c_f32", "c_high", "c_f16"):
        a = arrays[name]
        d[name] = nc.dram_tensor(f"in_{name}", a.shape, mybir.dt.from_np(a.dtype), kind="ExternalInput").ap()
    out = nc.dram_tensor("out_rows", [T + CAP, D], F32, kind="ExternalOutput")
    build(nc, d, out, {n: arrays[n].shape[1] for n in ("c_f32", "c_f16")})
    r = _run(nc, [{f"in_{n}": a for n, a in arrays.items()}], core_ids=[0])
    return r.results[0]["out_rows"][:T].reshape(B, N, D)
```

```python
from contextlib import ExitStack

import numpy as np

import concourse.bass as bass
from concourse import mybir

F32 = mybir.dt.float32
F32R = mybir.dt.float32r
F16 = mybir.dt.float16
I32 = mybir.dt.int32
ALU = mybir.AluOpType
ACT = mybir.ActivationFunctionType
AX = mybir.AxisListType.X

P = 128
B, N, D = 32, 256, 256
T = B * N
TILES = T // P
DH = D // P
CODES, HID = 2048, 1024
HC = HID // P
CHUNK = 64
BINS = CHUNK // 2 + 1
LOW = 4
HIGH = BINS - LOW
TAPS = 7
PAD = TAPS - 1
LOWC = 2 * 2 * LOW
SPEC = LOWC + 2 * 2 * HIGH
NH, NKV, HD = 16, 4, 64
GROUPS = TILES // 8
E, TOPK, NG, TG, FF, CAP = 64, 8, 8, 4, 128, 256
HALVES = CAP // P
XW = D + E
SCALE = 2.5
NEG = -1.0e30
COUNT_MAX = 512.0
TRASH = T
CREDIT = 2


def done(step):
    return step + (1 + CREDIT)


class Kept:
    pass


class Chain:

    def __init__(self, eng, sem):
        self.eng, self.sem, self.n = eng, sem, 0

    def mark(self, ins):
        ins.then_inc(self.sem, 1)
        self.n += 1
        return self.n

    def reach(self, n):
        self.eng.wait_ge(self.sem, n)

    def link(self, ins):
        self.reach(self.mark(ins))

    def restart(self):
        self.reach(self.n)
        self.eng.sem_clear(self.sem)
        self.n = 0


def shape_constants():
    t = np.arange(CHUNK)[:, None]
    k = np.arange(BINS)[None, :]
    ang = 2 * np.pi * ((t * k) % CHUNK) / CHUNK
    re, im = np.cos(ang), -np.sin(ang)
    im[:, 0] = 0
    im[:, BINS - 1] = 0
    dft = np.zeros((P, SPEC))
    for c in range(2):
        rows = slice(c * CHUNK, (c + 1) * CHUNK)
        for r, m in enumerate((re, im)):
            dft[rows, (c * 2 + r) * LOW:(c * 2 + r + 1) * LOW] = m[:, :LOW]
            at = LOWC + (r * 2 + c) * HIGH
            dft[rows, at:at + HIGH] = m[:, LOW:]
    weight = np.full(BINS, 2.0 / CHUNK)
    weight[0] = weight[-1] = 1.0 / CHUNK
    inv = [(re * weight).T, (im * weight).T]
    rows = 4 * HIGH
    idft_high = np.zeros((rows, 2, 2, P))
    for r in range(2):
        for tile in range(2):
            for c in range(2):
                at = (tile * 2 + c) * HIGH
                idft_high[at:at + HIGH, r, tile, c * CHUNK:(c + 1) * CHUNK] = 0.5 * inv[r][LOW:]
    idft_low = np.zeros((P, 8, P))
    for tile in range(8):
        for c in range(2):
            for r in range(2):
                at = tile * LOWC + (c * 2 + r) * LOW
                idft_low[at:at + LOW, tile, c * CHUNK:(c + 1) * CHUNK] = inv[r][:LOW]
    row = np.arange(P)
    batch, chunk, ri = row // (2 * LOWC), row // (2 * LOW) % 4, row // LOW % 2
    ok = (batch[:, None] == batch) & (ri[:, None] == ri) & (chunk[:, None] >= chunk)
    mask = np.where(ok, 0.0, NEG)
    eye = np.eye(P)
    tri = np.triu(np.ones((P, P)))
    before = (np.arange(NG)[None, :] < np.arange(NG)[:, None]).astype(float)
    tie = np.broadcast_to(np.stack([before, 1 - before]).reshape(1, 2 * NG * NG), (P, 2 * NG * NG))
    slot = np.broadcast_to(np.arange(CAP), (P, CAP))
    cols = np.zeros((P, 8))
    cols[:, 0], cols[:, 1] = row, row + P
    cols[:, 2], cols[:, 3] = TRASH - P + row, TRASH + row
    cols[:, 4], cols[:, 6] = -0.5, -1.0
    cols[:, 5] = row % TILES != 0
    f32 = np.concatenate([dft, idft_low.reshape(P, -1), mask, eye, tie, cols], 1).astype(np.float32)
    f16 = np.concatenate([slot, eye, (row % TILES)[:, None], np.zeros((P, 1)), tri, np.ones((P, P))], 1).astype(np.float16)
    return f32, idft_high.reshape(rows, -1).astype(np.float32), f16


def build(nc, d, out, sizes):
    ctx = ExitStack()
    with ctx:
        def sb(name, shape, dt=F32):
            return ctx.enter_context(nc.sbuf_tensor(name, shape, dt))

        def sem(name):
            return ctx.enter_context(nc.semaphore(name))

        k = Kept()
        k.dve_chain, k.act_chain, k.pool_chain = sem("dve_chain"), sem("act_chain"), sem("pool_chain")
        k.table = nc.dram_tensor("code_table", [CODES, 2 * D], F32)
        k.token_rows = nc.dram_tensor("token_rows", [T, XW], F32)
        k.z = sb("z", [P, TILES * D])
        k.const = sb("const", [P, sizes["c_f32"]])
        k.idft_high = sb("idft_high", [4 * HIGH, 2, 2, P])
        k.c16 = sb("c16", [P, sizes["c_f16"]], F16)
        at = [0]

        def part(n):
            at[0] += n
            return k.const[:, at[0] - n:at[0]]

        k.dft = part(SPEC)
        k.idft_low = part(8 * P).rearrange("p (v t) -> p v t", v=8)
        k.mask = part(P)
        k.ident = part(P)
        k.tie = part(2 * NG * NG).rearrange("p (a g h) -> p a g h", a=2, g=NG)
        k.cols = part(8)
        k.slot_row, k.ident16, k.tile_col = k.c16[:, 0:CAP], k.c16[:, CAP:CAP + P], k.c16[:, CAP + P:CAP + P + 1]
        k.tri, k.ones = (k.c16[:, CAP + P + 2 + i * P:CAP + P + 2 + (i + 1) * P] for i in range(2))
        k.idx = sb("idx", [P, TILES], I32)
        k.alpha_raw = sb("alpha_raw", [P, 1])
        k.alpha = sb("alpha", [P, 1])
        k.low_T = sb("low_T", [P, DH, TILES * LOWC])
        k.att = sb("att", [P, GROUPS * D])
        k.counts = sb("counts", [P, 2 + E * TILES], F16)
        k.gather_idx = sb("gather_idx", [P, E, HALVES], I32)
        k.scatter_idx = sb("scatter_idx", [P, E, HALVES], I32)
        k.trash_zeroed, k.trash_stored, k.pool_waited = sem("trash_zeroed"), sem("trash_stored"), sem("pool_waited")
        k.b_loaded, k.c_loaded, k.d_loaded = sem("b_loaded"), sem("c_loaded"), sem("d_loaded")
        k.route = sb("route", [P, DH, E])
        k.shared = sb("shared", [P, DH, 2 * D])
        k.down = sb("down", [P, DH, D])
        k.bias = sb("bias", [P, E])
        k.o_w = k.counts[:, 0:NH * D].bitcast(F32).rearrange("p (c n) -> p c n", c=NH // 2)
        with Stage(nc, "bw") as bw:
            k.pw = bw.sb("pw", [P, 2, DH, D])
            k.gate_w = bw.sb("gate_w", [P, DH, D])
            k.dw = bw.sb("dw", [P, 2, DH, TAPS])
            stage_a(nc, d, k)
            with Stage(nc, "cw") as cw:
                k.q_w = cw.sb("q_w", [P, DH, NH * HD])
                k.k_w = cw.sb("k_w", [P, DH, NKV * 2 * HD])
                k.v_w = cw.sb("v_w", [P, DH, NKV * HD])
                stage_b(nc, d, k)
                stage_c(nc, d, k)
        stage_d(nc, d, k, out)
        stage_e(nc, d, k, out)


class Stage:

    def __init__(self, nc, tag):
        self.nc, self.tag, self.ctx = nc, tag, ExitStack()

    def __enter__(self):
        return self

    def __exit__(self, *a):
        return self.ctx.__exit__(*a)

    def sb(self, name, shape, dt=F32):
        return self.ctx.enter_context(self.nc.sbuf_tensor(f"{self.tag}_{name}", shape, dt))

    def bank(self, name, dt=F32):
        return self.ctx.enter_context(self.nc.psum_tensor(f"{self.tag}_ps_{name}", [P, 512], dt))

    def banks(self, name, n):
        return self.ctx.enter_context(self.nc.psum_tensor(f"{self.tag}_ps_{name}", [P, n, 512], F32))

    def sems(self, names):
        return [self.ctx.enter_context(self.nc.semaphore(f"{self.tag}_{n}")) for n in names.split()]

    def block(self):
        return self.ctx.enter_context(self.nc.Block())


def stage_a(nc, d, k):
    with Stage(nc, "a") as st:
        w1_loaded, w2_loaded, c_loaded = st.sems("w1_loaded w2_loaded c_loaded")
        codes_loaded = st.sems("codes0 codes1 codes2 codes3")
        row_stored = st.sems("row_stored0 row_stored1 row_stored2 row_stored3")
        w1_hi_ready, w1_split, w2_split, codes_split = st.sems("w1_hi_ready w1_split w2_split codes_split")
        stages = st.sems("up_done gelu_done hid_split down_done row_read var_ready rstd_ready row_ready")
        up_done, gelu_done, hid_split, down_done, row_read, var_ready, rstd_ready, row_ready = stages
        up = [st.bank(f"up{i}") for i in range(2)]
        down = [st.bank(f"down{i}") for i in range(2)]
        used = [0]

        def zpart(n):
            used[0] += n
            return k.z[:, used[0] - n:used[0]]

        codes_T = zpart(DH * CODES).rearrange("p (c n) -> p c n", c=DH)
        w1 = zpart(DH * HID).rearrange("p (c n) -> p c n", c=DH)
        w2 = zpart(HC * D).rearrange("p (c n) -> p c n", c=HC)
        hid = zpart(HC * 512).rearrange("p (c n) -> p c n", c=HC)
        b1, b2 = zpart(HC), zpart(D)
        rows = [zpart(2 * D) for _ in range(4)]
        stats = zpart(6)
        mv, veps, rstd = ([zpart(n) for _ in range(2)] for n in (2, 1, 1))
        codes_hi, codes_lo = (st.sb(f"codes_{n}", [P, DH, CODES], F32R) for n in ("hi", "lo"))
        w1_hi, w1_lo = (st.sb(f"w1_{n}", [P, DH, HID], F32R) for n in ("hi", "lo"))
        w2_hi, w2_lo = (st.sb(f"w2_{n}", [P, HC, D], F32R) for n in ("hi", "lo"))
        hid_hi, hid_lo = (st.sb(f"hid_{n}", [P, HC, 512], F32R) for n in ("hi", "lo"))
        block = st.block()

        @block.sync
        def _(sp):
            for s in stages:
                sp.sem_inc(s, CREDIT)
            codes = d["codes_T"].rearrange("(c p) n -> p c n", p=P)

            def load_codes(g):
                sp.dma_start(codes_T[:, :, g * 512:(g + 1) * 512], codes[:, :, g * 512:(g + 1) * 512]
                             ).then_inc(codes_loaded[g], 16)

            sp.dma_start(w1, d["tok_W1"].rearrange("(c p) n -> p c n", p=P)).then_inc(w1_loaded, 16)
            sp.dma_start(b1, d["tok_b1"]).then_inc(w1_loaded, 16)
            load_codes(0)
            sp.dma_start(w2, d["tok_W2"].rearrange("(c p) n -> p c n", p=P)).then_inc(w2_loaded, 16)
            sp.dma_start(b2, d["tok_b2"].partition_broadcast(P)).then_inc(w2_loaded, 16)
            for g in range(1, 4):
                load_codes(g)
            sp.dma_start(k.const[:, :], d["c_f32"]).then_inc(c_loaded, 16)
            sp.dma_start(k.idft_high[:, :, :, :], d["c_high"].rearrange("p (a b c) -> p a b c", a=2, b=2)
                         ).then_inc(c_loaded, 16)
            sp.dma_start(k.c16[:, :], d["c_f16"]).then_inc(c_loaded, 16)
            sp.dma_start(k.idx[:, :], d["x"]).then_inc(c_loaded, 16)
            sp.dma_start(k.alpha_raw[:, :], d["alpha_raw"].partition_broadcast(P)).then_inc(c_loaded, 16)
            sp.dma_start(k.pw[:, :, :, :], d["pw_T"].rearrange("r (c p) n -> p r c n", p=P)).then_inc(k.b_loaded, 16)
            sp.dma_start(k.gate_w[:, :, :], d["gate_wT"].rearrange("(c p) n -> p c n", p=P)).then_inc(k.b_loaded, 16)
            sp.dma_start(k.dw[:, :, :, :], d["dw"].rearrange("p (r c t) -> p r c t", r=2, c=DH)).then_inc(k.b_loaded, 16)
            for s in row_stored:
                sp.sem_inc(s, 16)
            with sp.Fori(0, 4) as g:
                for r in range(4):
                    sp.wait_ge(row_ready, done(g * 4 + r))
                    sp.dma_start(k.table[bass.ds(g * 512 + r * P, P), :], rows[r]).then_inc(row_stored[r], 16)
            for s in row_stored:
                sp.wait_ge(s, 16 * (CODES // P // 4 + 1))

        @block.tensor
        def _(pe):
            def body(g):
                for h in range(HC):
                    pe.wait_ge(gelu_done, done(g * HC + (h - 2)))
                    for n, (w, x) in enumerate(((w1_hi, codes_hi), (w1_lo, codes_hi), (w1_hi, codes_lo))):
                        for c in range(DH):
                            mm = nc.tensor.matmul(up[h % 2][:, :], w[:, c, h * P:(h + 1) * P],
                                                  x[:, c, bass.ds(g * 512, 512)], start=n == 0 and c == 0,
                                                  stop=n == 2 and c == DH - 1)
                    mm.then_inc(up_done, 1)
                for r in range(4):
                    if r == 0:
                        pe.wait_ge(hid_split, done(g * HC + (HC - 1)))
                        pe.wait_ge(w2_split, 2)
                    pe.wait_ge(row_read, done(g * 4 + (r - 2)))
                    for n, (x, w) in enumerate(((hid_hi, w2_hi), (hid_lo, w2_hi), (hid_hi, w2_lo))):
                        for h in range(HC):
                            mm = nc.tensor.matmul(down[r % 2][:, 0:D], x[:, h, r * P:(r + 1) * P], w[:, h, :],
                                                  start=n == 0 and h == 0, stop=n == 2 and h == HC - 1)
                    mm.then_inc(down_done, 1)

            pe.wait_ge(w1_split, 3)
            body(0)
            with pe.Fori(1, 4) as g:
                pe.wait_ge(codes_split, g * 2)
                body(g)

        @block.scalar
        def _(act):
            act.wait_ge(w1_loaded, 16 * 2)
            for c in range(DH):
                nc.scalar.activation(w1_hi[:, c, :], w1[:, c, :], ACT.Copy).then_inc(w1_hi_ready, 1)
            act.wait_ge(codes_loaded[0], 16)
            nc.scalar.activation(codes_hi[:, :, 0:512], codes_T[:, :, 0:512], ACT.Copy).then_inc(w1_hi_ready, 1)
            act.wait_ge(w2_loaded, 16 * 2)
            nc.scalar.activation(w2_hi[:, :, :], w2, ACT.Copy).then_inc(w2_split, 1)
            with act.Fori(0, 4) as g:
                for h in range(HC):
                    act.wait_ge(up_done, done(g * HC + h))
                    if h == 0:
                        act.wait_ge(down_done, done(g * 4 - 1))
                    nc.scalar.activation(hid[:, h, :], up[h % 2][:, :], ACT.Gelu_apprx_tanh,
                                         bias=b1[:, h:h + 1]).then_inc(gelu_done, 1)
            act.wait_ge(c_loaded, 16 * 5)
            nc.scalar.activation(k.alpha[:, 0:1], k.alpha_raw[:, :], ACT.Sigmoid)

        @block.gpsimd
        def _(pool):
            def split_codes(g):
                cols = slice(g * 512, (g + 1) * 512)
                pool.wait_ge(codes_loaded[g], 16)
                nc.gpsimd.tensor_copy(codes_hi[:, :, cols], codes_T[:, :, cols]).then_inc(codes_split, 1)
                pool.wait_ge(codes_split, 2 * g - 1)
                nc.gpsimd.tensor_tensor(codes_lo[:, :, cols], codes_T[:, :, cols], codes_hi[:, :, cols].bitcast(F32),
                                        ALU.subtract).then_inc(codes_split, 1)

            def factors(m, par):
                pool.wait_ge(var_ready, done(m))
                pool.sem_inc(k.pool_waited, 1)
                nc.gpsimd.tensor_tensor(rstd[par], veps[par], k.cols[:, 4:5], ALU.pow).then_inc(rstd_ready, 1)

            pool.wait_ge(w2_split, 1)
            nc.gpsimd.tensor_tensor(w2_lo[:, :, :], w2, w2_hi[:, :, :].bitcast(F32), ALU.subtract).then_inc(w2_split, 1)
            split_codes(1)
            pool.wait_ge(c_loaded, 16 * 5)
            for g in range(2):
                for r in range(4):
                    factors(g * 4 + r, r % 2)
                split_codes(g + 2)
            with pool.Fori(4, 8) as i:
                for par in range(2):
                    factors(2 * i + par, par)

        @block.vector
        def _(dve):
            ch = Chain(dve, k.dve_chain)
            def split_hidden(g, h):
                dve.wait_ge(gelu_done, done(g * HC + h))
                ch.link(nc.vector.tensor_copy(hid_hi[:, h, :], hid[:, h, :]))
                nc.vector.tensor_tensor(hid_lo[:, h, :], hid[:, h, :], hid_hi[:, h, :].bitcast(F32), ALU.subtract
                                        ).then_inc(hid_split, 1)

            def take(g, r):
                m, par = g * 4 + r, r % 2
                dve.wait_ge(down_done, done(m))
                dve.wait_ge(row_stored[r], g * 16 + 16)
                nc.vector.tensor_tensor(rows[r][:, D:2 * D], down[par][:, 0:D], b2, ALU.add).then_inc(row_read, 1)
                dve.wait_ge(row_read, done(m))
                ch.link(nc.vector.bn_stats(stats, rows[r][:, D:2 * D]))
                ch.link(nc.vector.bn_aggr(mv[par], stats))
                nc.vector.tensor_scalar(veps[par], mv[par][:, 1:2], 1e-5, None, ALU.add).then_inc(var_ready, 1)

            def finish(g, r):
                m, par, row = g * 4 + r, r % 2, rows[r]
                dve.wait_ge(rstd_ready, done(m))
                ch.link(nc.vector.tensor_scalar(row[:, 0:D], row[:, D:2 * D], mv[par][:, 0:1], rstd[par],
                                                ALU.subtract, ALU.mult))
                nc.vector.tensor_tensor(row[:, D:2 * D], row[:, 0:D], row[:, D:2 * D], ALU.add).then_inc(row_ready, 1)

            for c in range(DH):
                dve.wait_ge(w1_hi_ready, c + 1)
                nc.vector.tensor_tensor(w1_lo[:, c, :], w1[:, c, :], w1_hi[:, c, :].bitcast(F32), ALU.subtract
                                        ).then_inc(w1_split, 1)
            dve.wait_ge(w1_hi_ready, DH + 1)
            nc.vector.tensor_tensor(codes_lo[:, :, 0:512], codes_T[:, :, 0:512], codes_hi[:, :, 0:512].bitcast(F32),
                                    ALU.subtract).then_inc(w1_split, 1)
            dve.wait_ge(w2_loaded, 16 * 2)
            with dve.Fori(0, 4) as g:
                for h in range(HC):
                    split_hidden(g, h)
                for r in range(4):
                    take(g, r)
                    if r > 0:
                        finish(g, r - 1)
                finish(g, 3)
                ch.restart()


def stage_b(nc, d, k):
    with Stage(nc, "b") as st:
        pads_zeroed, started = st.sems("pads_zeroed started")
        rows_gathered = st.sems("rows_gathered0 rows_gathered1 rows_gathered2 rows_gathered3")
        idx_ready = st.sems("idx_ready")[0]
        stages = st.sems("kept dft_done gate_mm gate_turned mixed back_mm low_copied high_copied first_tap gate_ready gate_copied "
                         "gelu_done mixed_copied conv_done summed z_done")
        (kept, dft_done, gate_mm, gate_turned, mixed, back_mm, low_copied, high_copied, first_tap, gate_ready, gate_copied,
         gelu_done, mixed_copied, conv_done, summed, z_done) = stages
        pw, gate_w, dw = k.pw, k.gate_w, k.dw
        rows = [st.sb(f"rows{i}", [P, 2, 2 * D]) for i in range(4)]
        tile_idx = [st.sb(f"tile_idx{i}", [P, 2], I32) for i in range(4)]
        high = [st.sb(f"high{i}", [P, DH, 2, 2, 4, PAD + HIGH]) for i in range(2)]
        conv = [st.sb(f"conv{i}", [P, DH, 2, 8, HIGH]) for i in range(2)]
        act_in = [st.sb(f"gelu{i}", [P, DH, 2, 2, 4 * HIGH]) for i in range(2)]
        mix = [st.sb(f"mix{i}", [4 * HIGH, 2, D]) for i in range(2)]
        spread = st.sb("spread", [P, DH * 8, CHUNK])
        gate = [st.sb(f"gate{i}", [P, 2 * D]) for i in range(4)]
        total = [st.sb(f"total{i}", [P, 2 * D]) for i in range(4)]
        spec_ps = st.banks("spec", 2)
        gate_ps, turn_ps = st.bank("gate"), st.bank("turn")
        mix_ps, back_ps = st.banks("mix", 2), st.banks("back", 2)
        block = st.block()
        BATCHES, PAIRS = B, B // 2

        @block.sync
        def _(sp):
            for s in stages:
                sp.sem_inc(s, CREDIT)
            sp.sem_inc(started, 1)
            sp.wait_ge(dft_done, done(7))
            for w, name in ((k.q_w, "q_T"), (k.k_w, "k_T"), (k.v_w, "v_T"), (k.o_w, "o_T")):
                sp.dma_start(w[:, :, :], d[name].rearrange("(c p) n -> p c n", p=P)).then_inc(k.c_loaded, 16)

        @block.gpsimd
        def _(pool):
            def gather(s, slot):
                nc.gpsimd.tensor_copy(tile_idx[slot][:, :], k.idx[:, bass.ds(s * 2, 2)]).then_inc(idx_ready, 1)
                pool.wait_ge(idx_ready, s + 1)
                pool.sem_inc(k.pool_waited, 1)
                for t in range(2):
                    nc.gpsimd.indirect_dma_start(rows[slot][:, t, :], None, k.table[:, :],
                                                 bass.IndirectOffsetOnAxis(ap=tile_idx[slot][:, t:t + 1], axis=0),
                                                 bounds_check=CODES - 1).then_inc(rows_gathered[slot], 16)

            def z_add(s, c):
                pool.wait_ge(summed, done(s))
                pool.sem_inc(k.pool_waited, 1)
                nc.gpsimd.tensor_tensor(k.z[:, bass.ds(s * 2 * D, 2 * D)], k.z[:, bass.ds(s * 2 * D, 2 * D)],
                                        total[c % 4][:, :], ALU.add).then_inc(z_done, 1)

            def free_slot(s):
                pool.wait_ge(dft_done, done(s))
                pool.sem_inc(k.pool_waited, 1)
                pool.wait_ge(kept, done(s))
                pool.sem_inc(k.pool_waited, 1)

            pool.wait_ge(started, 1)
            for c in range(4):
                gather(c, c)
            for c in range(4):
                free_slot(c)
                gather(c + 4, c)
            with pool.Fori(0, BATCHES // 4 - 2) as i:
                for c in range(4):
                    free_slot(4 * i + (c + 4))
                    gather(4 * i + (c + 8), c)
                    z_add(4 * i + c, c)
            for s in range(BATCHES - 8, BATCHES):
                if s + 4 < BATCHES:
                    free_slot(s + 4)
                z_add(s, s)

        @block.tensor
        def _(pe):
            def spectrum(i, c):
                s, slot = 4 * i + c, c % 4
                pe.wait_ge(rows_gathered[slot], i * 32 + 32 * (c // 4 + 1))
                pe.wait_ge(high_copied, done(s - 1))
                for c in range(DH):
                    for t in range(2):
                        mm = nc.tensor.matmul(spec_ps[:, c, t * SPEC:(t + 1) * SPEC], rows[slot][:, t, c * P:(c + 1) * P], k.dft,
                                              start=True, stop=True)
                mm.then_inc(dft_done, 1)

            def gate_up(pair):
                pe.wait_ge(low_copied, done(2 * pair + 1))
                pe.wait_ge(gate_ready, done(pair - 1))
                for o in range(DH):
                    for c in range(DH):
                        mean = k.low_T[:, c, bass.ds(pair * 4 * LOWC, 4 * LOWC)].rearrange("p (q n) -> p q n", n=2 * LOW)[:, :, 0]
                        mm = nc.tensor.matmul(gate_ps[:, o * 8:(o + 1) * 8], gate_w[:, c, o * P:(o + 1) * P], mean,
                                              start=c == 0, stop=c == DH - 1)
                mm.then_inc(gate_mm, 1)

            def gate_turn(s, u, pair):
                pe.wait_ge(gate_ready, done(pair))
                pe.wait_ge(gate_copied, done(s - 1))
                for t in range(2):
                    for o in range(DH):
                        q = o * 8 + (u * 2 + t) * 2
                        mm = nc.tensor.transpose(turn_ps[:, t * D + o * P:t * D + (o + 1) * P],
                                                 spread[:, q:q + 2, :].rearrange("p a n -> p (a n)"), k.ident)
                mm.then_inc(gate_turned, 1)

            def mixing(s, u, pair, pair_par):
                if u == 0:
                    pe.wait_ge(gelu_done, done(pair))
                pe.wait_ge(mixed_copied, done(s - 2))
                for r in range(2):
                    for c in range(DH):
                        mm = nc.tensor.matmul(mix_ps[0:4 * HIGH, u, r * D:(r + 1) * D], act_in[pair_par][:, c, r, u, :],
                                              pw[:, r, c, :], start=c == 0, stop=c == DH - 1)
                mm.then_inc(mixed, 1)

            def inverse(s, u):
                pe.wait_ge(mixed_copied, done(s))
                pe.wait_ge(summed, done(s - 2))
                for t in range(2):
                    for r in range(2):
                        mm = nc.tensor.matmul(back_ps[:, u, t * D:(t + 1) * D], k.idft_high[:, r, t, :], mix[u][:, r, :],
                                              start=r == 0, stop=r == 1)
                mm.then_inc(back_mm, 1)

            def body(i, j, last=PAIRS):
                pair, s = 2 * i + j, 4 * i + 2 * j
                if last > 2:
                    spectrum(i, 2 * j + 4)
                mixing(s, 0, pair, j % 2)
                if last > 1:
                    gate_up(pair + 1)
                if last > 2:
                    spectrum(i, 2 * j + 5)
                mixing(s + 1, 1, pair, j % 2)
                if last > 1:
                    gate_turn(s + 2, 0, pair + 1)
                inverse(s, 0)
                if last > 1:
                    gate_turn(s + 3, 1, pair + 1)
                inverse(s + 1, 1)

            pe.wait_ge(started, 1)
            pe.wait_ge(k.b_loaded, 16 * 3)
            for c in range(4):
                spectrum(0, c)
            gate_up(0)
            for c in range(2):
                gate_turn(c, c, 0)
            rounds = PAIRS // 2 - 1
            with pe.Fori(0, rounds) as i:
                for j in range(2):
                    body(i, j)
            for j in range(2):
                body(rounds, j, last=2 - j)

        @block.scalar
        def _(act):
            def unpack(s, slot, u, pair, pair_par):
                act.wait_ge(dft_done, done(s))
                spec = spec_ps[:, :, 0:2 * SPEC].rearrange("p c (t n) -> p c t n", t=2)
                nc.scalar.activation(k.low_T[:, :, bass.ds(s * 2 * LOWC, 2 * LOWC)].rearrange("p c (t n) -> p c t n", t=2),
                                     spec[:, :, :, 0:LOWC], ACT.Copy).then_inc(low_copied, 1)
                act.wait_ge(conv_done, done(pair - 2))
                for c in range(DH):
                    for t in range(2):
                        ins = nc.scalar.activation(high[pair_par][:, c, :, u, 2 * t:2 * t + 2, PAD:],
                                                   spec[:, c, t, LOWC:].rearrange("p (r q l) -> p r q l", r=2, l=HIGH), ACT.Copy)
                ins.then_inc(high_copied, 1)
                nc.scalar.activation(k.z[:, bass.ds(s * 2 * D, 2 * D)].rearrange("p (t n) -> p t n", t=2),
                                     rows[slot][:, :, D:2 * D], ACT.Copy).then_inc(kept, 1)

            def tap0(s, pair, pair_par):
                act.wait_ge(high_copied, done(s))
                act.wait_ge(gelu_done, done(pair - 2))
                for c in range(DH):
                    for r in range(2):
                        last = nc.scalar.activation(conv[pair_par][:, c, r, :, :],
                                                    high[pair_par][:, c, r, :, :, 0:HIGH].rearrange("p u q l -> p (u q) l"),
                                                    ACT.Copy, scale=dw[:, r, c, 0:1])
                last.then_inc(first_tap, 1)

            def gate_fn(pair):
                act.wait_ge(gate_mm, done(pair))
                act.wait_ge(gate_turned, done(2 * pair - 1))
                nc.scalar.activation(spread[:, :, :], gate_ps[:, 0:DH * 8].unsqueeze(2).to_broadcast([P, DH * 8, CHUNK]),
                                     ACT.Tanh, scale=0.5 / CHUNK).then_inc(gate_ready, 1)

            def gate_copy(s, slot, first=False):
                act.wait_ge(gate_turned, done(s))
                if not first:
                    act.wait_ge(summed, done(s - 4))
                nc.scalar.activation(gate[slot][:, :], turn_ps[:, :], ACT.Copy).then_inc(gate_copied, 1)

            def gelu(pair, pair_par, first=False):
                act.wait_ge(conv_done, done(pair))
                if not first:
                    act.wait_ge(mixed, done(pair * 2 - 3))
                nc.scalar.activation(act_in[pair_par][:, :, :, :, :].rearrange("p c r u n -> p (c r u n)"),
                                     conv[pair_par][:, :, :, :, :].rearrange("p c r q l -> p (c r q l)"), ACT.Gelu
                                     ).then_inc(gelu_done, 1)

            def mix_copy(s, u):
                act.wait_ge(mixed, done(s))
                act.wait_ge(back_mm, done(s - 2))
                nc.scalar.activation(mix[u][:, :, :].rearrange("p r n -> p (r n)"), mix_ps[0:4 * HIGH, u, :],
                                     ACT.Copy).then_inc(mixed_copied, 1)

            def body(i, j, last=PAIRS):
                pair, s, nxt = 2 * i + j, 4 * i + 2 * j, (2 * j + 2) % 4
                if last > 2:
                    unpack(s + 4, 2 * j, 0, pair + 2, j % 2)
                mix_copy(s, 0)
                if last > 2:
                    unpack(s + 5, 2 * j + 1, 1, pair + 2, j % 2)
                if last > 1:
                    gate_fn(pair + 1)
                mix_copy(s + 1, 1)
                if last > 1:
                    gate_copy(s + 2, nxt)
                if last > 2:
                    tap0(s + 5, pair + 2, j % 2)
                if last > 1:
                    gate_copy(s + 3, nxt + 1)
                    gelu(pair + 1, (j + 1) % 2)

            act.wait_ge(started, 1)
            act.wait_ge(k.b_loaded, 16 * 3)
            act.wait_ge(pads_zeroed, 2)
            for pair in range(2):
                for u in range(2):
                    unpack(2 * pair + u, 2 * pair + u, u, pair, pair)
                tap0(2 * pair + 1, pair, pair)
            gate_fn(0)
            for c in range(2):
                gate_copy(c, c, first=True)
            gelu(0, 0, first=True)
            rounds = PAIRS // 2 - 1
            with act.Fori(0, rounds) as i:
                for j in range(2):
                    body(i, j)
            for j in range(2):
                body(rounds, j, last=2 - j)

        @block.vector
        def _(dve):
            ch = Chain(dve, k.dve_chain)

            def convolve(pair, par, marks, taps):
                if taps[0] == 1:
                    dve.wait_ge(first_tap, done(pair))
                for tap in taps:
                    for g in range(4):
                        c, r = divmod(g, 2)
                        if tap > 1:
                            ch.reach(marks[g])
                        acc = conv[par][:, c, r, :, :]
                        ins = nc.vector.scalar_tensor_tensor(
                            out=acc, in0=high[par][:, c, r, :, :, tap:tap + HIGH].rearrange("p u q l -> p (u q) l"),
                            scalar=dw[:, r, c, tap:tap + 1], in1=acc, op0=ALU.mult, op1=ALU.add)
                        if tap == TAPS - 1 and g == 3:
                            ins.then_inc(conv_done, 1)
                        else:
                            marks[g] = ch.mark(ins)

            def sum_up(s, slot):
                dve.wait_ge(back_mm, done(s))
                dve.wait_ge(gate_copied, done(s))
                if not (isinstance(s, int) and s < 4):
                    dve.wait_ge(z_done, done(s - 4))
                nc.vector.scalar_tensor_tensor(out=total[slot][:, :], in0=gate[slot][:, :], scalar=1.0,
                                               in1=back_ps[:, slot % 2, :], op0=ALU.add, op1=ALU.mult).then_inc(summed, 1)

            def body(i, j, last=PAIRS):
                pair, s, marks = 2 * i + j, 4 * i + 2 * j, [0] * 4
                if last > 1:
                    convolve(pair + 1, (j + 1) % 2, marks, (1, 2, 3))
                if not (isinstance(s, int) and s == 0):
                    sum_up(s - 1, (2 * j - 1) % 4)
                if last > 1:
                    convolve(pair + 1, (j + 1) % 2, marks, (4, 5, 6))
                sum_up(s, 2 * j % 4)

            for t in range(2):
                nc.vector.memset(high[t][:, :, :, :, :, 0:PAD].rearrange("p c r u q l -> p (c r u q) l"), 0.0
                                 ).then_inc(pads_zeroed, 1)
            dve.wait_ge(started, 1)
            dve.wait_ge(k.b_loaded, 16 * 3)
            convolve(0, 0, [0] * 4, range(1, TAPS))
            for j in range(2):
                body(0, j)
            ch.restart()
            rounds = PAIRS // 2 - 1
            with dve.Fori(1, rounds) as i:
                for j in range(2):
                    body(i, j)
                ch.restart()
            for j in range(2):
                body(rounds, j, last=2 - j)
            sum_up(BATCHES - 1, 3)
            ch.restart()


def stage_c(nc, d, k):
    with Stage(nc, "c") as st:
        started = st.sems("started")[0]
        stages = st.sems("rows_ready q_mm kv_mm q_copied kv_copied scores_mm biased max_ready exp_done normed turned "
                         "turned_act turned_dve values_mm values_act values_dve out_mm out_copied low_scaled")
        (rows_ready, q_mm, kv_mm, q_copied, kv_copied, scores_mm, biased, max_ready, exp_done, normed, turned,
         turned_act, turned_dve, values_mm, values_act, values_dve, out_mm, out_copied, low_scaled) = stages
        q_w, k_w, v_w, o_w = k.q_w, k.k_w, k.v_w, k.o_w
        rows = [st.sb(f"rows{i}", [P, DH, P]) for i in range(2)]
        qT = [st.sb(f"qT{i}", [P, NH // 2, P]) for i in range(2)]
        kT = [st.sb(f"kT{i}", [P, NKV, P]) for i in range(2)]
        v = [st.sb(f"v{i}", [P, NKV * HD]) for i in range(2)]
        prob = st.sb("prob", [P, 4, 4, P])
        probT = st.sb("probT", [P, 4, 4, P])
        top = st.sb("top", [P, 4, 4])
        shift = st.sb("shift", [P, 4, 4])
        rsum = st.sb("rsum", [P, 4, 4])
        rinv = st.sb("rinv", [P, 4, 4])
        vals = st.sb("vals", [P, NH // 2, P])
        low_rows = [st.sb(f"low_rows{i}", [P, D]) for i in range(2)]
        psA, psB = st.banks("A", 4), st.banks("B", 4)
        block = st.block()
        INV = 1.0 / float(np.sqrt(HD))

        @block.sync
        def _(sp):
            for s in stages:
                sp.sem_inc(s, CREDIT)
            sp.sem_inc(started, 1)
            for w, name in ((k.route, "route_T"), (k.shared, "shared_T"), (k.down, "down_T")):
                sp.dma_start(w[:, :, :], d[name].rearrange("(c p) n -> p c n", p=P)).then_inc(k.d_loaded, 16)
            sp.dma_start(k.bias[:, :], d["e_bias"].partition_broadcast(P)).then_inc(k.d_loaded, 16)

        @block.gpsimd
        def _(pool):
            pool.wait_ge(started, 1)
            with pool.Fori(0, GROUPS // 2) as i:
                for par in range(2):
                    g = 2 * i + par
                    pool.wait_ge(kv_mm, done(g - 2))
                    pool.sem_inc(k.pool_waited, 1)
                    nc.gpsimd.tensor_copy(rows[par][:, :, :], k.low_T[:, :, bass.ds(g * P, P)]).then_inc(rows_ready, 1)

        @block.tensor
        def _(pe):
            def q_product(g, par):
                pe.wait_ge(rows_ready, done(g))
                pe.wait_ge(values_act, done(g - 2))
                pe.wait_ge(values_dve, done(g - 2))
                for hp in range(NH // 2):
                    for c in range(DH):
                        mm = nc.tensor.matmul(psA[:, hp // 4, hp % 4 * P:(hp % 4 + 1) * P], q_w[:, c, hp * P:(hp + 1) * P],
                                              rows[par][:, c, :], start=c == 0, stop=c == DH - 1)
                mm.then_inc(q_mm, 1)

            def kv_products(g, par):
                pe.wait_ge(out_copied, done(g - 2))
                pe.wait_ge(low_scaled, done(g - 1))
                for j in range(NKV):
                    for c in range(DH):
                        nc.tensor.matmul(psA[:, 2, j * P:(j + 1) * P], k_w[:, c, j * P:(j + 1) * P], rows[par][:, c, :],
                                         start=c == 0, stop=c == DH - 1)
                for c in range(DH):
                    nc.tensor.matmul(psA[:, 3, 0:NKV * HD], rows[par][:, c, :], v_w[:, c, :], start=c == 0, stop=c == DH - 1)
                for c in range(DH):
                    mm = nc.tensor.transpose(psA[:, 3, NKV * HD + c * P:NKV * HD + (c + 1) * P], rows[par][:, c, :], k.ident)
                mm.then_inc(kv_mm, 1)

            def scores(g, par):
                pe.wait_ge(q_copied, done(g))
                pe.wait_ge(kv_copied, done(g))
                pe.wait_ge(turned_act, done(g - 1))
                pe.wait_ge(turned_dve, done(g - 1))
                for n in range(4):
                    jj, parity = divmod(n, 2)
                    for i in range(4):
                        h = 8 * jj + parity + 2 * i
                        half = slice(parity * HD, (parity + 1) * HD)
                        mm = nc.tensor.matmul(psB[:, n, i * P:(i + 1) * P], qT[par][half, h // 2, :], kT[par][half, h // 4, :],
                                              start=True, stop=True)
                    mm.then_inc(scores_mm, 1)

            def turn(g):
                for n in range(4):
                    pe.wait_ge(normed, done(g * 4 + n))
                    for i in range(4):
                        mm = nc.tensor.transpose(psB[:, n, i * P:(i + 1) * P], prob[:, n, i, :], k.ident)
                    mm.then_inc(turned, 1)

            def values(g, par, more):
                pe.wait_ge(turned_act, done(g))
                pe.wait_ge(turned_dve, done(g))
                if more:
                    pe.wait_ge(q_copied, done(g + 1))
                for jj in range(2):
                    for parity in range(2):
                        for half in range(2):
                            j = 2 * jj + half
                            mm = nc.tensor.matmul(psA[parity * HD:(parity + 1) * HD, jj, half * 2 * P:(half + 1) * 2 * P],
                                                  v[par][:, j * HD:(j + 1) * HD],
                                                  probT[:, 2 * jj + parity, 2 * half:2 * half + 2, :].rearrange("p i n -> p (i n)"),
                                                  start=True, stop=True)
                mm.then_inc(values_mm, 1)

            def out_product(g):
                pe.wait_ge(values_act, done(g))
                pe.wait_ge(values_dve, done(g))
                for hp in range(NH // 2):
                    mm = nc.tensor.matmul(psA[:, 2, 0:D], vals[:, hp, :], o_w[:, hp, :], start=hp == 0, stop=hp == NH // 2 - 1)
                mm.then_inc(out_mm, 1)

            def body(g, par, more=True):
                if more:
                    q_product(g + 1, 1 - par)
                turn(g)
                if more:
                    kv_products(g + 1, 1 - par)
                values(g, par, more)
                if more:
                    scores(g + 1, 1 - par)
                out_product(g)

            pe.wait_ge(started, 1)
            pe.wait_ge(k.c_loaded, 16 * 4)
            pe.wait_ge(rows_ready, done(0))
            for hp in range(NH // 2):
                for c in range(DH):
                    mm = nc.tensor.matmul(psA[:, hp // 4, hp % 4 * P:(hp % 4 + 1) * P], q_w[:, c, hp * P:(hp + 1) * P],
                                          rows[0][:, c, :], start=c == 0, stop=c == DH - 1)
            mm.then_inc(q_mm, 1)
            kv_products(0, 0)
            scores(0, 0)
            with pe.Fori(0, GROUPS // 2 - 1) as i:
                for par in range(2):
                    body(2 * i + par, par)
            body(GROUPS - 2, 0)
            body(GROUPS - 1, 1, more=False)

        @block.scalar
        def _(act):
            def q_copy(g, par):
                act.wait_ge(q_mm, done(g))
                nc.scalar.activation(qT[par][:, :, :].rearrange("p h n -> p (h n)"),
                                     psA[:, 0:2, :].rearrange("p a n -> p (a n)"), ACT.Copy).then_inc(q_copied, 1)

            def low_scale(g, par):
                act.wait_ge(kv_copied, done(g))
                act.wait_ge(out_copied, done(g - 2))
                nc.scalar.activation(low_rows[par][:, :], psA[:, 3, NKV * HD:], ACT.Copy, scale=k.alpha[:, 0:1]
                                     ).then_inc(low_scaled, 1)

            def exps(g):
                for n in range(4):
                    act.wait_ge(max_ready, done(g * 4 + n))
                    for i in range(4):
                        ins = nc.scalar.activation(prob[:, n, i, :], prob[:, n, i, :], ACT.Exp, scale=INV,
                                                   bias=shift[:, n, i:i + 1], accum_out=rsum[:, n, i:i + 1])
                    ins.then_inc(exp_done, 1)

            def body(g, par, more=True):
                if more:
                    q_copy(g + 1, 1 - par)
                for n in range(2):
                    act.wait_ge(turned, done(g * 4 + n))
                act.wait_ge(values_mm, done(g - 1))
                nc.scalar.activation(probT[:, 0:2, :, :].rearrange("p a i n -> p (a i n)"),
                                     psB[:, 0:2, :].rearrange("p a n -> p (a n)"), ACT.Copy).then_inc(turned_act, 1)
                if more:
                    low_scale(g + 1, 1 - par)
                act.wait_ge(values_mm, done(g))
                act.wait_ge(out_mm, done(g - 1))
                nc.scalar.activation(vals[:, 0:4, :].rearrange("p h n -> p (h n)"), psA[:, 0, :], ACT.Copy
                                     ).then_inc(values_act, 1)
                if more:
                    exps(g + 1)

            act.wait_ge(started, 1)
            q_copy(0, 0)
            act.wait_ge(kv_copied, done(0))
            nc.scalar.activation(low_rows[0][:, :], psA[:, 3, NKV * HD:], ACT.Copy, scale=k.alpha[:, 0:1]
                                 ).then_inc(low_scaled, 1)
            exps(0)
            with act.Fori(0, GROUPS // 2 - 1) as i:
                for par in range(2):
                    body(2 * i + par, par)
            body(GROUPS - 2, 0)
            body(GROUPS - 1, 1, more=False)

        @block.vector
        def _(dve):
            ch = Chain(dve, k.dve_chain)

            def kv_copy(g, par):
                dve.wait_ge(kv_mm, done(g))
                nc.vector.tensor_copy(kT[par][:, :, :].rearrange("p j n -> p (j n)"), psA[:, 2, :])
                nc.vector.tensor_copy(v[par][:, :], psA[:, 3, 0:NKV * HD]).then_inc(kv_copied, 1)

            def row_max(g):
                for n in range(4):
                    dve.wait_ge(scores_mm, done(g * 4 + n))
                    if n == 0:
                        dve.wait_ge(turned, done(g * 4 - 1))
                    ch.link(nc.vector.tensor_tensor(prob[:, n, :, :], psB[:, n, :].rearrange("p (i n) -> p i n", i=4),
                                                    k.mask.unsqueeze(1).to_broadcast([P, 4, P]), ALU.add))
                    ch.link(nc.vector.tensor_reduce(top[:, n, :], prob[:, n, :, :], AX, ALU.max))
                    nc.vector.tensor_scalar(shift[:, n, :], top[:, n, :], -INV, None, ALU.mult).then_inc(max_ready, 1)

            def normalise(g):
                for n in range(4):
                    dve.wait_ge(exp_done, done(g * 4 + n))
                    ch.link(nc.vector.reciprocal(rinv[:, n, :], rsum[:, n, :]))
                    nc.vector.tensor_tensor(prob[:, n, :, :], prob[:, n, :, :],
                                            rinv[:, n, :].unsqueeze(2).to_broadcast([P, 4, P]), ALU.mult
                                            ).then_inc(normed, 1)

            def body(g, par, more=True):
                normalise(g)
                for n in range(2, 4):
                    dve.wait_ge(turned, done(g * 4 + n))
                dve.wait_ge(values_mm, done(g - 1))
                nc.vector.tensor_copy(probT[:, 2:4, :, :].rearrange("p a i n -> p (a i n)"),
                                      psB[:, 2:4, :].rearrange("p a n -> p (a n)")).then_inc(turned_dve, 1)
                if more:
                    kv_copy(g + 1, 1 - par)
                dve.wait_ge(values_mm, done(g))
                dve.wait_ge(out_mm, done(g - 1))
                nc.vector.tensor_copy(vals[:, 4:8, :].rearrange("p h n -> p (h n)"), psA[:, 1, :]).then_inc(values_dve, 1)
                if more:
                    row_max(g + 1)
                dve.wait_ge(out_mm, done(g))
                dve.wait_ge(low_scaled, done(g))
                nc.vector.scalar_tensor_tensor(out=k.att[:, bass.ds(g * D, D)], in0=psA[:, 2, 0:D], scalar=k.alpha[:, 0:1],
                                               in1=low_rows[par][:, :], op0=ALU.mult, op1=ALU.subtract).then_inc(out_copied, 1)

            dve.wait_ge(started, 1)
            kv_copy(0, 0)
            row_max(0)
            ch.restart()
            with dve.Fori(0, GROUPS // 2 - 1) as i:
                for par in range(2):
                    body(2 * i + par, par)
                ch.restart()
            body(GROUPS - 2, 0)
            body(GROUPS - 1, 1, more=False)
            ch.restart()


def stage_d(nc, d, k, out):
    QT = 4
    STEPS = TILES // QT
    QE = QT * E
    ROUND = 4
    ROUNDS = STEPS // ROUND
    with Stage(nc, "d") as st:
        counts_zeroed, started = st.sems("counts_zeroed started")
        rows_stored = st.sems("rows_stored0 rows_stored1 rows_stored2 rows_stored3")
        out_stored = st.sems("out_stored0 out_stored1")
        stages = st.sems("low_mm h_ready var_ready rstd_ready x_ready turned xT_ready hi_ready route_mm scores_ready chosen counts_mm "
                         "counted total_ready up_mm silu_done hidden_ready down_mm out_ready rows_ready pow_done split_done weights_split weighted")
        (low_mm, h_ready, var_ready, rstd_ready, x_ready, turned, xT_ready, hi_ready, route_mm, scores_ready, chosen, counts_mm,
         counted, total_ready, up_mm, silu_done, hidden_ready, down_mm, out_ready, rows_ready, pow_done,
         split_done, weights_split, weighted) = stages
        zeros = st.sb("zeros", [P, HALVES * D])[:, :]
        route, shared, down, bias = k.route, k.shared, k.down, k.bias
        h = [st.sb(f"h{i}", [P, QT, D]) for i in range(ROUND)]
        x = [st.sb(f"x{i}", [P, QT, XW]) for i in range(ROUND)]
        xT = [st.sb(f"xT{i}", [P, DH, QT * P]) for i in range(2)]
        xT_hi = [st.sb(f"xT_hi{i}", [P, DH, QT * P], F32R) for i in range(2)]
        xT_lo = [st.sb(f"xT_lo{i}", [P, DH, QT * P], F32R) for i in range(2)]
        shared_hi, shared_lo = (st.sb(f"shared_{n}", [P, DH, 2 * D], F32R) for n in ("hi", "lo"))
        stats = st.sb("stats", [P, QT, 6])
        mv = st.sb("mv", [P, QT, 2])
        veps = st.sb("veps", [P, QT])
        rstd = st.sb("rstd", [P, QT])
        shift = st.sb("shift", [P, QT])
        neg_mean = st.sb("neg_mean", [P, QT])
        scores = [st.sb(f"scores{i}", [P, QE]) for i in range(2)]
        biased = st.sb("biased", [P, QE])
        m1, n1 = st.sb("m1", [P, QT * NG * 4]), st.sb("n1", [P, QT * NG * 4])
        m2, n2, l2 = (st.sb(n, [P, QT * NG * 2]) for n in ("m2", "n2", "l2"))
        m3, n3, l3 = (st.sb(n, [P, QT * NG]) for n in ("m3", "n3", "l3"))
        ge, gt = st.sb("ge", [P, QT, NG * NG]), st.sb("gt", [P, QT, NG * NG])
        best = st.sb("best", [P, QT, 8])
        taken = st.sb("taken", [P, QE])
        sel = st.sb("sel", [P, QE], F16)
        before = st.sb("before", [P, E], F16)
        wsum, winv = st.sb("wsum", [P, QT]), st.sb("winv", [P, QT])
        silu_table = st.sb("silu_table", [P, 1])
        silu = [st.sb(f"silu{i}", [P, QT * P]) for i in range(2)]
        hidden = [st.sb(f"hidden{i}", [P, 2, QT * P]) for i in range(2)]
        res = [st.sb(f"res{i}", [P, QT, D]) for i in range(2)]
        low_ps, x_ps = st.banks("low", 2), st.banks("x", 2)
        route_ps, count_ps = st.bank("route"), st.bank("count")
        gate_ps, up_ps = st.bank("gate"), st.bank("up")
        block = st.block()

        @block.sync
        def _(sp):
            for s in stages:
                sp.sem_inc(s, CREDIT)
            for s in rows_stored + out_stored:
                sp.sem_inc(s, 16)
            sp.sem_inc(started, 1)
            with sp.Fori(0, ROUNDS) as i:
                for c in range(ROUND):
                    s, par = ROUND * i + c, c % 2
                    sp.wait_ge(rows_ready, done(s))
                    sp.wait_ge(x_ready, done(s))
                    sp.dma_start(k.token_rows[bass.ds(s * QT * P, QT * P), :].rearrange("(t p) n -> p t n", p=P),
                                 x[c][:, :, :]).then_inc(rows_stored[c], 16)
                    sp.wait_ge(out_ready, done(s))
                    sp.dma_start(out[bass.ds(s * QT * P, QT * P), :].rearrange("(t p) n -> p t n", p=P),
                                 res[par][:, :, :]).then_inc(out_stored[par], 16)
            for s in rows_stored:
                sp.wait_ge(s, 16 * (ROUNDS + 1))
            for s in out_stored:
                sp.wait_ge(s, 16 * (STEPS // 2 + 1))

        @block.gpsimd
        def _(pool):
            pool.wait_ge(started, 1)
            pool.wait_ge(k.trash_zeroed, 1)
            pool.dma_start(out[T:T + CAP, :].rearrange("(t p) n -> p t n", p=P),
                           zeros.rearrange("p (t n) -> p t n", t=HALVES)).then_inc(k.trash_stored, 16)
            def norm_factors(s):
                pool.wait_ge(var_ready, done(s))
                pool.sem_inc(k.pool_waited, 1)
                pool.wait_ge(x_ready, done(s - 1))
                pool.sem_inc(k.pool_waited, 1)
                ch.link(nc.gpsimd.tensor_scalar(veps[:, :], mv[:, :, 1], 1e-5, None, ALU.add))
                nc.gpsimd.tensor_tensor(rstd[:, :], veps[:, :], k.cols[:, 4:5].to_broadcast([P, QT]), ALU.pow
                                        ).then_inc(pow_done, 1)
                ch.link(nc.gpsimd.tensor_scalar(neg_mean[:, :], mv[:, :, 0], -1.0, None, ALU.mult))
                pool.wait_ge(pow_done, done(s))
                pool.sem_inc(k.pool_waited, 1)
                nc.gpsimd.tensor_tensor(shift[:, :], neg_mean[:, :], rstd[:, :], ALU.mult).then_inc(rstd_ready, 1)

            def split_x(s, par):
                pool.wait_ge(hi_ready, done(s))
                pool.sem_inc(k.pool_waited, 1)
                pool.wait_ge(up_mm, done(2 * s - 3))
                pool.sem_inc(k.pool_waited, 1)
                nc.gpsimd.tensor_tensor(xT_lo[par][:, :, :].rearrange("p c n -> p (c n)"),
                                        xT[par][:, :, :].rearrange("p c n -> p (c n)"),
                                        xT_hi[par][:, :, :].bitcast(F32).rearrange("p c n -> p (c n)"),
                                        ALU.subtract).then_inc(split_done, 1)

            def weights(s, slot):
                w = x[slot][:, :, D:XW]
                pool.wait_ge(weighted, done(s))
                pool.sem_inc(k.pool_waited, 1)
                ch.link(nc.gpsimd.tensor_scalar(wsum[:, :], wsum[:, :], 1e-20, None, ALU.add))
                ch.link(nc.gpsimd.tensor_scalar(w, w, SCALE, None, ALU.mult))
                ch.link(nc.gpsimd.tensor_tensor(winv[:, :], wsum[:, :], k.cols[:, 6:7].to_broadcast([P, QT]), ALU.pow))
                nc.gpsimd.tensor_tensor(w, w, winv[:, :].unsqueeze(2).to_broadcast([P, QT, E]), ALU.mult).then_inc(rows_ready, 1)

            def totals(s):
                pool.wait_ge(chosen, done(s))
                pool.sem_inc(k.pool_waited, 1)
                pool.wait_ge(counts_mm, done(s))
                pool.sem_inc(k.pool_waited, 1)
                for t in range(QT - 1):
                    ch.link(nc.gpsimd.tensor_tensor(before[:, :], before[:, :], sel[:, t * E:(t + 1) * E], ALU.add))
                nc.gpsimd.tensor_tensor(before[:, :], before[:, :], sel[:, (QT - 1) * E:QT * E], ALU.add).then_inc(total_ready, 1)

            ch = Chain(pool, k.pool_chain)
            norm_factors(0)
            norm_factors(1)
            split_x(0, 0)
            pool.wait_ge(counts_zeroed, 2)
            ch.restart()
            with pool.Fori(0, ROUNDS - 1) as i:
                for c in range(ROUND):
                    s = ROUND * i + c
                    norm_factors(s + 2)
                    split_x(s + 1, (c + 1) % 2)
                    totals(s)
                    weights(s, c)
                ch.restart()
            for c in range(ROUND):
                s = STEPS - ROUND + c
                if c < ROUND - 2:
                    norm_factors(s + 2)
                if c < ROUND - 1:
                    split_x(s + 1, (c + 1) % 2)
                totals(s)
                weights(s, c)
            ch.restart()
            pool.wait_ge(k.trash_stored, 16)

        @block.tensor
        def _(pe):
            def low_bins(i, c):
                s = ROUND * i + c
                pe.wait_ge(h_ready, done(s - 1))
                for t in range(QT):
                    mm = nc.tensor.matmul(low_ps[:, t // 2, t % 2 * D:(t % 2 + 1) * D], k.idft_low[:, QT * (c % 2) + t, :],
                                          k.att[:, bass.ds((2 * i + c // 2) * D, D)], start=True, stop=True)
                mm.then_inc(low_mm, 1)

            def turn(s, slot):
                pe.wait_ge(x_ready, done(s))
                pe.wait_ge(out_ready, done(s - 2))
                for t in range(QT):
                    for c in range(DH):
                        mm = nc.tensor.transpose(x_ps[:, c, t * P:(t + 1) * P], x[slot][:, t, c * P:(c + 1) * P], k.ident)
                mm.then_inc(turned, 1)

            def routing(s, par):
                pe.wait_ge(xT_ready, done(s))
                pe.wait_ge(scores_ready, done(s - 1))
                for t in range(QT):
                    for c in range(DH):
                        mm = nc.tensor.matmul(route_ps[:, t * E:(t + 1) * E], xT[par][:, c, t * P:(t + 1) * P], route[:, c, :],
                                              start=c == 0, stop=c == DH - 1)
                mm.then_inc(route_mm, 1)

            def up(s, par, f):
                pe.wait_ge(hidden_ready, done(s * 2 + (f - 1)))
                if f == 0:
                    pe.wait_ge(hi_ready, done(s))
                parts = ((shared_hi, xT_hi[par]), (shared_lo, xT_hi[par]), (shared_hi, xT_lo[par]))
                for ps, o in ((gate_ps, 0), (up_ps, D)):
                    for n, (w, moving) in enumerate(parts):
                        if f == 0 and o == 0 and n == 2:
                            pe.wait_ge(split_done, done(s))
                        for c in range(DH):
                            mm = nc.tensor.matmul(ps[:, :], w[:, c, o + f * P:o + (f + 1) * P], moving[:, c, :],
                                                  start=n == 0 and c == 0, stop=n == 2 and c == DH - 1)
                mm.then_inc(up_mm, 1)

            def down_product(s, par, tiles, turned_later=1):
                if tiles[0] == 0:
                    pe.wait_ge(hidden_ready, done(s * 2 + 1))
                    pe.wait_ge(hi_ready, done(s + turned_later))
                for t in tiles:
                    for f in range(2):
                        mm = nc.tensor.matmul(x_ps[:, t // 2, t % 2 * D:(t % 2 + 1) * D], hidden[par][:, f, t * P:(t + 1) * P],
                                              down[:, f, :], start=f == 0, stop=f == 1)
                if tiles[-1] == QT - 1:
                    mm.then_inc(down_mm, 1)

            def count(s):
                pe.wait_ge(chosen, done(s))
                pe.wait_ge(total_ready, done(s - 1))
                pe.wait_ge(counted, done(s - 1))
                for t in range(QT):
                    to = count_ps[:, t * E:(t + 1) * E]
                    nc.tensor.matmul(to, k.ones, before[:, :], start=True, stop=False)
                    for u in range(t):
                        nc.tensor.matmul(to, k.ones, sel[:, u * E:(u + 1) * E], start=False, stop=False)
                    mm = nc.tensor.matmul(to, k.tri, sel[:, t * E:(t + 1) * E], start=False, stop=True)
                mm.then_inc(counts_mm, 1)

            def body(i, c, left=STEPS):
                s, par, nxt = ROUND * i + c, c % 2, (c + 1) % 2
                up(s, par, 1)
                if left > 1:
                    turn(s + 1, (c + 1) % ROUND)
                if left > 3:
                    low_bins(i, c + 3)
                if left > 1:
                    routing(s + 1, nxt)
                down_product(s, par, (0, 1), turned_later=min(1, left - 1))
                if left > 1:
                    up(s + 1, nxt, 0)
                down_product(s, par, (2, 3))
                count(s)

            pe.wait_ge(started, 1)
            pe.wait_ge(k.d_loaded, 16 * 4)
            low_bins(0, 0)
            low_bins(0, 1)
            turn(0, 0)
            routing(0, 0)
            pe.wait_ge(weights_split, 2 + CREDIT)
            up(0, 0, 0)
            pe.wait_ge(counts_zeroed, 2)
            low_bins(0, 2)
            with pe.Fori(0, ROUNDS - 1) as i:
                for c in range(ROUND):
                    body(i, c)
            for c in range(ROUND):
                body(ROUNDS - 1, c, left=ROUND - c)

        @block.scalar
        def _(act):
            def normalise(i, c):
                s, slot = ROUND * i + c, c % ROUND
                act.wait_ge(rstd_ready, done(s))
                act.wait_ge(rows_stored[slot], 16 * i + 16 * (c // ROUND + 1))
                for t in range(QT):
                    ins = nc.scalar.activation(x[slot][:, t, 0:D], h[slot][:, t, :], ACT.Identity, scale=rstd[:, t:t + 1],
                                               bias=shift[:, t:t + 1])
                ins.then_inc(x_ready, 1)

            def turn_copy(s, par):
                act.wait_ge(turned, done(s))
                act.wait_ge(up_mm, done(2 * s - 3))
                for to, ready in ((xT[par], xT_ready), (xT_hi[par], hi_ready)):
                    nc.scalar.activation(to[:, :, :].rearrange("p c n -> p (c n)"),
                                         x_ps[:, :, :].rearrange("p c n -> p (c n)"), ACT.Copy).then_inc(ready, 1)

            def score(s, par):
                act.wait_ge(route_mm, done(s))
                act.wait_ge(rows_ready, done(s - 2))
                nc.scalar.activation(scores[par][:, :], route_ps[:, 0:QE], ACT.Sigmoid).then_inc(scores_ready, 1)
                nc.scalar.activation(silu_table[:, :], k.cols[:, 4:5], ACT.Silu)

            def silu_fn(s, f):
                act.wait_ge(up_mm, done(s * 2 + f))
                act.wait_ge(hidden_ready, done(s * 2 + (f - 2)))
                nc.scalar.activation(silu[f][:, :], gate_ps[:, :], ACT.Silu).then_inc(silu_done, 1)

            def body(i, c, left=STEPS):
                s, nxt = ROUND * i + c, (c + 1) % 2
                silu_fn(s, 1)
                if left > 1:
                    turn_copy(s + 1, nxt)
                if left > 2:
                    normalise(i, c + 2)
                if left > 1:
                    score(s + 1, nxt)
                    silu_fn(s + 1, 0)

            act.wait_ge(started, 1)
            normalise(0, 0)
            act.wait_ge(turned, done(0))
            for to, ready in ((xT[0], xT_ready), (xT_hi[0], hi_ready)):
                nc.scalar.activation(to[:, :, :].rearrange("p c n -> p (c n)"),
                                     x_ps[:, :, :].rearrange("p c n -> p (c n)"), ACT.Copy).then_inc(ready, 1)
            score(0, 0)
            normalise(0, 1)
            silu_fn(0, 0)
            with act.Fori(0, ROUNDS - 1) as i:
                for c in range(ROUND):
                    body(i, c)
            for c in range(ROUND):
                body(ROUNDS - 1, c, left=ROUND - c)

        @block.vector
        def _(dve):
            ch = Chain(dve, k.dve_chain)

            def tt(o, a, b, op):
                return nc.vector.tensor_tensor(o, a, b, op)

            def token_norm(s, slot):
                dve.wait_ge(low_mm, done(s))
                dve.wait_ge(rstd_ready, done(s - 1))
                for b in range(2):
                    ch.mark(tt(h[slot][:, 2 * b:2 * b + 2, :].rearrange("p t n -> p (t n)"), low_ps[:, b, :],
                               k.z[:, bass.ds(s * QT * D + b * 2 * D, 2 * D)], ALU.add))
                ch.reach(ch.n)
                for t in range(QT):
                    ins = nc.vector.bn_stats(stats[:, t, :], h[slot][:, t, :])
                    if t == 0:
                        ins.then_inc(h_ready, 1)
                    else:
                        ch.mark(ins)
                ch.reach(ch.n)
                for t in range(QT):
                    ins = nc.vector.bn_aggr(mv[:, t, :], stats[:, t, :])
                ins.then_inc(var_ready, 1)

            def rank_groups(s, par):
                dve.wait_ge(scores_ready, done(s))
                ch.link(tt(biased[:, :].rearrange("p (t e) -> p t e", t=QT), scores[par][:, :].rearrange("p (t e) -> p t e", t=QT),
                           bias[:, :].unsqueeze(1).to_broadcast([P, QT, E]), ALU.add))
                v = biased[:, :].rearrange("p (g a) -> p g a", a=2)
                ch.mark(tt(m1[:, :], v[:, :, 0], v[:, :, 1], ALU.max))
                ch.link(tt(n1[:, :], v[:, :, 0], v[:, :, 1], ALU.min))
                for (m, n), (mo, no, lo) in (((m1, n1), (m2, n2, l2)), ((m2, n2), (m3, n3, l3))):
                    mm, nn = (q[:, :].rearrange("p (g a) -> p g a", a=2) for q in (m, n))
                    ch.mark(tt(mo[:, :], mm[:, :, 0], mm[:, :, 1], ALU.max))
                    ch.mark(tt(lo[:, :], mm[:, :, 0], mm[:, :, 1], ALU.min))
                    ch.link(tt(no[:, :], nn[:, :, 0], nn[:, :, 1], ALU.max))
                    ch.link(tt(no[:, :], no[:, :], lo[:, :], ALU.max))
                ch.link(tt(m3[:, :], m3[:, :], n3[:, :], ALU.add))
                gs = m3[:, :].rearrange("p (t g) -> p t g", t=QT)
                other = gs.unsqueeze(2).to_broadcast([P, QT, NG, NG])
                own = gs.unsqueeze(3).to_broadcast([P, QT, NG, NG])
                ch.mark(tt(ge[:, :, :].rearrange("p t (g o) -> p t g o", g=NG), other, own, ALU.is_ge))
                ch.mark(tt(gt[:, :, :].rearrange("p t (g o) -> p t g o", g=NG), other, own, ALU.is_gt))
                ch.reach(ch.n)
                for q, a in ((ge, 0), (gt, 1)):
                    ch.mark(tt(q[:, :, :], q[:, :, :], k.tie[:, a, :, :].rearrange("p g o -> p (g o)").unsqueeze(1)
                               .to_broadcast([P, QT, NG * NG]), ALU.mult))
                ch.reach(ch.n)
                ch.link(tt(ge[:, :, :], ge[:, :, :], gt[:, :, :], ALU.add))
                ch.mark(nc.vector.tensor_reduce(l3[:, :], ge[:, :, :].rearrange("p t (g o) -> p (t g) o", g=NG), AX, ALU.add))

            def choose(s):
                ch.reach(ch.n)
                ch.link(nc.vector.scalar_tensor_tensor(
                    out=biased[:, :].rearrange("p (g e) -> p g e", e=E // NG),
                    in0=l3[:, :].unsqueeze(2).to_broadcast([P, QT * NG, E // NG]), scalar=float(TG),
                    in1=biased[:, :].rearrange("p (g e) -> p g e", e=E // NG), op0=ALU.is_lt, op1=ALU.mult))
                for t in range(QT):
                    ch.mark(nc.vector.max(best[:, t, :], biased[:, t * E:(t + 1) * E]))
                ch.reach(ch.n)
                for t in range(QT):
                    ch.mark(nc.vector.match_replace(taken[:, t * E:(t + 1) * E], best[:, t, :],
                                                    biased[:, t * E:(t + 1) * E], NEG))
                ch.reach(ch.n)
                dve.wait_ge(counts_mm, done(s - 1))
                dve.wait_ge(total_ready, done(s - 1))
                tt(sel[:, :], taken[:, :], biased[:, :], ALU.not_equal).then_inc(chosen, 1)

            def weigh(s, slot, par):
                w = x[slot][:, :, D:XW]
                dve.wait_ge(chosen, done(s))
                ch.link(tt(w, scores[par][:, :].rearrange("p (t e) -> p t e", t=QT), sel[:, :].rearrange("p (t e) -> p t e", t=QT),
                           ALU.mult))
                dve.wait_ge(rows_ready, done(s - 1))
                nc.vector.tensor_reduce(wsum[:, :], w, AX, ALU.add).then_inc(weighted, 1)

            def act_mul(s, par, f):
                dve.wait_ge(silu_done, done(s * 2 + f))
                dve.wait_ge(down_mm, done(s - 2))
                tt(hidden[par][:, f, :], up_ps[:, :], silu[f][:, :], ALU.mult).then_inc(hidden_ready, 1)

            def result(i, c):
                s, par = ROUND * i + c, c % 2
                dve.wait_ge(down_mm, done(s))
                dve.wait_ge(out_stored[par], 32 * i + 16 * (c // 2 + 1))
                for b in range(2):
                    ins = tt(res[par][:, 2 * b:2 * b + 2, :].rearrange("p t n -> p (t n)"), x_ps[:, b, :],
                             h[c][:, 2 * b:2 * b + 2, :].rearrange("p t n -> p (t n)"), ALU.add)
                ins.then_inc(out_ready, 1)

            def count(s):
                dve.wait_ge(counts_mm, done(s))
                to = k.counts[:, 1:1 + E * TILES].rearrange("p (e t) -> p t e", e=E)[:, bass.ds(s * QT, QT), :]
                nc.vector.tensor_scalar(to, count_ps[:, 0:QE].rearrange("p (t e) -> p t e", t=QT), COUNT_MAX, None, ALU.min
                                        ).then_inc(counted, 1)

            ch.link(nc.vector.memset(zeros, 0.0))
            nc.vector.memset(before[:, :], 0.0).then_inc(counts_zeroed, 1)
            nc.vector.memset(k.counts[:, 0:1], 0.0).then_inc(counts_zeroed, 1)
            nc.vector.memset(l3[:, :], 0.0).then_inc(k.trash_zeroed, 1)
            ch.restart()
            dve.wait_ge(started, 1)
            dve.wait_ge(k.d_loaded, 16 * 4)
            def body(i, c, left=STEPS):
                s, par = ROUND * i + c, c % 2
                if left > 2:
                    token_norm(s + 2, (c + 2) % ROUND)
                act_mul(s, par, 1)
                rank_groups(s, par)
                choose(s)
                if left > 1:
                    act_mul(s + 1, 1 - par, 0)
                weigh(s, c, par)
                result(i, c)
                count(s)

            token_norm(0, 0)
            flat = [q[:, :, :].rearrange("p c n -> p (c n)") for q in (shared, shared_hi, shared_lo)]
            nc.vector.tensor_copy(flat[1], flat[0]).then_inc(weights_split, 1)
            dve.wait_ge(weights_split, 1 + CREDIT)
            tt(flat[2], flat[0], shared_hi[:, :, :].bitcast(F32).rearrange("p c n -> p (c n)"), ALU.subtract
               ).then_inc(weights_split, 1)
            token_norm(1, 1)
            act_mul(0, 0, 0)
            ch.restart()
            with dve.Fori(0, ROUNDS - 1) as i:
                for c in range(ROUND):
                    body(i, c)
                ch.restart()
            for c in range(ROUND):
                body(ROUNDS - 1, c, left=ROUND - c)
            ch.restart()


def stage_e(nc, d, k, out):
    PAIRS, LEAD, AHEAD, ROUND = E // 2, 4, 3, 4
    LOOPS = (PAIRS - LEAD) // 2
    with Stage(nc, "e") as st:
        w_loaded = st.sems("w_loaded0 w_loaded1 w_loaded2 w_loaded3")
        gathered = st.sems("gathered0 gathered1 gathered2 gathered3")
        added = st.sems("added0 added1")
        stages = st.sems("indices_ready gi_ready counts_mm counts_copied bounds_ready tile_found picked compared turned xT_ready "
                         "gate_mm up_mm gate_ready hidden_ready down_mm weights_ready scaled")
        (indices_ready, gi_ready, counts_mm, counts_copied, bounds_ready, tile_found, picked, compared, turned, xT_ready,
         gate_mm, up_mm, gate_ready, hidden_ready, down_mm, weights_ready, scaled) = stages
        cts = st.sb("cts", [P, P], F16)
        bounds = st.sb("bounds", [P, 2])
        hot = st.sb("hot", [P, CAP], F16)
        below = st.sb("below", [P, 2, HALVES, P])
        fine = st.sb("fine", [P, 2 * HALVES])
        token = st.sb("token", [P, 2 * HALVES])
        empty = st.sb("empty", [P, 2 * HALVES])
        w = [st.sb(f"w{i}", [P, 3 * D]) for i in range(ROUND)]
        x = [st.sb(f"x{i}", [P, HALVES, XW]) for i in range(ROUND)]
        gi = [st.sb(f"gi{i}", [P, HALVES], I32) for i in range(ROUND)]
        si = [st.sb(f"si{i}", [P, HALVES], I32) for i in range(ROUND)]
        xT = [st.sb(f"xT{i}", [P, DH, CAP]) for i in range(2)]
        gate = [st.sb(f"gate{i}", [P, CAP]) for i in range(2)]
        hidden = [st.sb(f"hidden{i}", [P, CAP]) for i in range(2)]
        wcol = [st.sb(f"wcol{i}", [P, HALVES]) for i in range(2)]
        y = [st.sb(f"y{i}", [P, HALVES, D]) for i in range(2)]
        x_ps = [st.bank(f"x{i}") for i in range(2)]
        gate_ps, up_ps, down_ps, col_ps = (st.bank(n) for n in ("gate", "up", "down", "col"))
        pick_ps = st.banks("pick", 2)
        block = st.block()

        def seen(s_sems, i, c):
            return s_sems[c % ROUND], 32 * i + 32 * (c // ROUND + 1)

        @block.sync
        def _(sp):
            for s in stages:
                sp.sem_inc(s, CREDIT)

            def load(i, c):
                sp.dma_start(w[c][:, :], d["experts"][bass.ds(ROUND * i + c, 1), :, :].rearrange("a p n -> p (a n)")
                             ).then_inc(w_loaded[c], 16)

            for c in range(ROUND):
                load(0, c)
            with sp.Fori(1, E // ROUND) as i:
                for c in range(ROUND):
                    sp.wait_ge(down_mm, done(ROUND * i + (c - ROUND)))
                    load(i, c)

        @block.gpsimd
        def _(pool):
            def gather(i, c):
                s, slot = ROUND * i + c, c % ROUND
                pool.wait_ge(gi_ready, done(s))
                pool.sem_inc(k.pool_waited, 1)
                if not (isinstance(s, int) and s < ROUND):
                    pool.wait_ge(turned, done(s - ROUND))
                    pool.sem_inc(k.pool_waited, 1)
                for hf in range(HALVES):
                    nc.gpsimd.indirect_dma_start(x[slot][:, hf, :], None, k.token_rows[:, :],
                                                 bass.IndirectOffsetOnAxis(ap=gi[slot][:, hf:hf + 1], axis=0),
                                                 bounds_check=T - 1).then_inc(gathered[slot], 16)

            def add(i, c):
                s, par = ROUND * i + c, c % 2
                pool.wait_ge(scaled, done(s))
                pool.sem_inc(k.pool_waited, 1)
                if not (isinstance(s, int) and s == 0):
                    pool.wait_ge(added[1 - par], 64 * i + 32 * ((c + 1) // 2))
                    pool.sem_inc(k.pool_waited, 1)
                for hf in range(HALVES):
                    nc.gpsimd.indirect_dma_start(out[:, :], bass.IndirectOffsetOnAxis(ap=si[c % ROUND][:, hf:hf + 1], axis=0),
                                                 y[par][:, hf, :], None, bounds_check=T + CAP - 1, compute_op=ALU.add
                                                 ).then_inc(added[par], 16)

            for c in range(AHEAD):
                gather(0, c)
            for c in range(ROUND):
                gather(0, c + AHEAD)
                add(0, c)
            with pool.Fori(1, LOOPS) as i:
                for c in range(ROUND):
                    gather(i, c + AHEAD)
                    add(i, c)
            for c in range(2 * ROUND):
                if c + AHEAD < 2 * ROUND:
                    gather(LOOPS, c + AHEAD)
                add(LOOPS, c)
            for s in added:
                pool.wait_ge(s, 32 * (E // 2))

        @block.tensor
        def _(pe):
            def columns(q):
                pe.wait_ge(counts_copied, done(q - 1))
                now = k.counts[:, bass.ds(q * P + 1, P)]
                last = k.counts[:, bass.ds(q * P, P)]
                nc.tensor.matmul(col_ps[:, 0:P], now, k.ident16, start=True, stop=True)
                nc.tensor.matmul(col_ps[:, P:P + 1], last, k.ident16[:, P - 1:P], start=True, stop=True
                                 ).then_inc(counts_mm, 1)

            def pick(q):
                pe.wait_ge(tile_found, done(q))
                pe.wait_ge(counts_copied, done(q))
                pe.wait_ge(compared, done(q - 1))
                for e in range(2):
                    rows = slice(e * TILES, (e + 1) * TILES)
                    for hf in range(HALVES):
                        one = hot[rows, hf * P:(hf + 1) * P]
                        nc.tensor.matmul(pick_ps[:, e, hf * P:(hf + 1) * P], one, cts[rows, :], start=True, stop=True)
                        mm = nc.tensor.matmul(pick_ps[:, e, CAP + hf:CAP + hf + 1], one, k.tile_col[rows, :],
                                              start=True, stop=True)
                mm.then_inc(picked, 1)

            def turn(i, c):
                s, slot, par = ROUND * i + c, c % ROUND, c % 2
                pe.wait_ge(*seen(gathered, i, c))
                pe.wait_ge(xT_ready, done(s - 2))
                for hf in range(HALVES):
                    for h in range(DH):
                        mm = nc.tensor.transpose(x_ps[par][:, h * CAP + hf * P:h * CAP + (hf + 1) * P],
                                                 x[slot][:, hf, h * P:(h + 1) * P], k.ident)
                mm.then_inc(turned, 1)

            def expand(i, c):
                s, slot, par = ROUND * i + c, c % ROUND, c % 2
                pe.wait_ge(xT_ready, done(s))
                pe.wait_ge(hidden_ready, done(s - 1))
                pe.wait_ge(w_loaded[slot], 16 * i + 16 * (c // ROUND + 1))
                for m, (ps, mm_done) in enumerate(((gate_ps, gate_mm), (up_ps, up_mm))):
                    for h in range(DH):
                        mm = nc.tensor.matmul(ps[:, 0:CAP], w[slot][:, m * D + h * FF:m * D + (h + 1) * FF], xT[par][:, h, :],
                                              start=h == 0, stop=h == DH - 1)
                    mm.then_inc(mm_done, 1)

            def contract(i, c):
                s, slot, par = ROUND * i + c, c % ROUND, c % 2
                pe.wait_ge(hidden_ready, done(s))
                pe.wait_ge(scaled, done(s - 1))
                for hf in range(HALVES):
                    mm = nc.tensor.matmul(down_ps[:, hf * D:(hf + 1) * D], hidden[par][:, hf * P:(hf + 1) * P],
                                          w[slot][:, 2 * D:3 * D], start=True, stop=True)
                mm.then_inc(down_mm, 1)

            def body(i, c, slots=True, more=True):
                if more:
                    turn(i, c + 1)
                if slots:
                    (columns if c % 2 == 0 else pick)(2 * i + (c // 2 + LEAD))
                contract(i, c)
                if more:
                    expand(i, c + 1)

            for q in range(LEAD):
                columns(q)
                pick(q)
            turn(0, 0)
            expand(0, 0)
            with pe.Fori(0, LOOPS) as i:
                for c in range(ROUND):
                    body(i, c)
            for c in range(2 * ROUND):
                body(LOOPS, c, slots=False, more=c < 2 * ROUND - 1)

        @block.scalar
        def _(act):
            def column_copies(q):
                act.wait_ge(counts_mm, done(q))
                act.wait_ge(tile_found, done(q - 1))
                nc.scalar.activation(bounds[:, 0:1], col_ps[:, P - 1:P], ACT.Copy)
                nc.scalar.activation(bounds[:, 1:2], col_ps[:, P:P + 1], ACT.Copy, scale=k.cols[:, 5:6]
                                     ).then_inc(bounds_ready, 1)
                act.wait_ge(picked, done(q - 1))
                nc.scalar.activation(cts[:, :], col_ps[:, 0:P], ACT.Copy).then_inc(counts_copied, 1)

            def turn_copy(s, par):
                act.wait_ge(turned, done(s))
                act.wait_ge(up_mm, done(s - 2))
                nc.scalar.activation(xT[par][:, :, :].rearrange("p c n -> p (c n)"), x_ps[par][:, :], ACT.Copy
                                     ).then_inc(xT_ready, 1)

            def gate_fn(s, par):
                act.wait_ge(gate_mm, done(s))
                act.wait_ge(hidden_ready, done(s - 2))
                nc.scalar.activation(gate[par][:, :], gate_ps[:, 0:CAP], ACT.Silu).then_inc(gate_ready, 1)

            def scale(i, c):
                s, par = ROUND * i + c, c % 2
                act.wait_ge(down_mm, done(s))
                act.wait_ge(weights_ready, done(s))
                if not (isinstance(s, int) and s < 2):
                    act.wait_ge(added[par], 64 * i + 32 * (c // 2))
                for hf in range(HALVES):
                    ins = nc.scalar.activation(y[par][:, hf, :], down_ps[:, hf * D:(hf + 1) * D], ACT.Copy,
                                               scale=wcol[par][:, hf:hf + 1])
                ins.then_inc(scaled, 1)

            def body(i, c, slots=True, more=True):
                s = ROUND * i + c
                if more:
                    turn_copy(s + 1, (c + 1) % 2)
                if slots and c % 2 == 0:
                    column_copies(2 * i + (c // 2 + LEAD))
                scale(i, c)
                if more:
                    gate_fn(s + 1, (c + 1) % 2)

            for q in range(LEAD):
                column_copies(q)
            turn_copy(0, 0)
            gate_fn(0, 0)
            for c in range(ROUND):
                body(0, c)
            with act.Fori(1, LOOPS) as i:
                for c in range(ROUND):
                    body(i, c)
            for c in range(2 * ROUND):
                body(LOOPS, c, slots=False, more=c < 2 * ROUND - 1)

        @block.vector
        def _(dve):
            ch = Chain(dve, k.dve_chain)

            def find_tile(q):
                dve.wait_ge(bounds_ready, done(q))
                dve.wait_ge(picked, done(q - 1))
                ch.link(nc.vector.tensor_scalar(hot[:, :], k.slot_row, bounds[:, 1:2], None, ALU.is_ge))
                nc.vector.scalar_tensor_tensor(out=hot[:, :], in0=k.slot_row, scalar=bounds[:, 0:1],
                                               in1=hot[:, :], op0=ALU.is_lt, op1=ALU.mult).then_inc(tile_found, 1)

            def find_token(q):
                dve.wait_ge(picked, done(q))
                for hf in range(HALVES):
                    ch.mark(nc.vector.tensor_scalar(below[:, :, hf, :], pick_ps[:, :, hf * P:(hf + 1) * P],
                                                    k.cols[:, hf:hf + 1], None, ALU.is_le))
                ch.reach(ch.n)
                ch.link(nc.vector.tensor_reduce(fine[:, :], below[:, :, :, :].rearrange("p e h n -> p (e h) n"), AX, ALU.add))
                ch.mark(nc.vector.tensor_scalar(empty[:, :], fine[:, :], P - 0.5, None, ALU.is_ge))
                nc.vector.scalar_tensor_tensor(out=token[:, :].rearrange("p (e h) -> p e h", e=2),
                                               in0=pick_ps[:, :, CAP:CAP + HALVES], scalar=float(P),
                                               in1=fine[:, :].rearrange("p (e h) -> p e h", e=2),
                                               op0=ALU.mult, op1=ALU.add).then_inc(compared, 1)
                dve.wait_ge(compared, done(q))
                ch.reach(ch.n)
                pair = token[:, :].rearrange("p (e h) -> p e h", e=2)
                ch.mark(nc.vector.tensor_copy(k.gather_idx[:, bass.ds(2 * q, 2), :], pair))
                ch.link(nc.vector.tensor_tensor(empty[:, :].rearrange("p (e h) -> p e h", e=2),
                                                empty[:, :].rearrange("p (e h) -> p e h", e=2),
                                                k.cols[:, 2:4].unsqueeze(1).to_broadcast([P, 2, HALVES]), ALU.mult))
                nc.vector.tensor_tensor(k.scatter_idx[:, bass.ds(2 * q, 2), :], pair,
                                        empty[:, :].rearrange("p (e h) -> p e h", e=2), ALU.add).then_inc(indices_ready, 1)

            def weight_columns(i, c):
                s, slot, par = ROUND * i + c, c % ROUND, c % 2
                dve.wait_ge(*seen(gathered, i, c))
                dve.wait_ge(scaled, done(s - 2))
                nc.vector.tensor_copy(si[slot][:, :], k.scatter_idx[:, bass.ds(s, 1), :].rearrange("p a h -> p (a h)"))
                nc.vector.tensor_copy(wcol[par][:, :], x[slot][:, :, bass.ds(s + D, 1)].rearrange("p h a -> p (h a)")
                                      ).then_inc(weights_ready, 1)

            def gather_indices(i, c):
                s, slot = ROUND * i + c, c % ROUND
                dve.wait_ge(indices_ready, done((ROUND // 2) * i + c // 2))
                nc.vector.tensor_copy(gi[slot][:, :], k.gather_idx[:, bass.ds(s, 1), :].rearrange("p a h -> p (a h)")
                                      ).then_inc(gi_ready, 1)

            def act_mul(i, c):
                s, par = ROUND * i + c, c % 2
                dve.wait_ge(gate_ready, done(s))
                dve.wait_ge(down_mm, done(s - 2))
                dve.wait_ge(up_mm, done(s))
                nc.vector.tensor_tensor(hidden[par][:, :], up_ps[:, 0:CAP], gate[par][:, :], ALU.mult
                                        ).then_inc(hidden_ready, 1)

            def body(i, c, slots=True, more=True):
                if more:
                    weight_columns(i, c + 1)
                if slots or c < ROUND:
                    gather_indices(i, c + ROUND)
                if slots:
                    (find_tile if c % 2 == 0 else find_token)(2 * i + (c // 2 + LEAD))
                if more:
                    act_mul(i, c + 1)

            for q in range(LEAD):
                find_tile(q)
                find_token(q)
                if q < ROUND // 2:
                    gather_indices(0, 2 * q)
                    gather_indices(0, 2 * q + 1)
            weight_columns(0, 0)
            act_mul(0, 0)
            ch.restart()
            with dve.Fori(0, LOOPS) as i:
                for c in range(ROUND):
                    body(i, c)
                ch.restart()
            for c in range(2 * ROUND):
                body(LOOPS, c, slots=False, more=c < 2 * ROUND - 1)
            ch.restart()


_IN = [("x", [P, TILES], I32), ("codes_T", [D, CODES], F32), ("tok_W1", [D, HID], F32), ("tok_b1", [P, HC], F32),
       ("tok_W2", [HID, D], F32), ("tok_b2", [1, D], F32), ("alpha_raw", [1, 1], F32),
       ("pw_T", [2, D, D], F32), ("gate_wT", [D, D], F32), ("dw", [P, 2 * DH * TAPS], F32),
       ("q_T", [D, NH * HD], F32), ("k_T", [D, NKV * 2 * HD], F32), ("v_T", [D, NKV * HD], F32), ("o_T", [NH * HD, D], F32),
       ("route_T", [D, E], F32), ("e_bias", [1, E], F32), ("shared_T", [D, 2 * D], F32), ("down_T", [D, D], F32),
       ("experts", [E, P, 3 * D], F32)]


def kernel(x, L0_tok_codebook, L0_tok_W1, L0_tok_b1, L0_tok_W2, L0_tok_b2, L0_attn_q_w, L0_attn_k_w, L0_attn_v_w,
           L0_attn_o_w, L0_attn_dw_r, L0_attn_pw_r, L0_attn_dw_i, L0_attn_pw_i, L0_attn_gate_w, L0_attn_alpha_raw,
           L0_ffn_gate_weight, L0_ffn_e_bias, L0_ffn_w1, L0_ffn_w2, L0_ffn_w3, L0_ffn_shared_gate, L0_ffn_shared_up,
           L0_ffn_shared_down):
    import numpy as _np
    import concourse.bacc as _bacc
    from concourse.bass_utils import run_bass_kernel_spmd as _run

    def c(a):
        return _np.ascontiguousarray(a)

    def a_(a):
        return _np.asarray(a)

    f32, high, f16 = shape_constants()
    dw = _np.stack([a_(L0_attn_dw_r)[:, 0], a_(L0_attn_dw_i)[:, 0]]).reshape(2, DH, P, TAPS).transpose(2, 0, 1, 3)
    k_T = a_(L0_attn_k_w).reshape(NKV, 1, HD, D).repeat(2, 1).reshape(NKV * 2 * HD, D).T
    w1, w3 = (a_(w).transpose(0, 2, 1).reshape(E, DH, P, FF).transpose(0, 2, 1, 3).reshape(E, P, DH * FF)
              for w in (L0_ffn_w1, L0_ffn_w3))
    w2 = a_(L0_ffn_w2).transpose(0, 2, 1)
    arrays = {
        "x": c(a_(x).reshape(TILES, P).T), "codes_T": c(a_(L0_tok_codebook).T), "tok_W1": c(L0_tok_W1),
        "tok_b1": c(a_(L0_tok_b1).reshape(HC, P).T), "tok_W2": c(L0_tok_W2), "tok_b2": c(a_(L0_tok_b2).reshape(1, D)),
        "alpha_raw": c(a_(L0_attn_alpha_raw).reshape(1, 1)),
        "pw_T": c(_np.stack([a_(L0_attn_pw_r).T, a_(L0_attn_pw_i).T])), "gate_wT": c(a_(L0_attn_gate_w).T),
        "dw": c(dw.reshape(P, -1)), "q_T": c(a_(L0_attn_q_w).T), "k_T": c(k_T), "v_T": c(a_(L0_attn_v_w).T),
        "o_T": c(a_(L0_attn_o_w).T), "route_T": c(a_(L0_ffn_gate_weight).T), "e_bias": c(a_(L0_ffn_e_bias).reshape(1, E)),
        "shared_T": c(_np.concatenate([a_(L0_ffn_shared_gate), a_(L0_ffn_shared_up)]).T),
        "down_T": c(a_(L0_ffn_shared_down).T), "experts": c(_np.concatenate([w1, w3, w2], 2)),
        "c_f32": f32, "c_high": high, "c_f16": f16,
    }
    nc = _bacc.Bacc("TRN2", target_bir_lowering=False, num_devices=1)
    d = {}
    for name, shape, dt in _IN:
        assert list(arrays[name].shape) == shape, (name, arrays[name].shape)
        d[name] = nc.dram_tensor(f"in_{name}", shape, dt, kind="ExternalInput").ap()
    for name in ("c_f32", "c_high", "c_f16"):
        a = arrays[name]
        d[name] = nc.dram_tensor(f"in_{name}", a.shape, mybir.dt.from_np(a.dtype), kind="ExternalInput").ap()
    out = nc.dram_tensor("out_rows", [T + CAP, D], F32, kind="ExternalOutput")
    build(nc, d, out, {n: arrays[n].shape[1] for n in ("c_f32", "c_f16")})
    r = _run(nc, [{f"in_{n}": a for n, a in arrays.items()}], core_ids=[0])
    return r.results[0]["out_rows"][:T].reshape(B, N, D)
```
